# Optimizing a Trainium2 kernel written in Bass

```python
import numpy as np
import jax
import jax.numpy as jnp

def _softmax(x, axis=-1):
    return jax.nn.softmax(x, axis=axis)

def _gelu(x):
    return jax.nn.gelu(x, approximate=True)

def _silu(x):
    return jax.nn.silu(x)

def _sigmoid(x):
    return jax.nn.sigmoid(x)

def _layernorm(x, axis=-1, eps=1e-05):
    m = jnp.mean(x, axis=axis, keepdims=True)
    v = jnp.var(x, axis=axis, keepdims=True)
    return (x - m) / jnp.sqrt(v + eps)

def _scatter_add(tgt, idx, src, axis=0):
    return tgt.at[idx].add(src)

def _segment_sum(src, seg, n):
    return jax.ops.segment_sum(src, seg, n)
kernel_name = 'mk_decoder_preln_d1_seqx_r2_76e2da'

def setup_inputs(seed: int=0):
    np.random.seed(seed)
    _w = jnp.asarray

    def _rec_inputs():
        import jax
        import jax.numpy as jnp
        _rk = jax.random.key(seed)
        x = 0.0002417 + 0.9998 * jax.random.normal(jax.random.fold_in(_rk, 1), (8, 512, 512), jnp.float32)
        _lenS = 512 - jax.random.randint(jax.random.fold_in(_rk, 7), (8,), 0, max(1, 512 // 4) + 1, jnp.int32)
        _lenS2 = 77 - jax.random.randint(jax.random.fold_in(_rk, 8), (8,), 0, max(1, 77 // 4) + 1, jnp.int32)
        _ctx_1024P = jax.random.normal(jax.random.fold_in(_rk, 11), (8, 16, 512), jnp.float32)
        _ctx_1024c = jax.random.dirichlet(jax.random.fold_in(_rk, 511), 0.3 * jnp.ones((16,), jnp.float32), (8, 77))
        _ctx_1024t = jnp.einsum('bsk,bkd->bsd', _ctx_1024c, _ctx_1024P)
        _ctx_1024t = _ctx_1024t * jax.lax.rsqrt(jnp.mean(jnp.square(_ctx_1024t)) + 1e-12) * 0.953939
        ctx_1024 = 7.22013e-05 + 1.00017 * (_ctx_1024t + 0.3 * jax.random.normal(jax.random.fold_in(_rk, 611), (8, 77, 512), jnp.float32))
        _validS = jnp.arange(512)[None, :] < _lenS[:, None]
        _validS2 = jnp.arange(77)[None, :] < _lenS2[:, None]
        _causal = jnp.tril(jnp.ones((512, 512), dtype=bool))
        mask_1x1xSxS2_fk0 = jnp.where(jnp.broadcast_to(_validS2[0:1, None, None, :], (1, 1, 512, 77)), 0.0, 1.0).astype(jnp.float32)
        return (x, ctx_1024, mask_1x1xSxS2_fk0)
    x, ctx_1024, mask_1x1xSxS2_fk0 = _rec_inputs()

    def _L0_attn_setup():
        import jax, jax.numpy as jnp
        import numpy as np
        H = 16
        HD = 64
        W = 512
        G = 128
        EPS = 1e-06
        NEG = -1e+30
        key = jax.random.key(seed)
        ks = jax.random.split(key, 7)
        B, S, D = (1, 4096, 512)
        inner = H * HD
        s = 0.02
        return {'x': jax.random.normal(ks[0], (B, S, D), jnp.float32), 'norm_w': jnp.ones((D,), jnp.float32), 'w_q': jax.random.normal(ks[1], (D, inner), jnp.float32) * s, 'w_k': jax.random.normal(ks[2], (D, inner), jnp.float32) * s, 'w_v': jax.random.normal(ks[3], (D, inner), jnp.float32) * s, 'w_out': jax.random.normal(ks[4], (inner, D), jnp.float32) * s, 'scorer_w': jax.random.normal(ks[5], (D, 1), jnp.float32) * s, 'scorer_b': jnp.zeros((1,), jnp.float32)}
    _L0_attn_all = _L0_attn_setup()
    _L0_attn_in = {k: v for k, v in _L0_attn_all.items() if k in ('norm_w', 'w_q', 'w_k', 'w_v', 'w_out', 'scorer_w', 'scorer_b')}
    del _L0_attn_all

    def _L0_xattn_setup():
        import jax, jax.numpy as jnp
        import numpy as np
        HEAD = 16
        NEG_FILL = -1e+20
        key = jax.random.key(seed)
        ks = jax.random.split(key, 6)
        N, S, E = (4, 1024, 512)
        D = E // HEAD
        value = jax.random.normal(ks[0], (N, S, E), dtype=jnp.float32)
        key_t = jax.random.normal(ks[1], (N, S, E), dtype=jnp.float32)
        query = jax.random.normal(ks[2], (N, S, E), dtype=jnp.float32)
        mask = jnp.tril(jnp.ones((S, S), dtype=jnp.float32))[None, None, :, :]
        sc = 1.0 / np.sqrt(D)
        Wq = jax.random.normal(ks[3], (D, D), dtype=jnp.float32) * sc
        Wk = jax.random.normal(ks[4], (D, D), dtype=jnp.float32) * sc
        Wv = jax.random.normal(ks[5], (D, D), dtype=jnp.float32) * sc
        return {'value': value, 'key': key_t, 'query': query, 'mask': mask, 'Wq': Wq, 'Wk': Wk, 'Wv': Wv}
    _L0_xattn_all = _L0_xattn_setup()
    _L0_xattn_in = {k: v for k, v in _L0_xattn_all.items() if k in ('Wq', 'Wk', 'Wv')}
    del _L0_xattn_all

    def _L0_ffn_setup():
        import jax, jax.numpy as jnp
        import numpy as np
        B, S, D, H, F = (4, 2048, 512, 16, 2048)
        CAP = 0.125
        ROPE_BASE = 10000.0

        def rmsnorm(x, g):
            return x * jax.lax.rsqrt(jnp.mean(x * x, -1, keepdims=True) + 1e-06) * g

        def rope(t, pos):
            hd = t.shape[-1]
            inv = 1.0 / ROPE_BASE ** (jnp.arange(0, hd, 2, dtype=jnp.float32) / hd)
            f = pos[:, None, :, None].astype(jnp.float32) * inv
            emb = jnp.concatenate([f, f], axis=-1)
            cos, sin = (jnp.cos(emb), jnp.sin(emb))
            rot = jnp.concatenate([-t[..., hd // 2:], t[..., :hd // 2]], axis=-1)
            return t * cos + rot * sin
        key = jax.random.key(seed)
        ks = jax.random.split(key, 9)
        scale = 0.02
        x = jax.random.normal(ks[0], (B, S, D), jnp.float32)
        causal = jnp.where(jnp.tril(jnp.ones((S, S), bool)), 0.0, -1000000000.0).astype(jnp.float32)
        attention_mask = jnp.broadcast_to(causal[None, None], (B, 1, S, S))
        position_ids = jnp.broadcast_to(jnp.arange(S, dtype=jnp.int32), (B, S))
        return {'x': x, 'attention_mask': attention_mask, 'position_ids': position_ids, 'router_w': jax.random.normal(ks[1], (D, 1), jnp.float32) * scale, 'router_b': jnp.zeros((1,), jnp.float32), 'wq': jax.random.normal(ks[2], (D, D), jnp.float32) * scale, 'wk': jax.random.normal(ks[3], (D, D), jnp.float32) * scale, 'wv': jax.random.normal(ks[4], (D, D), jnp.float32) * scale, 'wo': jax.random.normal(ks[5], (D, D), jnp.float32) * scale, 'w1': jax.random.normal(ks[6], (D, F), jnp.float32) * scale, 'w2': jax.random.normal(ks[7], (F, D), jnp.float32) * scale, 'ln1': jnp.ones((D,), jnp.float32), 'ln2': jnp.ones((D,), jnp.float32)}
    _L0_ffn_all = _L0_ffn_setup()
    _L0_ffn_in = {k: v for k, v in _L0_ffn_all.items() if k in ('attention_mask', 'position_ids', 'router_w', 'router_b', 'wq', 'wk', 'wv', 'wo', 'w1', 'w2', 'ln1', 'ln2')}
    del _L0_ffn_all
    return {'x': x, 'ctx_1024': ctx_1024, 'mask_1x1xSxS2_fk0': mask_1x1xSxS2_fk0, 'L0_attn_norm_w': _L0_attn_in['norm_w'], 'L0_attn_w_q': _L0_attn_in['w_q'], 'L0_attn_w_k': _L0_attn_in['w_k'], 'L0_attn_w_v': _L0_attn_in['w_v'], 'L0_attn_w_out': _L0_attn_in['w_out'], 'L0_attn_scorer_w': _L0_attn_in['scorer_w'], 'L0_attn_scorer_b': _L0_attn_in['scorer_b'], 'L0_xattn_Wq': _L0_xattn_in['Wq'], 'L0_xattn_Wk': _L0_xattn_in['Wk'], 'L0_xattn_Wv': _L0_xattn_in['Wv'], 'L0_ffn_attention_mask': _L0_ffn_in['attention_mask'], 'L0_ffn_position_ids': _L0_ffn_in['position_ids'], 'L0_ffn_router_w': _L0_ffn_in['router_w'], 'L0_ffn_router_b': _L0_ffn_in['router_b'], 'L0_ffn_wq': _L0_ffn_in['wq'], 'L0_ffn_wk': _L0_ffn_in['wk'], 'L0_ffn_wv': _L0_ffn_in['wv'], 'L0_ffn_wo': _L0_ffn_in['wo'], 'L0_ffn_w1': _L0_ffn_in['w1'], 'L0_ffn_w2': _L0_ffn_in['w2'], 'L0_ffn_ln1': _L0_ffn_in['ln1'], 'L0_ffn_ln2': _L0_ffn_in['ln2']}

def reference(x, ctx_1024, mask_1x1xSxS2_fk0, L0_attn_norm_w, L0_attn_w_q, L0_attn_w_k, L0_attn_w_v, L0_attn_w_out, L0_attn_scorer_w, L0_attn_scorer_b, L0_xattn_Wq, L0_xattn_Wk, L0_xattn_Wv, L0_ffn_attention_mask, L0_ffn_position_ids, L0_ffn_router_w, L0_ffn_router_b, L0_ffn_wq, L0_ffn_wk, L0_ffn_wv, L0_ffn_wo, L0_ffn_w1, L0_ffn_w2, L0_ffn_ln1, L0_ffn_ln2):
    import jax
    import jax.numpy as jnp

    def _L0_attn_ref(x, norm_w, w_q, w_k, w_v, w_out, scorer_w, scorer_b):
        import jax, jax.numpy as jnp
        import numpy as np
        H = 16
        HD = 64
        W = 512
        G = 128
        EPS = 1e-06
        NEG = -1e+30
        B, S, D = x.shape
        h = x * jax.lax.rsqrt(jnp.mean(x * x, axis=-1, keepdims=True) + EPS) * norm_w

        def proj(w):
            return jnp.einsum('bsd,de->bse', h, w).reshape(B, S, H, HD).transpose(0, 2, 1, 3)
        q, k, v = (proj(w_q), proj(w_k), proj(w_v))
        scale = HD ** (-0.5)
        nW = S // W
        qw = q.reshape(B, H, nW, W, HD)
        kw = k.reshape(B, H, nW, W, HD)
        vw = v.reshape(B, H, nW, W, HD)
        ll = jnp.einsum('bhnqd,bhnkd->bhnqk', qw, kw) * scale
        cm = jnp.tril(jnp.ones((W, W), bool))
        ll = jnp.where(cm, ll, NEG).reshape(B, H, S, W)
        scores = (jnp.einsum('bsd,do->bso', h, scorer_w) + scorer_b)[..., 0]
        _, idx = jax.lax.top_k(scores, G)
        kg = jnp.take_along_axis(k, idx[:, None, :, None], axis=2)
        vg = jnp.take_along_axis(v, idx[:, None, :, None], axis=2)
        lg = jnp.einsum('bhsd,bhgd->bhsg', q, kg) * scale
        pos = jnp.arange(S)
        gmask = idx[:, None, None, :] <= pos[None, None, :, None]
        lg = jnp.where(gmask, lg, NEG)
        attn = jax.nn.softmax(jnp.concatenate([ll, lg], axis=-1), axis=-1)
        a_loc = attn[..., :W].reshape(B, H, nW, W, W)
        o = jnp.einsum('bhnqk,bhnkd->bhnqd', a_loc, vw).reshape(B, H, S, HD)
        o = o + jnp.einsum('bhsg,bhgd->bhsd', attn[..., W:], vg)
        o = o.transpose(0, 2, 1, 3).reshape(B, S, H * HD)
        return x + jnp.einsum('bse,ed->bsd', o, w_out)

    def _L0_xattn_ref(value, key, query, mask, Wq, Wk, Wv):
        import jax, jax.numpy as jnp
        import numpy as np
        HEAD = 16
        NEG_FILL = -1e+20
        N, Lq, E = query.shape
        H = HEAD
        D = E // H
        q = jnp.einsum('nqhd,de->nqhe', query.reshape(N, Lq, H, D), Wq)
        k = jnp.einsum('nkhd,de->nkhe', key.reshape(N, key.shape[1], H, D), Wk)
        v = jnp.einsum('nvhd,de->nvhe', value.reshape(N, value.shape[1], H, D), Wv)
        energy = jnp.einsum('nqhd,nkhd->nhqk', q, k)
        energy = energy * mask
        energy = jnp.where(energy == 0, NEG_FILL, energy)
        attention = jax.nn.softmax(energy, axis=-1)
        out = jnp.einsum('nhql,nlhd->nqhd', attention, v).reshape(N, Lq, H * D)
        return out

    def _L0_ffn_ref(x, attention_mask, position_ids, router_w, router_b, wq, wk, wv, wo, w1, w2, ln1, ln2):
        import jax, jax.numpy as jnp
        import numpy as np
        B, S, D, H, F = (4, 2048, 512, 16, 2048)
        CAP = 0.125
        ROPE_BASE = 10000.0

        def rmsnorm(x, g):
            return x * jax.lax.rsqrt(jnp.mean(x * x, -1, keepdims=True) + 1e-06) * g

        def rope(t, pos):
            hd = t.shape[-1]
            inv = 1.0 / ROPE_BASE ** (jnp.arange(0, hd, 2, dtype=jnp.float32) / hd)
            f = pos[:, None, :, None].astype(jnp.float32) * inv
            emb = jnp.concatenate([f, f], axis=-1)
            cos, sin = (jnp.cos(emb), jnp.sin(emb))
            rot = jnp.concatenate([-t[..., hd // 2:], t[..., :hd // 2]], axis=-1)
            return t * cos + rot * sin
        b, s, d = x.shape
        hd = d // H
        weights = (x @ router_w)[..., 0] + router_b[0]
        k = int(CAP * s)
        topv, topi = jax.lax.top_k(weights, k)
        thr = topv[:, -1]
        sel_mask = (weights > thr[:, None]).astype(x.dtype)
        kc = k - 1
        sel_idx = jnp.sort(topi[:, :kc], axis=1)
        bidx = jnp.arange(b)[:, None]
        x_sel = x[bidx, sel_idx]
        pos_sel = position_ids[bidx, sel_idx]
        w_sel = weights[bidx, sel_idx]
        m = attention_mask[:, 0]
        m_sel = m[bidx[:, :, None], sel_idx[:, :, None], sel_idx[:, None, :]]
        hn = rmsnorm(x_sel, ln1)

        def heads(t):
            return t.reshape(b, kc, H, hd).transpose(0, 2, 1, 3)
        q = rope(heads(hn @ wq), pos_sel)
        kk = rope(heads(hn @ wk), pos_sel)
        v = heads(hn @ wv)
        sc = jnp.einsum('bhqd,bhkd->bhqk', q, kk) / np.sqrt(hd).astype(np.float32)
        sc = sc + m_sel[:, None]
        a = jax.nn.softmax(sc, axis=-1)
        o = jnp.einsum('bhqk,bhkd->bhqd', a, v).transpose(0, 2, 1, 3).reshape(b, kc, d) @ wo
        x1 = x_sel + o
        x2 = x1 + jax.nn.gelu(rmsnorm(x1, ln2) @ w1) @ w2
        proc = x2 * w_sel[..., None]
        out = jnp.zeros_like(x).at[bidx, sel_idx].set(proc)
        return out + x * (1.0 - sel_mask)[..., None]
    x = x + _L0_attn_ref(_layernorm(x, axis=-1), L0_attn_norm_w, L0_attn_w_q, L0_attn_w_k, L0_attn_w_v, L0_attn_w_out, L0_attn_scorer_w, L0_attn_scorer_b)
    x = x + _L0_xattn_ref(ctx_1024, ctx_1024, _layernorm(x, axis=-1), mask_1x1xSxS2_fk0, L0_xattn_Wq, L0_xattn_Wk, L0_xattn_Wv)
    x = x + _L0_ffn_ref(_layernorm(x, axis=-1), L0_ffn_attention_mask, L0_ffn_position_ids, L0_ffn_router_w, L0_ffn_router_b, L0_ffn_wq, L0_ffn_wk, L0_ffn_wv, L0_ffn_wo, L0_ffn_w1, L0_ffn_w2, L0_ffn_ln1, L0_ffn_ln2)
    return x

_drawn_inputs = setup_inputs


def setup_inputs(seed=0):
    import zlib

    import numpy as np

    out = dict(_drawn_inputs(seed))
    spreads = {'L0_attn_norm_w': (1.0, 0.6), 'L0_ffn_ln1': (1.0, 0.6), 'L0_ffn_ln2': (1.0, 0.6)}
    factors = {'L0_attn_w_q': 8.0,
     'L0_attn_w_k': 8.0,
     'L0_attn_scorer_w': 6.5,
     'L0_ffn_wq': 8.0,
     'L0_ffn_wk': 8.0,
     'L0_ffn_wv': 4.44,
     'L0_ffn_wo': 4.448}
    for name, (base, spread) in spreads.items():
        noise = np.random.default_rng([zlib.crc32(name.encode()), seed]).standard_normal(out[name].shape)
        drawn = base * np.exp(spread * noise) if base else spread * noise
        out[name] = jnp.asarray(drawn.astype(out[name].dtype))
    for name, factor in factors.items():
        out[name] = (out[name] * factor).astype(out[name].dtype)
    return out
```

```python
from contextlib import ExitStack, contextmanager

import numpy as np
import concourse.bass as bass
from concourse import mybir
from concourse.bass import IndirectOffsetOnAxis

F32 = mybir.dt.float32
F32R = mybir.dt.float32r
BF16 = mybir.dt.bfloat16
I8 = mybir.dt.int8
I32 = mybir.dt.int32
U32 = mybir.dt.uint32
ALU = mybir.AluOpType
ACT = mybir.ActivationFunctionType
AX = mybir.AxisListType

P = 128
B, S, D = 8, 512, 512
TT = S // P
DC = D // P
EPS_LN = 1e-5
EPS_RMS = 1e-6

H, HD = 16, 64
NPAIR = H // 2
TOPK = 128
NEG = -1e30
UNITS = 5
NU = NPAIR * UNITS
VW = HD + 1


class Tally:

    def __init__(self, sem):
        self.sem, self.start, self.round, self.n = sem, 0, 0, 0

    @contextmanager
    def loop(self, i, per, trips):
        self.start, self.round, self.n = self.start + self.n, i * per, 0
        yield
        assert self.n == per, (self.n, per)
        self.start, self.round, self.n = self.start + trips * per, 0, 0

    def mark(self, ins):
        ins.then_inc(self.sem, 1)
        self.n += 1

    def wait(self, eng):
        eng.wait_ge(self.sem, self.round + (self.start + self.n))


def unit_blocks(u):
    if u < 2:
        return [(u, 3, 0, 512)]
    if u < 4:
        return [(u - 2, 0, 0, 128), (u - 2, 2, 128, 384)]
    return [(0, 1, 0, 256), (1, 1, 256, 256)]


def attention_plan():
    plan = [("v", i) for i in range(2 * TT)] + [("q", 0), ("k", 0)]
    for g in range(NU + 7):
        p, u = divmod(g, UNITS)
        if g < NU:
            plan.append(("s", g))
            if p + 1 < NPAIR and u in (0, 2):
                plan.append(("q" if u == 0 else "k", p + 1))
        if 2 <= g < NU + 2:
            plan.append(("t", g - 2))
        if 3 <= g < NU + 3:
            plan.append(("pv", g - 3))
        if g == 3:
            plan.append(("stats", 0))
        if g == 14:
            plan.append(("dot", 0))
        if g == 18:
            plan.append(("score", 0))
        if g in (21, 23, 26, 28):
            plan.append(("rank", (21, 23, 26, 28).index(g)))
        if NU <= g < NU + DC:
            plan.append(("ht", g - NU))
        if g >= 9 and (g - 9) % UNITS == 0 and (g - 9) // UNITS < NPAIR - 1:
            plan.append(("ot", (g - 9) // UNITS))
    plan.append(("ot", NPAIR - 1))
    plan += [("out", t) for t in range(TT)]
    return plan


def bank_index(plan, kinds):
    return {s: i for i, s in enumerate([s for s in plan if s[0] in kinds])}


def self_attention(nc, x, norm_w, w_q, w_k, w_v, w_out, scorer_w, scorer_b, x1):
    plan = attention_plan()
    PROJ, PT = bank_index(plan, ("v", "q", "k", "out")), bank_index(plan, ("t", "score", "ht", "ot"))
    with ExitStack() as ctx:
        def sb(name, shape, dt=F32):
            return ctx.enter_context(nc.sbuf_tensor(name, shape, dt))

        def bank(name):
            return ctx.enter_context(nc.psum_tensor(name, [P, 512], F32))

        def sem(name):
            return ctx.enter_context(nc.semaphore(name))

        w_hi = {n: sb(f"w{n}_hi", [P, DC, H * HD], F32R) for n in "qkv"}
        w_lo = {n: sb(f"w{n}_lo", [P, DC, H * HD], F32R) for n in "qkv"}
        w_o = sb("w_o", [P, NPAIR, D])
        xb = sb("xb", [P, TT, D])
        ht_hi, ht_lo = sb("ht_hi", [P, DC, S], F32R), sb("ht_lo", [P, DC, S], F32R)
        vals = sb("vals", [P, TT, H, VW])
        q_hi, q_lo, k_hi, k_lo = (sb(n, [P, 2, S], F32R) for n in ("q_hi", "q_lo", "k_hi", "k_lo"))
        probs = sb("probs", [P, 2, 512])
        probs_t = sb("probs_t", [P, 2, 512])
        o_rden = sb("o_rden", [P, 2, 2])
        o_norm = sb("o_norm", [P, 2, TT, 2, HD])
        o_t = sb("o_t", [P, NPAIR, S])
        xr = sb("xr", [P, 2, D])
        ident = sb("ident", [P, P])
        ident_b = sb("ident_b", [P, P], BF16)
        causal_b = sb("causal_b", [P, P], BF16)
        before = sb("before", [P, S + P * (TT - 1)], I8)
        row_s = sb("row_s", [P, S])
        junk = sb("junk", [P, S], BF16)
        carrier = sb("carrier", [P, 4])
        nw = sb("nw", [P, DC])
        sw = sb("sw", [P, D])
        sbias = sb("sbias", [P, 1])
        bn = sb("bn", [P, TT, 6])
        mv = sb("mv", [P, TT, 2])
        half, ones, minus, eps_ln, eps_rms, idle = (
            sb(n, [P, TT]) for n in ("half", "ones", "minus", "eps_ln", "eps_rms", "idle"))
        st = sb("st", [P, 5, TT])
        RS, MS, S2, NM, NB = range(5)
        res_next, res_now = sb("res_next", [P, 2, TT]), sb("res_now", [P, 2, TT])
        score = sb("score", [P, TT])
        cnt = sb("cnt", [P, 2, TT])
        twice = sb("twice", [P, TT])
        nmax = sb("nmax", [P, 4, 2])

        s_bank = [bank(f"s_bank{i}") for i in range(2)]
        pt_bank = [bank(f"pt_bank{i}") for i in range(2)]
        pj_bank = [bank(f"pj_bank{i}") for i in range(2)]
        o_bank = [bank(f"o_bank{i}") for i in range(2)]

        w_loaded, split_hi, split_lo = [sem(f"w_loaded{i}") for i in range(2)], sem("split_hi"), sem("split_lo")
        small_in, wo_in, x_in = sem("small_in"), sem("wo_in"), sem("x_in")
        xr_in, x1_out = [sem(f"xr_in{i}") for i in range(2)], [sem(f"x1_out{i}") for i in range(2)]
        const_made, pool_step, dve_step = sem("const_made"), sem("pool_step"), sem("dve_step")
        sw_made, stats_ready, h_ready, score_ready, twice_ready = (
            sem(n) for n in ("sw_made", "stats_ready", "h_ready", "score_ready", "twice_ready"))
        ht_hi_ready, ht_lo_ready = sem("ht_hi_ready"), sem("ht_lo_ready")
        pj_ready, row_copied = sem("pj_ready"), sem("row_copied")
        v_ready, v_sum_ready, qk_hi, qk_lo = sem("v_ready"), sem("v_sum_ready"), sem("qk_hi"), sem("qk_lo")
        s_ready, s_half = sem("s_ready"), sem("s_half")
        max_ready, p_ready = sem("max_ready"), sem("p_ready")
        pt_ready = sem("pt_ready")
        ts_ready, pv_ready, o_copied = sem("ts_ready"), sem("pv_ready"), sem("o_copied")
        ot_ready = sem("ot_ready")
        xr_ready, y_ready = sem("xr_ready"), sem("y_ready")

        NPJ, NPT = len(PROJ), len(PT)
        PT0 = {("ht", c): c for c in range(DC)}
        PT0["score", 0] = DC
        NPT0 = len(PT0)
        W_ORDER = [("v", 0), ("v", 1), ("q", 0), ("k", 0), ("q", 1), ("k", 1)]
        N_CONST = 9
        assert NPJ % 2 == 0

        def pj(b, key):
            return PROJ[key] % 2, b * NPJ + PROJ[key] + 1

        def pt(b, key):
            if b is None:
                return PT0[key] % 2, PT0[key] + 1
            return PT[key] % 2, b * NPT + (PT[key] + 1 + NPT0)

        def taken(eng, b, key):
            kind, i = key
            if kind == "v":
                eng.wait_ge(v_ready, b * (2 * TT) + i + 1)
            elif kind in ("q", "k"):
                eng.wait_ge(qk_lo, b * (2 * NPAIR) + 2 * i + (1 if kind == "q" else 2))
            elif kind == "out":
                eng.wait_ge(y_ready, b * TT + i + 2)
            elif kind == "t":
                eng.wait_ge(ts_ready, b * NU + i + 1)
            elif kind == "ot":
                eng.wait_ge(ot_ready, b * NPAIR + i + 1)
            elif kind == "ht":
                eng.wait_ge(ht_lo_ready, (b + 1) * DC + i + 1)
            elif kind == "score":
                eng.wait_ge(row_copied, b + 2)

        def before_use(order, key):
            keys = list(order)
            return keys[order[key] - 2] if order[key] >= 2 else None

        x_rows = x.rearrange("b (t p) d -> b p t d", p=P)
        x1_rows = x1.rearrange("b (t p) d -> b p t d", p=P)
        w_dram = {n: w.rearrange("(c p) e -> p c e", p=P) for n, w in (("q", w_q), ("k", w_k), ("v", w_v))}

        block = ctx.enter_context(nc.Block())

        @block.sync
        def _(sp):
            sp.dma_start(xb[:, :, :], x_rows[0]).then_inc(x_in, 16)
            with nc.allow_non_contiguous_dma(reason="one column per chunk"):
                sp.dma_start(nw[:, :], norm_w.rearrange("(c p) -> p c", p=P)).then_inc(small_in, 16)
            sp.dma_start(sw[:, :], scorer_w.rearrange("d o -> o d").broadcast_to((P, D))).then_inc(small_in, 16)
            sp.dma_start(row_s[:, :], norm_w.rearrange("(o d) -> o d", o=1).broadcast_to((P, D))).then_inc(small_in, 16)
            sp.dma_start(sbias[:, :], scorer_b.rearrange("(o d) -> o d", o=1).broadcast_to((P, 1))).then_inc(small_in, 16)
            for i, (n, hw) in enumerate(W_ORDER):
                if i >= 2:
                    sp.wait_ge(split_lo, i - 1)
                sp.dma_start(o_t[:, DC * (i % 2):DC * (i % 2) + DC, :],
                             w_dram[n][:, :, 512 * hw:512 * hw + 512]).then_inc(w_loaded[i % 2], 16)
            sp.dma_start(w_o[:, :, :], w_out.rearrange("(c p) d -> p c d", p=P)).then_inc(wo_in, 16)

            def results(b):
                for t in range(TT + 1):
                    if t < TT:
                        sp.wait_ge(x1_out[t % 2], b * (16 * TT // 2) + 16 * (t // 2) + 1)
                        sp.dma_start(xr[:, t % 2, :], x_rows[b][:, t, :]).then_inc(xr_in[t % 2], 16)
                    if t:
                        sp.wait_ge(y_ready, b * TT + t + 1)
                        sp.dma_start(x1_rows[b][:, t - 1, :], xr[:, (t - 1) % 2, :]).then_inc(x1_out[(t - 1) % 2], 16)

            with sp.Fori(0, B - 1) as b:
                sp.wait_ge(ht_lo_ready, b * DC + DC)
                sp.dma_start(xb[:, :, :], x_rows[b + 1]).then_inc(x_in, 16)
                results(b)
            sp.wait_ge(ht_lo_ready, DC * B)
            sp.dma_start(xb[:, :, :], x_rows[0]).then_inc(x_in, 16)
            results(B - 1)
            for half_done in x1_out:
                sp.wait_ge(half_done, 16 * B * TT // 2 + 1)

        @block.gpsimd
        def _(pl):
            done = Tally(pool_step)
            done.mark(nc.gpsimd.memset(ident[:, :], 0.0))
            done.mark(nc.gpsimd.memset(causal_b[:, :], 0.0))
            done.mark(nc.gpsimd.memset(before[:, :], 1.0))
            for tile, value in ((half, -0.5), (ones, 1.0), (minus, -1.0), (eps_ln, EPS_LN), (eps_rms, EPS_RMS)):
                nc.gpsimd.memset(tile[:, :], value).then_inc(const_made, 1)
            done.wait(pl)
            done.mark(nc.gpsimd.affine_select(out=ident[:, :], in_=ident[:, :], compare_op=ALU.not_equal, fill=1.0,
                                              base=0, pattern=[[-1, P]], channel_multiplier=1))
            nc.gpsimd.affine_select(out=causal_b[:, :], in_=causal_b[:, :], compare_op=ALU.is_ge, fill=NEG,
                                    base=0, pattern=[[-1, P]], channel_multiplier=1).then_inc(const_made, 1)
            nc.gpsimd.affine_select(out=before[:, :], in_=before[:, :], compare_op=ALU.is_gt, fill=0.0,
                                    base=P * (TT - 1), pattern=[[-1, S + P * (TT - 1)]],
                                    channel_multiplier=1).then_inc(const_made, 1)
            done.wait(pl)
            nc.gpsimd.tensor_copy(ident_b[:, :], ident[:, :]).then_inc(const_made, 1)
            nc.gpsimd.memset(junk[:, :], 0.0).then_inc(const_made, 1)
            pl.wait_ge(const_made, N_CONST)

            def step(ins):
                done.mark(ins)
                done.wait(pl)

            def carry():
                done.wait(pl)
                done.mark(nc.gpsimd.tensor_tensor(idle[:, :], ones[:, :], ones[:, :], ALU.mult))

            def stats(n):
                pl.wait_ge(stats_ready, n + 1)
                m, v = mv[:, :, 0], mv[:, :, 1]
                step(nc.gpsimd.tensor_tensor(st[:, RS], v, eps_ln[:, :], ALU.add))
                step(nc.gpsimd.tensor_tensor(st[:, RS], st[:, RS], half[:, :], ALU.pow))
                step(nc.gpsimd.tensor_tensor(st[:, MS], st[:, RS], st[:, RS], ALU.mult))
                step(nc.gpsimd.tensor_tensor(st[:, MS], st[:, MS], v, ALU.mult))
                step(nc.gpsimd.tensor_tensor(st[:, MS], st[:, MS], eps_rms[:, :], ALU.add))
                step(nc.gpsimd.tensor_tensor(st[:, S2], st[:, MS], half[:, :], ALU.pow))
                step(nc.gpsimd.tensor_tensor(st[:, S2], st[:, S2], st[:, RS], ALU.mult))
                step(nc.gpsimd.tensor_tensor(st[:, NM], minus[:, :], m, ALU.mult))
                step(nc.gpsimd.tensor_tensor(st[:, NB], st[:, S2], st[:, NM], ALU.mult))
                step(nc.gpsimd.tensor_tensor(res_next[:, 0], st[:, RS], ones[:, :], ALU.add))
                step(nc.gpsimd.tensor_tensor(res_next[:, 1], st[:, RS], st[:, NM], ALU.mult))
                pl.wait_ge(x_in, n * 16 + 16)
                carry()
                for t in range(TT):
                    nc.gpsimd.tensor_scalar(xb[:, t, :], xb[:, t, :], st[:, S2, t:t + 1], st[:, NB, t:t + 1],
                                            ALU.mult, ALU.add).then_inc(h_ready, 1)

            stats(0)
            with pl.Fori(0, B) as b, done.loop(b, 14 + TT, B):
                for r in range(2):
                    step(nc.gpsimd.tensor_tensor(res_now[:, r], res_next[:, r], ones[:, :], ALU.mult))
                for kind, i in plan:
                    if kind == "stats":
                        pl.wait_ge(h_ready, b * TT + TT)
                        stats(b + 1)
                    if kind == "out":
                        pl.wait_ge(xr_in[i % 2], b * (16 * TT // 2) + 16 * (i // 2 + 1))
                        carry()
                        nc.gpsimd.tensor_scalar(xr[:, i % 2, :], xr[:, i % 2, :], res_now[:, 0, i:i + 1],
                                                res_now[:, 1, i:i + 1], ALU.mult, ALU.add).then_inc(xr_ready, 1)
                pl.wait_ge(xr_ready, b * TT + TT)

        @block.scalar
        def _(act):
            def normed(b, n, c):
                slot, ready = pt(b, ("ht", c))
                act.wait_ge(pt_ready, ready)
                nc.scalar.activation(ht_hi[:, c, :], pt_bank[slot][:, :], ACT.Copy,
                                     scale=nw[:, c:c + 1]).then_inc(ht_hi_ready, 1)

            for i, (n, hw) in enumerate(W_ORDER):
                act.wait_ge(w_loaded[i % 2], 16 * (i // 2 + 1))
                nc.scalar.copy(w_hi[n][:, :, 512 * hw:512 * hw + 512],
                               o_t[:, DC * (i % 2):DC * (i % 2) + DC, :]).then_inc(split_hi, 1)
                if i == 1:
                    act.wait_ge(small_in, 64)
                    for c in range(DC):
                        normed(None, 0, c)
            act.wait_ge(split_lo, len(W_ORDER))
            with act.Fori(0, B) as b:
                for kind, i in plan:
                    if kind == "v":
                        t, hw = divmod(i, 2)
                        slot, ready = pj(b, (kind, i))
                        act.wait_ge(pj_ready, ready)
                        if i == 0:
                            act.wait_ge(twice_ready, b + 1)
                        nc.scalar.activation(vals[:, t, 8 * hw:8 * hw + 8, 0:HD],
                                             pj_bank[slot][:, :].rearrange("p (h d) -> p h d", d=HD), ACT.Copy,
                                             scale=twice[:, t:t + 1]).then_inc(v_ready, 1)
                    if kind in ("q", "k"):
                        slot, ready = pj(b, (kind, i))
                        act.wait_ge(pj_ready, ready)
                        hi = q_hi if kind == "q" else k_hi
                        nc.scalar.activation(hi[:, i % 2, :], pj_bank[slot][:, :], ACT.Copy,
                                             scale=HD ** -0.5 if kind == "q" else 1.0).then_inc(qk_hi, 1)
                    if kind == "s":
                        act.wait_ge(max_ready, b * NU + i + 1)
                        if i >= 2:
                            act.wait_ge(pt_ready, pt(b, ("t", i - 2))[1])
                        for n, (_, _, c0, nk) in enumerate(unit_blocks(i % UNITS)):
                            ins = nc.scalar.activation(probs[:, i % 2, c0:c0 + nk], s_bank[i % 2][:, c0:c0 + nk],
                                                       ACT.Exp, bias=nmax[:, i % 4, n:n + 1])
                        ins.then_inc(p_ready, 1)
                    if kind == "ht":
                        normed(b, b + 1, i)
                    if kind == "ot":
                        slot, ready = pt(b, (kind, i))
                        act.wait_ge(pt_ready, ready)
                        nc.scalar.copy(o_t[:, i, :], pt_bank[slot][:, :]).then_inc(ot_ready, 1)

        @block.vector
        def _(dv):
            done = Tally(dve_step)

            def step(ins):
                done.mark(ins)
                done.wait(dv)

            def stats(n):
                dv.wait_ge(x_in, n * 16 + 16)
                for t in range(TT):
                    done.mark(nc.vector.bn_stats(bn[:, t, :], xb[:, t, :]))
                done.wait(dv)
                nc.vector.memset(carrier[:, 0:1], 0.0)
                for t in range(TT):
                    ins = nc.vector.bn_aggr(mv[:, t, :], bn[:, t, :])
                ins.then_inc(stats_ready, 1)

            def dot(n):
                dv.wait_ge(h_ready, n * TT + TT)
                for t in range(TT):
                    step(nc.vector.tensor_tensor_reduce(junk[:, :], xb[:, t, :], sw[:, :], 1.0, 0.0, ALU.mult,
                                                             ALU.add, score[:, t:t + 1]))
                done.wait(dv)
                nc.vector.tensor_scalar(score[:, :], score[:, :], sbias[:, 0:1], None, ALU.add).then_inc(score_ready, 1)

            def score_row(b, n):
                slot, ready = pt(b, ("score", 0))
                dv.wait_ge(pt_ready, ready)
                nc.vector.tensor_copy(row_s[:, :], pt_bank[slot][:, :]).then_inc(row_copied, 1)

            def rank(b, n, t):
                if t == 0:
                    dv.wait_ge(row_copied, n + 1)
                step(nc.vector.tensor_scalar(junk[:, :], row_s[:, :], score[:, t:t + 1], None, ALU.is_gt, ALU.add,
                                                  accum_out=cnt[:, 0, t:t + 1]))
                y0 = P * (TT - 1 - t)
                step(nc.vector.scalar_tensor_tensor(junk[:, :], row_s[:, :], score[:, t:t + 1],
                                                         before[:, y0:y0 + S], ALU.is_equal, ALU.mult,
                                                         accum_out=cnt[:, 1, t:t + 1]))
                if t == TT - 1:
                    done.wait(dv)
                    step(nc.vector.tensor_tensor(cnt[:, 0, :], cnt[:, 0, :], cnt[:, 1, :], ALU.add))
                    if b is not None:
                        dv.wait_ge(v_ready, n * (2 * TT))
                    nc.vector.tensor_scalar(twice[:, :], cnt[:, 0, :], TOPK - 0.5, 1.0, ALU.is_lt,
                                            ALU.add).then_inc(twice_ready, 1)

            def normed(b, n, c):
                slot, _ = pt(b, ("ht", c))
                dv.wait_ge(ht_hi_ready, n * DC + c + 1)
                nc.vector.scalar_tensor_tensor(ht_lo[:, c, :], pt_bank[slot][:, :], nw[:, c:c + 1],
                                               ht_hi[:, c, :].bitcast(F32), ALU.mult,
                                               ALU.subtract).then_inc(ht_lo_ready, 1)

            def split(i):
                n, hw = W_ORDER[i]
                dv.wait_ge(split_hi, i + 1)
                cols = slice(512 * hw, 512 * hw + 512)
                nc.vector.tensor_tensor(w_lo[n][:, :, cols], o_t[:, DC * (i % 2):DC * (i % 2) + DC, :],
                                        w_hi[n][:, :, cols].bitcast(F32), ALU.subtract).then_inc(split_lo, 1)

            dv.wait_ge(const_made, N_CONST)
            for i, at_one in enumerate((y_ready, *x1_out)):
                nc.vector.memset(carrier[:, 1 + i:2 + i], 0.0).then_inc(at_one, 1)
            stats(0)
            dv.wait_ge(small_in, 64)
            nc.vector.tensor_tensor(sw[:, :], sw[:, :], row_s[:, :], ALU.mult).then_inc(sw_made, 1)
            dv.wait_ge(sw_made, 1)
            split(0)
            split(1)
            for c in range(DC):
                normed(None, 0, c)
            dot(0)
            score_row(None, 0)
            for t in range(TT):
                rank(None, 0, t)
            for i in range(2, len(W_ORDER)):
                split(i)
            with dv.Fori(0, B) as b, done.loop(b, 2 * TT + 2 * TT + 1 + NU, B):
                for kind, i in plan:
                    if kind == "v" and i == 0:
                        dv.wait_ge(twice_ready, b + 1)
                        dv.wait_ge(pj_ready, pj(b, (kind, 0))[1])
                        nc.vector.tensor_copy(vals[:, :, :, HD], twice[:, :].unsqueeze(2).broadcast_to((P, TT, H))
                                              ).then_inc(v_sum_ready, 1)
                    if kind in ("q", "k"):
                        slot, _ = pj(b, (kind, i))
                        dv.wait_ge(qk_hi, b * (2 * NPAIR) + 2 * i + (1 if kind == "q" else 2))
                        if kind == "q":
                            ins = nc.vector.scalar_tensor_tensor(q_lo[:, i % 2, :], pj_bank[slot][:, :], HD ** -0.5,
                                                                 q_hi[:, i % 2, :].bitcast(F32), ALU.mult,
                                                                 ALU.subtract)
                        else:
                            ins = nc.vector.tensor_tensor(k_lo[:, i % 2, :], pj_bank[slot][:, :],
                                                          k_hi[:, i % 2, :].bitcast(F32), ALU.subtract)
                        ins.then_inc(qk_lo, 1)
                    if kind == "s":
                        dv.wait_ge(s_ready, b * NU + i + 1)
                        blocks = unit_blocks(i % UNITS)
                        if i % UNITS == UNITS - 1:
                            ins = nc.vector.tensor_reduce(nmax[:, i % 4, :],
                                                          s_bank[i % 2][:, :].rearrange("p (h k) -> p h k", h=2),
                                                          AX.X, ALU.max, negate=True)
                        else:
                            for n, (_, _, c0, nk) in enumerate(blocks):
                                ins = nc.vector.tensor_reduce(nmax[:, i % 4, n:n + 1], s_bank[i % 2][:, c0:c0 + nk],
                                                              AX.X, ALU.max, negate=True)
                        ins.then_inc(max_ready, 1)
                    if kind == "t":
                        slot, ready = pt(b, (kind, i))
                        dv.wait_ge(pt_ready, ready)
                        if i >= 2:
                            dv.wait_ge(pv_ready, b * NU + i - 1)
                        nc.vector.tensor_copy(probs_t[:, i % 2, :], pt_bank[slot][:, :]).then_inc(ts_ready, 1)
                    if kind == "pv":
                        p, u = divmod(i, UNITS)
                        dv.wait_ge(pv_ready, b * NU + i + 1)
                        if u == 0 and p >= 2:
                            dv.wait_ge(pt_ready, pt(b, ("ot", p - 2))[1])
                        n = len(unit_blocks(u))
                        src = o_bank[i % 2][:, 0:n * VW].rearrange("p (n v) -> p n v", n=n)
                        if u < 2:
                            dst = o_norm[:, p % 2, 3:4, u, :]
                        elif u < 4:
                            dst = o_norm[:, p % 2, 0:3:2, u - 2, :]
                        else:
                            dst = o_norm[:, p % 2, 1, :, :]
                        step(nc.vector.reciprocal(o_rden[:, i % 2, 0:n], src[:, :, HD]))
                        nc.vector.tensor_tensor(dst, src[:, :, 0:HD], o_rden[:, i % 2, 0:n].unsqueeze(2).broadcast_to((P, n, HD)),
                                                ALU.mult).then_inc(o_copied, 1)
                    if kind == "stats":
                        stats(b + 1)
                    if kind == "dot":
                        dot(b + 1)
                    if kind == "score":
                        score_row(b, b + 1)
                    if kind == "rank":
                        rank(b, b + 1, i)
                    if kind == "ht":
                        normed(b, b + 1, i)
                    if kind == "out":
                        slot, ready = pj(b, (kind, i))
                        dv.wait_ge(pj_ready, ready)
                        dv.wait_ge(xr_ready, b * TT + i + 1)
                        nc.vector.tensor_tensor(xr[:, i % 2, :], pj_bank[slot][:, :], xr[:, i % 2, :],
                                                ALU.add).then_inc(y_ready, 1)

        @block.tensor
        def _(pe):
            def product(out, lhs_hi, lhs_lo, rhs_hi, rhs_lo, start, stop):
                nc.tensor.matmul(out, lhs_hi, rhs_hi, start=start, stop=False)
                nc.tensor.matmul(out, lhs_lo, rhs_hi, start=False, stop=False)
                return nc.tensor.matmul(out, lhs_hi, rhs_lo, start=False, stop=stop)

            def pt_empty(b, key):
                if b is None:
                    if PT0[key] >= 2:
                        pe.wait_ge(ht_lo_ready, PT0[key] - 1)
                elif before_use(PT, key):
                    taken(pe, b, before_use(PT, key))
                else:
                    pe.wait_ge(ht_lo_ready, b * DC + DC)
                    pe.wait_ge(row_copied, b + 1)

            def pj_empty(b, key):
                if before_use(PROJ, key):
                    taken(pe, b, before_use(PROJ, key))
                else:
                    pe.wait_ge(y_ready, b * TT + 1)

            def transposed(b, n, c):
                slot, _ = pt(b, ("ht", c))
                if c == 0:
                    pe.wait_ge(h_ready, n * TT + TT)
                pt_empty(b, ("ht", c))
                for t in range(TT):
                    ins = nc.tensor.transpose(pt_bank[slot][:, P * t:P * t + P], xb[:, t, P * c:P * c + P], ident[:, :])
                ins.then_inc(pt_ready, 1)

            def score_rows(b, n):
                slot, _ = pt(b, ("score", 0))
                pe.wait_ge(score_ready, n + 1)
                pt_empty(b, ("score", 0))
                for t in range(TT):
                    ins = nc.tensor.transpose(pt_bank[slot][:, P * t:P * t + P],
                                              score[:, t:t + 1].broadcast_to((P, P)), ident[:, :])
                ins.then_inc(pt_ready, 1)

            pe.wait_ge(const_made, N_CONST)
            for c in range(DC):
                transposed(None, 0, c)
            score_rows(None, 0)
            with pe.Fori(0, B) as b:
                for kind, i in plan:
                    if kind == "v":
                        t, hw = divmod(i, 2)
                        slot, _ = pj(b, (kind, i))
                        if i == 0:
                            pe.wait_ge(ht_lo_ready, b * DC + DC)
                        if i < 2:
                            pe.wait_ge(split_lo, 1 + i)
                        pj_empty(b, (kind, i))
                        for c in range(DC):
                            ins = product(pj_bank[slot][:, :], ht_hi[:, c, P * t:P * t + P], ht_lo[:, c, P * t:P * t + P],
                                          w_hi["v"][:, c, 512 * hw:512 * hw + 512],
                                          w_lo["v"][:, c, 512 * hw:512 * hw + 512], c == 0, c == DC - 1)
                        ins.then_inc(pj_ready, 1)
                    if kind in ("q", "k"):
                        slot, _ = pj(b, (kind, i))
                        pe.wait_ge(split_lo, 4 if i < NPAIR // 2 else 6)
                        pj_empty(b, (kind, i))
                        for c in range(DC):
                            ins = product(pj_bank[slot][:, :], w_hi[kind][:, c, P * i:P * i + P],
                                          w_lo[kind][:, c, P * i:P * i + P], ht_hi[:, c, :], ht_lo[:, c, :],
                                          c == 0, c == DC - 1)
                        ins.then_inc(pj_ready, 1)
                    if kind == "s":
                        p, u = divmod(i, UNITS)
                        slot = i % 2
                        if u == 0:
                            pe.wait_ge(qk_lo, b * (2 * NPAIR) + 2 * p + 2)
                        if i >= 2:
                            pe.wait_ge(p_ready, b * NU + i - 1)
                        for h, t, c0, nk in unit_blocks(u):
                            if u == UNITS - 1 and h == 1:
                                ins.then_inc(s_half, 1)
                                pe.wait_ge(s_half, b * NPAIR + p + 1)
                            rows = slice(HD * h, HD * h + HD)
                            product(s_bank[slot][:, c0:c0 + nk],
                                    q_hi[rows, p % 2, P * t:P * t + P], q_lo[rows, p % 2, P * t:P * t + P],
                                    k_hi[rows, p % 2, 0:nk], k_lo[rows, p % 2, 0:nk], True, False)
                            ins = nc.tensor.matmul(s_bank[slot][:, c0 + nk - P:c0 + nk], ident_b[:, :], causal_b[:, :],
                                                   start=False, stop=True)
                        ins.then_inc(s_ready, 1)
                    if kind == "t":
                        slot, _ = pt(b, (kind, i))
                        pe.wait_ge(p_ready, b * NU + i + 1)
                        pt_empty(b, (kind, i))
                        for j in range(4):
                            ins = nc.tensor.transpose(pt_bank[slot][:, P * j:P * j + P], probs[:, i % 2, P * j:P * j + P],
                                                      ident[:, :])
                        ins.then_inc(pt_ready, 1)
                    if kind == "pv":
                        p, u = divmod(i, UNITS)
                        slot = i % 2
                        if i == 0:
                            pe.wait_ge(v_ready, b * (2 * TT) + 2 * TT)
                            pe.wait_ge(v_sum_ready, b + 1)
                        pe.wait_ge(ts_ready, b * NU + i + 1)
                        if i >= 2:
                            pe.wait_ge(o_copied, b * NU + i - 1)
                        for n, (h, t, c0, nk) in enumerate(unit_blocks(u)):
                            o0 = n * VW
                            for kt in range(nk // P):
                                ins = nc.tensor.matmul(o_bank[slot][:, o0:o0 + VW],
                                                       probs_t[:, i % 2, c0 + P * kt:c0 + P * kt + P],
                                                       vals[:, kt, 2 * p + h, :], start=(kt == 0), stop=(kt == nk // P - 1))
                        ins.then_inc(pv_ready, 1)
                    if kind == "ot":
                        slot, _ = pt(b, (kind, i))
                        pe.wait_ge(o_copied, b * NU + UNITS * (i + 1))
                        pt_empty(b, (kind, i))
                        for t in range(TT):
                            ins = nc.tensor.transpose(pt_bank[slot][:, P * t:P * t + P], o_norm[:, i % 2, t, :, :].rearrange("p h d -> p (h d)"), ident[:, :])
                        ins.then_inc(pt_ready, 1)
                    if kind == "score":
                        score_rows(b, b + 1)
                    if kind == "ht":
                        transposed(b, b + 1, i)
                    if kind == "out":
                        slot, _ = pj(b, (kind, i))
                        if i == 0:
                            pe.wait_ge(ot_ready, b * NPAIR + NPAIR)
                            pe.wait_ge(wo_in, 16)
                        pj_empty(b, (kind, i))
                        for c in range(NPAIR):
                            ins = nc.tensor.matmul(pj_bank[slot][:, :], o_t[:, c, P * i:P * i + P], w_o[:, c, :],
                                                   start=(c == 0), stop=(c == NPAIR - 1))
                        ins.then_inc(pj_ready, 1)


SK = 77
XH, XD = 16, 32
CH = P // XD
VX = XD + 1
FILL = -1e20
KEEP = 64
NSEL = B * KEEP


def cross_plan():
    plan = [("stats", 0), ("ctx", 0), ("ctx", 1), ("ctx", 2), ("ctx", 3)]
    for s in range(2 * TT + 5):
        if s < 2 * TT:
            if s % 2 == 0:
                plan.append(("turn", s // 2))
            plan.append(("e", s))
        for kind, lag in (("max", 1), ("t", 2), ("pv", 3)):
            if lag <= s < 2 * TT + lag:
                plan.append((kind, s - lag))
    return plan


def router_plan():
    return ([("norm", t) for t in range(TT)] + [("dot", 0), ("row", 0)] + [("rank", t) for t in range(TT)]
            + [("pick", 0), ("xs", 0), ("a1", 0)] + [("base", t) for t in range(TT)])


def cross_and_router(nc, x1, ctx_in, mask, wq, wk, wv, amask, pos, router_w, router_b, base,
                     xsel_t, info_t, picked, mask_rows, later):
    with ExitStack() as ctx:
        def sb(name, shape, dt=F32):
            return ctx.enter_context(nc.sbuf_tensor(name, shape, dt))

        def banks(name, n=1):
            return ctx.enter_context(nc.psum_tensor(name, [P, n, 512] if n > 1 else [P, 512], F32))

        def sem(name):
            return ctx.enter_context(nc.semaphore(name))

        xt = sb("xt", [P, 2, TT, D])
        xl = sb("xl", [P, 2, D])
        xl_t = sb("xl_t", [P, 2, D])
        e = sb("e", [P, 4, 2 * CH, SK])
        fill = sb("fill", [P, 2, 2 * CH, SK])
        mk = sb("mk", [P, TT, SK])
        e_max = sb("e_max", [P, 2, 2 * CH])
        p_t = sb("p_t", [SK, 2, 2, 512])
        att_den = sb("att_den", [P, 2, 2 * CH])
        att = sb("att", [P, 2, 2 * CH, XD])
        cx = sb("cx", [SK, D])
        cx_t = sb("cx_t", [P, DC, SK])
        key_t = sb("key_t", [P, DC, SK])
        qk_bd = sb("qk_bd", [P, DC, CH, SK])
        vx = sb("vx", [SK, XH, VX])
        w_bd = sb("w_bd", [P, 3, P])
        wq_bt = sb("wq_bt", [P, P])
        ident = sb("x_ident", [P, P])
        rw = sb("rw", [P, D])
        rb = sb("rb", [P, 1])
        am = sb("am", [P, TT, S])
        pos_i = sb("pos_i", [P, TT], I32)
        xl2 = sb("xl2", [P, TT, D])
        row_s = sb("x_row_s", [P, S])
        junk = sb("x_junk", [P, S], BF16)
        before = sb("x_before", [P, S + P * (TT - 1)], I8)
        slots = sb("slots", [P, KEEP])
        bn, mv = sb("x_bn", [P, 2, TT, 6]), sb("x_mv", [P, 2, TT, 2])
        half, minus, eps_ln, ones, idle = (sb(n, [P, TT]) for n in ("x_half", "x_minus", "x_eps", "x_ones", "x_idle"))
        scales = sb("scales", [P, 2, 3, TT])
        RS, NM, NB = range(3)
        info = sb("info", [P, TT, 3])
        cnt = sb("x_cnt", [P, 3, TT])
        stay = sb("stay", [P, TT])
        sel = sb("sel", [P, TT, KEEP])

        e_bank, pt_bank = banks("e_bank", 2), [banks(f"x_pt_bank{i}") for i in range(2)]
        o_bank, t_bank, r_bank = banks("x_o_bank"), banks("t_bank"), [banks(f"r_bank{i}") for i in range(2)]

        x_in = [[sem(f"x_in{p}{t}") for t in range(TT)] for p in range(2)]
        base_out = [[sem(f"base_out{p}{t}") for t in range(TT)] for p in range(2)]
        cx_in, am_in, pos_in, const_in, later_in = (sem(n) for n in ("cx_in", "am_in", "pos_in", "x_const_in", "later_in"))
        idle_v = sb("idle_v", [P, 2])
        made, pool_step, dve_step = sem("x_made"), sem("x_pool_step"), sem("x_dve_step")
        wq_turned, wq_copied = sem("wq_turned"), sem("wq_copied")
        stats_ready, scales_ready, xl_ready, turned, t_copied = (
            sem(n) for n in ("x_stats_ready", "scales_ready", "xl_ready", "turned", "t_copied"))
        e_ready, masked, fill_ready, filled, max_ready, shifted, p_ready = (
            sem(n) for n in ("e_ready", "masked", "fill_ready", "filled", "x_max_ready", "shifted", "x_p_ready"))
        pt_ready, pt_act, pt_dve, pv_ready, att_ready, x2_ready = (
            sem(n) for n in ("x_pt_ready", "pt_act", "pt_dve", "x_pv_ready", "att_ready", "x2_ready"))
        stats2_ready, xl2_ready, info_ready, r_ready, row_copied, sel_ready, xs_copied, a1_copied, base_ready = (
            sem(n) for n in ("stats2_ready", "xl2_ready", "info_ready", "r_ready", "x_row_copied", "sel_ready",
                             "xs_copied", "a1_copied", "base_ready"))

        HALVES, TB, RB = 2 * TT, 4 + TT, 3
        x1_rows = x1.rearrange("b (t p) d -> b p t d", p=P)
        base_rows = base.rearrange("b (t p) d -> b p t d", p=P)
        N_MADE, CONST_IN, ROUNDS = 11, 16 * (3 + 3 * CH), (B - 2) // 2

        def cols(i):
            return slice(256 * (i % 2), 256 * (i % 2) + 256)

        a_plan, r_plan = cross_plan(), router_plan()

        def beside():
            out, r = [], list(r_plan)
            first = next(k for k, s in enumerate(a_plan) if s[0] == "e")
            body = len(a_plan) - first
            for k, s in enumerate(a_plan):
                out.append(("a", s))
                while r and k >= first and (len(r_plan) - len(r)) < (k - first + 1) * len(r_plan) / body:
                    out.append(("r", r.pop(0)))
            return out + [("r", s) for s in r]

        both = beside()

        def run(eng, attend, route, tally=None, per=0):
            def turn(n, par, had):
                for which, (kind, i) in both:
                    if which == "a":
                        attend(kind, i, n, par, had)
                    else:
                        route(kind, i, n - 1, 1 - par)

            def pairs(j):
                turn(2 * j + 1, 1, j)
                turn(2 * j + 2, 0, j + 1)
            for kind, i in a_plan:
                attend(kind, i, 0, 0, 0)
            with eng.Fori(0, ROUNDS) as j:
                if tally:
                    with tally.loop(j, per, ROUNDS):
                        pairs(j)
                else:
                    pairs(j)
            turn(B - 1, 1, ROUNDS)
            for kind, i in r_plan:
                route(kind, i, B - 1, 1)

        def wait(eng, sem_, value):
            if not isinstance(value, int) or value > 0:
                eng.wait_ge(sem_, value)

        block = ctx.enter_context(nc.Block())

        @block.sync
        def _(sp):
            def load_x(n, par, had):
                for t in range(TT):
                    wait(sp, base_out[par][t], 16 * had)
                    sp.dma_start(xt[:, par, t, :], x1_rows[n][:, t, :]).then_inc(x_in[par][t], 16)

            def load_context(n):
                wait(sp, turned, n * TB - TB + 1 if isinstance(n, int) else n * TB - (TB - 1))
                sp.dma_start(cx[:, :], ctx_in[n]).then_inc(cx_in, 16)

            def store(n, par):
                for t in range(TT):
                    sp.wait_ge(base_ready, n * TT + t + 1)
                    sp.dma_start(base_rows[n][:, t, :], xt[:, par, t, :]).then_inc(base_out[par][t], 16)

            def load_router(n, m):
                wait(sp, r_ready, n * RB)
                sp.dma_start(am[:, :, :], amask[m, 0, 0:S, 0:S].rearrange("(t p) k -> p t k", p=P)).then_inc(am_in, 16)
                wait(sp, info_ready, n * 1)
                with nc.allow_non_contiguous_dma(reason="512 numbers"):
                    sp.dma_start(pos_i[:, :], pos[m, 0:S].rearrange("(t p) -> p t", p=P)).then_inc(pos_in, 16)

            def turn(n, par, had, m):
                load_x(n, par, had)
                load_context(n)
                store(n - 1, 1 - par)
                load_router(n, m)

            load_x(0, 0, 0)
            load_context(0)
            sp.dma_start(mk[:, :, :], mask[0, 0].rearrange("(t p) k -> p t k", p=P)).then_inc(const_in, 16)
            sp.dma_start(rw[:, :], router_w.rearrange("d o -> o d").broadcast_to((P, D))).then_inc(const_in, 16)
            sp.dma_start(rb[:, :], router_b.rearrange("(o d) -> o d", o=1).broadcast_to((P, 1))).then_inc(const_in, 16)
            sp.wait_ge(made, N_MADE)
            for k, w in enumerate((wq, wk, wv)):
                for h in range(CH):
                    rows = slice(XD * h, XD * h + XD)
                    sp.dma_start(w_bd[rows, k, rows], w[:, :]).then_inc(const_in, 16)
            load_router(0, 0)
            for dst, src in later:
                sp.dma_start(dst, src).then_inc(later_in, 16)
            last_m = amask.shape[0] - 1
            for n in (1, 2, 3, 4):
                turn(n, n % 2, n // 2, min(n, last_m))
            with sp.Fori(2, ROUNDS) as j:
                turn(2 * j + 1, 1, j, last_m)
                turn(2 * j + 2, 0, j + 1, last_m)
            turn(B - 1, 1, ROUNDS, last_m)
            store(B - 1, 1)
            for par in range(2):
                for t in range(TT):
                    sp.wait_ge(base_out[par][t], 16 * B // 2)
            sp.wait_ge(later_in, 16 * len(later))

        @block.gpsimd
        def _(pl):
            done = Tally(pool_step)
            done.mark(nc.gpsimd.memset(ident[:, :], 0.0))
            done.mark(nc.gpsimd.memset(before[:, :], 1.0))
            for tile, value in ((half, -0.5), (minus, -1.0), (eps_ln, EPS_LN), (ones, 1.0)):
                nc.gpsimd.memset(tile[:, :], value).then_inc(made, 1)
            nc.gpsimd.memset(w_bd[:, :, :], 0.0).then_inc(made, 1)
            nc.gpsimd.memset(qk_bd[:, :, :, :], 0.0).then_inc(made, 1)
            nc.gpsimd.memset(vx[:, :, XD:VX], 1.0).then_inc(made, 1)
            nc.gpsimd.iota(slots[:, :], [[1, KEEP]], base=0, channel_multiplier=0,
                           allow_small_or_imprecise_dtypes=True).then_inc(made, 1)
            nc.gpsimd.iota(info[:, :, 2:3], [[P, TT]], base=0, channel_multiplier=1,
                           allow_small_or_imprecise_dtypes=True).then_inc(made, 1)
            done.wait(pl)
            nc.gpsimd.affine_select(out=ident[:, :], in_=ident[:, :], compare_op=ALU.not_equal, fill=1.0, base=0,
                                    pattern=[[-1, P]], channel_multiplier=1).then_inc(made, 1)
            nc.gpsimd.affine_select(out=before[:, :], in_=before[:, :], compare_op=ALU.is_gt, fill=0.0,
                                    base=P * (TT - 1), pattern=[[-1, S + P * (TT - 1)]],
                                    channel_multiplier=1).then_inc(made, 1)
            pl.wait_ge(made, N_MADE)

            def step(ins):
                done.mark(ins)
                done.wait(pl)

            def carry():
                done.wait(pl)
                done.mark(nc.gpsimd.tensor_tensor(idle[:, :], ones[:, :], ones[:, :], ALU.mult))

            def scale(r):
                step(nc.gpsimd.tensor_tensor(scales[:, r, RS], mv[:, r, :, 1], eps_ln[:, :], ALU.add))
                step(nc.gpsimd.tensor_tensor(scales[:, r, RS], scales[:, r, RS], half[:, :], ALU.pow))
                step(nc.gpsimd.tensor_tensor(scales[:, r, NM], minus[:, :], mv[:, r, :, 0], ALU.mult))
                step(nc.gpsimd.tensor_tensor(scales[:, r, NB], scales[:, r, NM], scales[:, r, RS], ALU.mult))

            def norm(out, src, r, t, ready):
                carry()
                nc.gpsimd.tensor_scalar(out, src, scales[:, r, RS, t:t + 1], scales[:, r, NB, t:t + 1], ALU.mult,
                                        ALU.add).then_inc(ready, 1)

            def attend(kind, i, n, par, had):
                if kind == "stats":
                    pl.wait_ge(stats_ready, n + 1)
                    scale(0)
                if kind == "turn":
                    wait(pl, turned, n * TB + (CH + i - 1 if i >= 2 else 0))
                    norm(xl[:, i % 2, :], xt[:, par, i, :], 0, i, xl_ready)
                if kind == "e":
                    pl.wait_ge(fill_ready, n * HALVES + i + 1)
                    nc.gpsimd.tensor_tensor(e[:, i % 4], e[:, i % 4], fill[:, i % 2], ALU.add).then_inc(filled, 1)
                if kind == "max":
                    pl.wait_ge(max_ready, n * HALVES + i + 1)
                    nc.gpsimd.tensor_tensor(e[:, i % 4], e[:, i % 4],
                                            e_max[:, i % 2].unsqueeze(2).broadcast_to((P, 2 * CH, SK)),
                                            ALU.add).then_inc(shifted, 1)
                if kind == "pv":
                    pl.wait_ge(att_ready, n * HALVES + i + 1)
                    rows = xt[:, par, i // 2, cols(i)]
                    nc.gpsimd.tensor_tensor(rows, rows, att[:, i % 2].rearrange("p h d -> p (h d)"),
                                            ALU.add).then_inc(x2_ready, 1)

            def route(kind, i, n, par):
                if kind == "norm" and i == TT - 1:
                    pl.wait_ge(stats2_ready, n + 1)
                    scale(1)
                    for t in range(TT):
                        norm(xl2[:, t, :], xt[:, par, t, :], 1, t, xl2_ready)

            run(pl, attend, route, done, 2 * (4 + TT + 4 + TT))

        @block.scalar
        def _(act):
            act.wait_ge(wq_turned, 1)
            nc.scalar.copy(wq_bt[:, :], t_bank[:, 0:P]).then_inc(wq_copied, 1)
            act.wait_ge(made, N_MADE)

            def attend(kind, i, n, par, had):
                if kind == "ctx":
                    act.wait_ge(turned, n * TB + i + 1)
                    chunks = t_bank[:, 0:DC * SK].rearrange("p (c k) -> p c k", c=DC)
                    if i == 0:
                        ins = nc.scalar.copy(cx_t[:, :, :], chunks)
                    elif i == 1:
                        ins = nc.scalar.copy(key_t[:, :, :], chunks)
                    elif i == 2:
                        for h in range(CH):
                            rows = slice(XD * h, XD * h + XD)
                            ins = nc.scalar.copy(qk_bd[rows, :, h, :], chunks[rows])
                    else:
                        ins = nc.scalar.copy(vx[:, :, 0:XD], t_bank[0:SK, :].rearrange("p (h d) -> p h d", d=XD))
                    ins.then_inc(t_copied, 1)
                if kind == "turn":
                    act.wait_ge(turned, n * TB + CH + i + 1)
                    wait(act, e_ready, n * HALVES + (2 * i - 2 if i >= 2 else 0))
                    nc.scalar.copy(xl_t[:, i % 2, :], t_bank[:, :]).then_inc(t_copied, 1)
                if kind == "max":
                    act.wait_ge(shifted, n * HALVES + i + 1)
                    nc.scalar.activation(e[:, i % 4], e[:, i % 4], ACT.Exp).then_inc(p_ready, 1)
                if kind == "t":
                    act.wait_ge(pt_ready, n * HALVES + i + 1)
                    wait(act, pv_ready, n * HALVES + i - 1)
                    nc.scalar.copy(p_t[:, i % 2, 0, :], pt_bank[0][0:SK, :]).then_inc(pt_act, 1)

            run(act, attend, lambda *a: None)

        @block.vector
        def _(dv):
            done = Tally(dve_step)

            def step(ins):
                done.mark(ins)
                done.wait(dv)

            def aggregate(r, ready):
                done.wait(dv)
                nc.vector.memset(idle_v[:, r:r + 1], 0.0)
                for t in range(TT):
                    ins = nc.vector.bn_aggr(mv[:, r, t, :], bn[:, r, t, :])
                ins.then_inc(ready, 1)

            def attend(kind, i, n, par, had):
                if kind == "stats":
                    wait(dv, xl_ready, n * TT)
                    for t in range(TT):
                        dv.wait_ge(x_in[par][t], 16 * had + 16)
                        done.mark(nc.vector.bn_stats(bn[:, 0, t, :], xt[:, par, t, :]))
                    aggregate(0, stats_ready)
                if kind == "e":
                    four = (P, 2, CH, SK)
                    dv.wait_ge(e_ready, n * HALVES + i + 1)
                    wait(dv, pt_ready, n * HALVES + i - 3)
                    nc.vector.tensor_tensor(e[:, i % 4].rearrange("p (c h) k -> p c h k", c=2),
                                            e_bank[:, :, 0:CH * SK].rearrange("p c (h k) -> p c h k", h=CH),
                                            mk[:, i // 2, :].unsqueeze(1).unsqueeze(1).broadcast_to(four),
                                            ALU.mult).then_inc(masked, 1)
                    dv.wait_ge(masked, n * HALVES + i + 1)
                    wait(dv, filled, n * HALVES + i - 1)
                    nc.vector.tensor_scalar(fill[:, i % 2], e[:, i % 4], 0.0, FILL, ALU.is_equal,
                                            ALU.mult).then_inc(fill_ready, 1)
                if kind == "max":
                    dv.wait_ge(filled, n * HALVES + i + 1)
                    wait(dv, shifted, n * HALVES + i - 1)
                    nc.vector.tensor_reduce(e_max[:, i % 2], e[:, i % 4], AX.X, ALU.max,
                                            negate=True).then_inc(max_ready, 1)
                if kind == "t":
                    dv.wait_ge(pt_ready, n * HALVES + i + 1)
                    wait(dv, pv_ready, n * HALVES + i - 1)
                    nc.vector.tensor_copy(p_t[:, i % 2, 1, :], pt_bank[1][0:SK, :]).then_inc(pt_dve, 1)
                if kind == "pv":
                    dv.wait_ge(pv_ready, n * HALVES + i + 1)
                    o = o_bank[:, 0:2 * CH * VX].rearrange("p (h v) -> p h v", v=VX)
                    step(nc.vector.reciprocal(att_den[:, i % 2], o[:, :, XD]))
                    wait(dv, x2_ready, n * HALVES + i - 1)
                    nc.vector.tensor_tensor(att[:, i % 2], o[:, :, 0:XD],
                                            att_den[:, i % 2].unsqueeze(2).broadcast_to((P, 2 * CH, XD)),
                                            ALU.mult).then_inc(att_ready, 1)

            def route(kind, i, n, par):
                batch = bass.ts(n, KEEP)
                if kind == "norm":
                    dv.wait_ge(x2_ready, n * HALVES + 2 * i + 2)
                    done.mark(nc.vector.bn_stats(bn[:, 1, i, :], xt[:, par, i, :]))
                    if i == TT - 1:
                        aggregate(1, stats2_ready)
                if kind == "dot":
                    dv.wait_ge(xl2_ready, n * TT + TT)
                    for t in range(TT):
                        step(nc.vector.tensor_tensor_reduce(junk[:, :], xl2[:, t, :], rw[:, :], 1.0, 0.0, ALU.mult,
                                                            ALU.add, info[:, t, 0:1]))
                    step(nc.vector.tensor_scalar(info[:, :, 0], info[:, :, 0], rb[:, 0:1], None, ALU.add))
                    dv.wait_ge(pos_in, n * 16 + 16)
                    nc.vector.tensor_copy(info[:, :, 1], pos_i[:, :]).then_inc(info_ready, 1)
                if kind == "row":
                    dv.wait_ge(r_ready, n * RB + 1)
                    nc.vector.tensor_copy(row_s[:, :], r_bank[0][:, :]).then_inc(row_copied, 1)
                    dv.wait_ge(row_copied, n + 1)
                if kind == "rank":
                    w = info[:, i, 0:1]
                    y0 = P * (TT - 1 - i)
                    step(nc.vector.tensor_scalar(junk[:, :], row_s[:, :], w, None, ALU.is_gt, ALU.add,
                                                 accum_out=cnt[:, 0, i:i + 1]))
                    step(nc.vector.scalar_tensor_tensor(junk[:, :], row_s[:, :], w, before[:, y0:y0 + S],
                                                        ALU.is_equal, ALU.mult, accum_out=cnt[:, 1, i:i + 1]))
                    step(nc.vector.tensor_scalar(junk[:, :], row_s[:, :], w, None, ALU.is_ge, ALU.add,
                                                 accum_out=cnt[:, 2, i:i + 1]))
                if kind == "pick":
                    step(nc.vector.tensor_tensor(cnt[:, 0, :], cnt[:, 0, :], cnt[:, 1, :], ALU.add))
                    step(nc.vector.tensor_scalar(stay[:, :], cnt[:, 2, :], KEEP - 0.5, None, ALU.is_gt))
                    for t in range(TT):
                        ins = nc.vector.tensor_scalar(sel[:, t, :], slots[:, :], cnt[:, 0, t:t + 1], None, ALU.is_equal)
                    ins.then_inc(sel_ready, 1)
                    dv.wait_ge(sel_ready, n + 1)
                    nc.vector.tensor_scalar(picked[:, :, batch], sel[:, :, :], 1.0, None, ALU.mult)
                if kind == "xs":
                    dv.wait_ge(r_ready, n * RB + 2)
                    nc.vector.tensor_scalar(xsel_t[:, :, batch],
                                            r_bank[1][:, 0:DC * KEEP].rearrange("p (c s) -> p c s", c=DC), 1.0, None,
                                            ALU.mult)
                    nc.vector.tensor_scalar(info_t[0:3, batch], r_bank[1][0:3, DC * KEEP:DC * KEEP + KEEP], 1.0, None,
                                            ALU.mult).then_inc(xs_copied, 1)
                if kind == "a1":
                    dv.wait_ge(r_ready, n * RB + 3)
                    nc.vector.tensor_scalar(mask_rows[:, :, batch],
                                            r_bank[0][:, 0:TT * KEEP].rearrange("p (c s) -> p c s", c=TT), 1.0, None,
                                            ALU.mult).then_inc(a1_copied, 1)
                if kind == "base":
                    rows = xt[:, par, i, :]
                    nc.vector.scalar_tensor_tensor(rows, xl2[:, i, :], stay[:, i:i + 1], rows, ALU.mult,
                                                   ALU.add).then_inc(base_ready, 1)

            dv.wait_ge(made, N_MADE)
            dv.wait_ge(const_in, CONST_IN)
            run(dv, attend, route, done, 2 * (TT + HALVES + TT + TT + 1 + 3 * TT + 2))

        @block.tensor
        def _(pe):
            pe.wait_ge(made, N_MADE)
            pe.wait_ge(const_in, CONST_IN)
            nc.tensor.transpose(t_bank[:, 0:P], w_bd[:, 0, :], ident[:, :]).then_inc(wq_turned, 1)
            pe.wait_ge(wq_copied, 1)

            def attend(kind, i, n, par, had):
                if kind == "ctx":
                    if i == 0:
                        pe.wait_ge(cx_in, n * 16 + 16)
                    wait(pe, t_copied, n * TB + i)
                    if i == 0:
                        for c in range(DC):
                            ins = nc.tensor.transpose(t_bank[:, SK * c:SK * c + SK], cx[:, P * c:P * c + P],
                                                      ident[0:SK, 0:SK])
                    elif i == 1:
                        ins = nc.tensor.matmul(t_bank[:, 0:DC * SK], w_bd[:, 1, :],
                                               cx_t[:, :, :].rearrange("p c k -> p (c k)"), start=True, stop=True)
                    elif i == 2:
                        ins = nc.tensor.matmul(t_bank[:, 0:DC * SK], wq_bt[:, :],
                                               key_t[:, :, :].rearrange("p c k -> p (c k)"), start=True, stop=True)
                    else:
                        for c in range(DC):
                            ins = nc.tensor.matmul(t_bank[0:SK, P * c:P * c + P], cx_t[:, c, :], w_bd[:, 2, :],
                                                   start=True, stop=True)
                    ins.then_inc(turned, 1)
                if kind == "turn":
                    pe.wait_ge(xl_ready, n * TT + i + 1)
                    wait(pe, t_copied, n * TB + CH + i)
                    for c in range(DC):
                        ins = nc.tensor.transpose(t_bank[:, P * c:P * c + P], xl[:, i % 2, P * c:P * c + P], ident[:, :])
                    ins.then_inc(turned, 1)
                if kind == "e":
                    pe.wait_ge(t_copied, n * TB + CH + i // 2 + 1)
                    wait(pe, masked, n * HALVES + i)
                    for c in range(2):
                        k = 2 * (i % 2) + c
                        ins = nc.tensor.matmul(e_bank[:, c, 0:CH * SK], xl_t[:, (i // 2) % 2, P * k:P * k + P],
                                               qk_bd[:, k].rearrange("p h k -> p (h k)"), start=True, stop=True)
                    ins.then_inc(e_ready, 1)
                if kind == "t":
                    pe.wait_ge(p_ready, n * HALVES + i + 1)
                    wait(pe, pt_act, n * HALVES + i)
                    wait(pe, pt_dve, n * HALVES + i)
                    for h in range(2 * CH):
                        ins = nc.tensor.transpose(pt_bank[h // CH][0:SK, P * (h % CH):P * (h % CH) + P], e[:, i % 4, h, :],
                                                  ident[:, :])
                    ins.then_inc(pt_ready, 1)
                if kind == "pv":
                    pe.wait_ge(pt_act, n * HALVES + i + 1)
                    pe.wait_ge(pt_dve, n * HALVES + i + 1)
                    wait(pe, att_ready, n * HALVES + i)
                    for h in range(2 * CH):
                        ins = nc.tensor.matmul(o_bank[:, VX * h:VX * h + VX],
                                               p_t[:, i % 2, h // CH, P * (h % CH):P * (h % CH) + P],
                                               vx[:, 2 * CH * (i % 2) + h, :], start=True, stop=True)
                    ins.then_inc(pv_ready, 1)

            def route(kind, i, n, par):
                if kind == "row":
                    pe.wait_ge(info_ready, n + 1)
                    for t in range(TT):
                        ins = nc.tensor.transpose(r_bank[0][:, P * t:P * t + P], info[:, t, 0:1].broadcast_to((P, P)),
                                                  ident[:, :])
                    ins.then_inc(r_ready, 1)
                if kind == "xs":
                    pe.wait_ge(sel_ready, n + 1)
                    for c in range(DC):
                        for t in range(TT):
                            nc.tensor.matmul(r_bank[1][:, KEEP * c:KEEP * c + KEEP], xl2[:, t, P * c:P * c + P],
                                             sel[:, t, :], start=(t == 0), stop=(t == TT - 1))
                    for t in range(TT):
                        ins = nc.tensor.matmul(r_bank[1][0:3, DC * KEEP:DC * KEEP + KEEP], info[:, t, :], sel[:, t, :],
                                               start=(t == 0), stop=(t == TT - 1))
                    ins.then_inc(r_ready, 1)
                if kind == "a1":
                    pe.wait_ge(am_in, n * 16 + 16)
                    for c in range(TT):
                        for t in range(TT):
                            ins = nc.tensor.matmul(r_bank[0][:, KEEP * c:KEEP * c + KEEP], am[:, t, P * c:P * c + P],
                                                   sel[:, t, :], start=(t == 0), stop=(t == TT - 1))
                    ins.then_inc(r_ready, 1)

            run(pe, attend, route)


FH, FD = 16, 32
FF = 2048
FC = FF // P
FV = FD + 1
ROPE_BASE = 10000.0
TURN = 2 * np.pi
TURN_PARTS = (6.28125, 1.93500518798828125e-3, 3.0199159795074593e-7)
ROUNDING = 1.5 * 2.0 ** 23
HALF_TURN = float(np.nextafter(np.float32(np.pi), np.float32(0)))
NT = NSEL // P


def routed_plan():
    plan = [("info", 0), ("mask", 0)] + [("xs", t) for t in range(NT)]
    plan += [(k, 0) for k in ("q", "k", "v", "tq", "tk")] + [(k, 1) for k in ("q", "k", "v")]
    units = NT * DC
    for s in range(units + 8):
        if s < units:
            plan.append(("s", s))
            t, c = divmod(s, DC)
            if c == 0 and 1 <= t < NT - 1:
                plan += [(k, t + 1) for k in ("q", "k")]
            if c == 1 and t + 1 < NT:
                plan += [("tq", t + 1), ("tk", t + 1)]
            if c == 2 and 1 <= t < NT - 1:
                plan.append(("v", t + 1))
        if 1 <= s < units + 1:
            plan.append(("t", s - 1))
        if 2 <= s < units + 2:
            plan.append(("pv", s - 2))
        if s >= DC + 2 and (s - DC - 2) % DC == 0 and (s - DC - 2) // DC < NT:
            plan.append(("ot", (s - DC - 2) // DC))
        if s >= DC + 3 and (s - DC - 3) % DC == 0 and (s - DC - 3) // DC < NT:
            plan.append(("wo", (s - DC - 3) // DC))
        if s >= DC + 5 and (s - DC - 5) % DC == 0 and (s - DC - 5) // DC < NT:
            plan.append(("th", (s - DC - 5) // DC))
    plan += [("th", t) for t in range(NT) if ("th", t) not in plan]
    return plan + [("w1", f) for f in range(FC)] + [("w2", t) for t in range(NT)]


def routed_block(nc, xsel_t, info_t, picked, mask_rows, w4, ln1, ln2, w1, w2, out):
    plan = routed_plan()
    RINGS = {}
    for name, kinds in (("big", ("q", "k", "v", "wo", "w1", "w2")), ("turn", ("xs", "tq", "tk", "t", "ot", "th")),
                        ("score", ("s",)), ("small", ("info", "mask", "pv"))):
        keys = [s for s in plan if s[0] in kinds]
        for n, key in enumerate(keys):
            RINGS[key] = (name, n % 2, keys[n - 2] if n >= 2 else None)
    KINDS = sorted({s[0] for s in plan})
    with ExitStack() as ctx:
        def sb(name, shape, dt=F32):
            return ctx.enter_context(nc.sbuf_tensor(name, shape, dt))

        def sem(name):
            return ctx.enter_context(nc.semaphore(name))

        w1_sb, w2_sb = sb("w1_sb", [P, DC, FF]), sb("w2_sb", [P, FC, D])
        xs = sb("xs", [P, NT, D])
        x1f = sb("x1f", [P, NT, D])
        h_t = xsel_t
        h2_t = mask_rows
        g_t = w4
        rot, rot_b = sb("rot", [P, 2, D]), sb("rot_b", [P, 2, D])
        q_t = sb("q_t", [P, 2, DC, P])
        k_bd = sb("k_bd", [P, 2, DC, CH, P])
        v_sb = sb("v_sb", [P, 2, FH, FV])
        e = sb("f_e", [P, 2, CH, P])
        p_t = sb("f_p_t", [P, 2, CH, P])
        o_n = sb("f_o_n", [P, 2, D])
        o_t = sb("f_o_t", [P, 2, DC, P])
        hn = sb("hn", [P, 2, D])
        m_full = sb("m_full", [P, NT, P])
        m_slot = sb("m_slot", [P, P])
        fin = picked
        junk = sb("f_junk", [P, D], BF16)
        ident = sb("f_ident", [P, P])
        l1, l2 = sb("l1", [P, DC]), sb("l2", [P, DC])
        info = sb("f_info", [P, NT, 3])
        idx = sb("idx", [P, NT], U32)
        first_row, live, inv = sb("first_row", [P, NT]), sb("live", [P, 1]), sb("inv", [P, FD // 2])
        half = sb("f_half", [P, NT])
        w_sel = sb("w_sel", [P, NT])
        ang, turns, sc = sb("ang", [P, NT, 16]), sb("turns", [P, 2, NT, 16]), sb("sc", [P, 2, NT, 16])
        minus_sin = sb("minus_sin", [P, NT, 16])
        ss, ss2 = sb("ss", [P, NT]), sb("ss2", [P, NT])
        r1, rq, r2 = sb("r1", [P, 2, NT]), sb("rq", [P, NT]), sb("r2", [P, 2, NT])
        nmax, den = sb("f_nmax", [P, 2, CH]), sb("f_den", [P, 2, CH])

        banks = {n: [ctx.enter_context(nc.psum_tensor(f"{n}_bank{i}", [P, 512], F32)) for i in range(2)]
                 for n in ("big", "turn", "score", "small")}
        made = {k: sem(f"{k}_made") for k in KINDS}
        read = {k: sem(f"{k}_read") for k in KINDS}
        w1_in, w2_in, ln_in, idx_ready, rows_in, out_done = (
            sem(n) for n in ("w1_in", "w2_in", "ln_in", "idx_ready", "rows_in", "out_done"))
        const, pool_step, dve_step, act_step = (sem(n) for n in ("f_const", "f_pool_step", "f_dve_step", "f_act_step"))
        ht_ready, angles_ready, sincos_ready, ss_ready, r1_ready = (
            sem(n) for n in ("ht_ready", "angles_ready", "sincos_ready", "ss_ready", "r1_ready"))
        rot_ready, fmax_ready, exp_ready, ss2_ready, hn_ready, fin_ready = (
            sem(n) for n in ("rot_ready", "fmax_ready", "exp_ready", "ss2_ready", "hn_ready", "fin_ready"))

        def bank(key):
            name, slot, _ = RINGS[key]
            return banks[name][slot]

        N_CONST_MADE = 1
        out_rows = out.rearrange("b s d -> (b s) d")
        block = ctx.enter_context(nc.Block())

        @block.sync
        def _(sp):
            with nc.allow_non_contiguous_dma(reason="one column per chunk"):
                for dst, src in ((l1, ln1), (l2, ln2)):
                    sp.dma_start(dst[:, :], src.rearrange("(c p) -> p c", p=P)).then_inc(ln_in, 16)
            sp.dma_start(w1_sb[:, :, :], w1.rearrange("(c p) f -> p c f", p=P)).then_inc(w1_in, 16)
            sp.dma_start(w2_sb[:, :, :], w2.rearrange("(c p) d -> p c d", p=P)).then_inc(w2_in, 16)

        @block.gpsimd
        def _(pl):
            done = Tally(pool_step)

            def step(ins):
                done.mark(ins)
                done.wait(pl)

            for t in range(NT):
                for b in range(2):
                    step(nc.gpsimd.memset(first_row[KEEP * b:KEEP * b + KEEP, t:t + 1], float(S * (2 * t + b))))
            step(nc.gpsimd.memset(half[:, :], -0.5))
            step(nc.gpsimd.memset(ident[:, :], 0.0))
            step(nc.gpsimd.affine_select(out=ident[:, :], in_=ident[:, :], compare_op=ALU.not_equal, fill=1.0, base=0,
                                         pattern=[[-1, P]], channel_multiplier=1))
            for j in range(FD // 2):
                step(nc.gpsimd.memset(inv[:, j:j + 1], float(np.float32(1.0) / np.float32(ROPE_BASE)
                                                           ** np.float32(2 * j / FD))))
            step(nc.gpsimd.memset(m_slot[:, :], 0.0))
            step(nc.gpsimd.memset(m_slot[0:KEEP, KEEP:P], NEG))
            step(nc.gpsimd.memset(m_slot[KEEP:P, 0:KEEP], NEG))
            step(nc.gpsimd.memset(m_slot[:, KEEP - 1:KEEP], NEG))
            step(nc.gpsimd.memset(m_slot[:, P - 1:P], NEG))
            step(nc.gpsimd.memset(live[:, :], 1.0))
            for last in (KEEP - 1, P - 1):
                step(nc.gpsimd.affine_select(out=live[:, :], in_=live[:, :], compare_op=ALU.not_equal, fill=0.0,
                                             base=-last, pattern=[[0, 1]], channel_multiplier=1))
            step(nc.gpsimd.memset(v_sb[:, :, :, FD:FV], 1.0))
            nc.gpsimd.memset(k_bd[:, :, :, :, :], 0.0).then_inc(const, 1)
            pl.wait_ge(made["mask"], 1)
            pl.wait_ge(idx_ready, 1)
            for t in range(NT):
                nc.gpsimd.indirect_dma_start(fin[:, t, :], None, out_rows, IndirectOffsetOnAxis(ap=idx[:, t:t + 1], axis=0)
                                             ).then_inc(rows_in, 16)
            pl.wait_ge(ss_ready, NT)
            step(nc.gpsimd.tensor_scalar(r1[:, 0], ss[:, :], 1.0 / D, EPS_RMS, ALU.mult, ALU.add))
            step(nc.gpsimd.tensor_tensor(r1[:, 1], r1[:, 0], half[:, :], ALU.pow))
            nc.gpsimd.tensor_scalar(rq[:, :], r1[:, 1], FD ** -0.5, 1.0, ALU.mult, ALU.mult).then_inc(r1_ready, 1)
            for t in range(NT):
                pl.wait_ge(ss2_ready, t + 1)
                step(nc.gpsimd.tensor_scalar(r2[:, 0, t:t + 1], ss2[:, t:t + 1], 1.0 / D, EPS_RMS, ALU.mult, ALU.add))
                step(nc.gpsimd.tensor_tensor(r2[:, 1, t:t + 1], r2[:, 0, t:t + 1], half[:, 0:1], ALU.pow))
                if t >= 2:
                    pl.wait_ge(made["th"], t - 1)
                nc.gpsimd.tensor_scalar(hn[:, t % 2, :], x1f[:, t, :], r2[:, 1, t:t + 1], 1.0, ALU.mult,
                                        ALU.mult).then_inc(hn_ready, 1)
            for t in range(NT):
                pl.wait_ge(fin_ready, t + 1)
                nc.gpsimd.indirect_dma_start(out_rows, IndirectOffsetOnAxis(ap=idx[:, t:t + 1], axis=0), fin[:, t, :], None
                                             ).then_inc(out_done, 16)
            pl.wait_ge(out_done, 16 * NT)

        @block.scalar
        def _(act):
            for kind, i in plan:
                t, c = divmod(i, DC) if kind in ("s", "t", "pv") else (i, 0)
                if kind == "xs":
                    act.wait_ge(made[kind], i + 1)
                    nc.scalar.copy(xs[:, i, :], bank((kind, i))[:, :]).then_inc(read[kind], 1)
                    if i == NT - 1:
                        act.wait_ge(ln_in, 32)
                        for n in range(DC):
                            nc.scalar.activation(h_t[:, n, :], h_t[:, n, :], ACT.Copy,
                                                 scale=l1[:, n:n + 1]).then_inc(ht_ready, 1)
                        act.wait_ge(angles_ready, 1)
                        nc.scalar.activation(sc[:, :, :, :], turns[:, :, :, :], ACT.Sin).then_inc(sincos_ready, 1)
                if kind == "v":
                    act.wait_ge(made[kind], i + 1)
                    act.wait_ge(r1_ready, 1)
                    act.wait_ge(const, N_CONST_MADE)
                    if i >= 2:
                        act.wait_ge(made["pv"], DC * (i - 1))
                    nc.scalar.activation(v_sb[:, i % 2, :, 0:FD], bank((kind, i))[:, :].rearrange("p (h d) -> p h d", d=FD),
                                         ACT.Copy, scale=r1[:, 1, i:i + 1]).then_inc(read[kind], 1)
                if kind == "tq":
                    act.wait_ge(made[kind], i + 1)
                    if i >= 2:
                        act.wait_ge(made["s"], DC * (i - 1))
                    nc.scalar.copy(q_t[:, i % 2].rearrange("p c k -> p (c k)"), bank((kind, i))[:, :]).then_inc(read[kind], 1)
                if kind == "tk":
                    act.wait_ge(made[kind], i + 1)
                    for h in range(CH):
                        rows = slice(FD * h, FD * h + FD)
                        ins = nc.scalar.copy(k_bd[rows, i % 2, :, h, :],
                                             bank((kind, i))[rows, :].rearrange("p (c k) -> p c k", c=DC))
                    ins.then_inc(read[kind], 1)
                if kind == "s":
                    act.wait_ge(fmax_ready, i + 1)
                    for h in range(CH):
                        ins = nc.scalar.activation(e[:, i % 2, h, :], e[:, i % 2, h, :], ACT.Exp,
                                                   bias=nmax[:, i % 2, h:h + 1])
                    ins.then_inc(exp_ready, 1)
                if kind == "ot":
                    act.wait_ge(made[kind], i + 1)
                    if i >= 2:
                        act.wait_ge(made["wo"], i - 1)
                    nc.scalar.copy(o_t[:, i % 2].rearrange("p c k -> p (c k)"), bank((kind, i))[:, :]).then_inc(read[kind], 1)
                if kind == "w1":
                    act.wait_ge(made[kind], i + 1)
                    if i == 0:
                        act.wait_ge(made["wo"], NT)
                    nc.scalar.activation(g_t[:, i // DC, i % DC, :], bank((kind, i))[:, :],
                                         ACT.Gelu_apprx_tanh).then_inc(read[kind], 1)

        @block.vector
        def _(dv):
            done = Tally(dve_step)

            def step(ins):
                done.mark(ins)
                done.wait(dv)

            dv.wait_ge(const, N_CONST_MADE)
            for kind, i in plan:
                t, c = divmod(i, DC) if kind in ("s", "t", "pv") else (i, 0)
                if kind in ("info", "mask", "q", "k", "t", "pv", "wo", "th", "w2", "s"):
                    dv.wait_ge(made[kind], i + 1)
                if kind == "info":
                    nc.vector.tensor_copy(info[:, :, :], bank((kind, i))[:, 0:3 * NT].rearrange("p (t k) -> p t k", k=3)
                                          ).then_inc(read[kind], 1)
                    dv.wait_ge(read[kind], 1)
                    nc.vector.tensor_tensor(idx[:, :], info[:, :, 2], first_row[:, :], ALU.add).then_inc(idx_ready, 1)
                    nc.vector.tensor_scalar(w_sel[:, :], info[:, :, 0], live[:, 0:1], None, ALU.mult)
                    shape = (P, NT, FD // 2)
                    step(nc.vector.tensor_tensor(ang[:, :, :], info[:, :, 1].unsqueeze(2).broadcast_to(shape),
                                                 inv[:, :].unsqueeze(1).broadcast_to(shape), ALU.mult))
                    for n in range(2):
                        step(nc.vector.tensor_scalar(sc[:, n], ang[:, :, :], 1 / TURN, 0.25 * n, ALU.mult, ALU.add))
                        step(nc.vector.tensor_scalar(sc[:, n], sc[:, n], ROUNDING, None, ALU.add))
                        step(nc.vector.tensor_scalar(sc[:, n], sc[:, n], -ROUNDING, None, ALU.add))
                        src = ang[:, :, :]
                        for part in TURN_PARTS:
                            step(nc.vector.scalar_tensor_tensor(turns[:, n], sc[:, n], -part, src, ALU.mult, ALU.add))
                            src = turns[:, n]
                        if n:
                            step(nc.vector.tensor_scalar(turns[:, n], turns[:, n], TURN / 4, None, ALU.add))
                        ins = nc.vector.tensor_scalar(turns[:, n], turns[:, n], HALF_TURN, -HALF_TURN, ALU.min, ALU.max)
                    ins.then_inc(angles_ready, 1)
                if kind == "mask":
                    nc.vector.tensor_tensor(m_full[:, :, :], bank((kind, i))[:, :].rearrange("p (t k) -> p t k", t=NT),
                                            m_slot[:, :].unsqueeze(1).broadcast_to((P, NT, P)), ALU.add
                                            ).then_inc(read[kind], 1)
                if kind == "xs":
                    dv.wait_ge(read["xs"], i + 1)
                    nc.vector.tensor_tensor_reduce(junk[:, :], xs[:, i, :], xs[:, i, :], 1.0, 0.0, ALU.mult, ALU.add,
                                                   ss[:, i:i + 1]).then_inc(ss_ready, 1)
                    dv.wait_ge(ss_ready, i + 1)
                    if i == NT - 1:
                        dv.wait_ge(sincos_ready, 1)
                        step(nc.vector.tensor_scalar(minus_sin[:, :, :], sc[:, 0], -1.0, None, ALU.mult))
                        dv.wait_ge(r1_ready, 1)
                if kind in ("q", "k"):
                    n = 2 * t + (kind == "k")
                    scale = rq[:, t:t + 1] if kind == "q" else r1[:, 1, t:t + 1]
                    b4 = bank((kind, i))[:, :].rearrange("p (h m j) -> p h m j", h=FH, m=2)
                    r4 = rot_b[:, n % 2, :].rearrange("p (h m j) -> p h m j", h=FH, m=2)
                    if n >= 2:
                        dv.wait_ge(made["tq" if kind == "q" else "tk"], t)
                    done.mark(nc.vector.scalar_tensor_tensor(
                        rot[:, n % 2, :].rearrange("p (r j) -> p r j", j=16),
                        bank((kind, i))[:, :].rearrange("p (r j) -> p r j", j=16), scale,
                        sc[:, 1, t, :].unsqueeze(1).broadcast_to((P, 2 * FH, 16)), ALU.mult, ALU.mult))
                    done.mark(nc.vector.scalar_tensor_tensor(
                        r4[:, :, 0, :], b4[:, :, 1, :], scale, minus_sin[:, t, :].unsqueeze(1).broadcast_to((P, FH, 16)),
                        ALU.mult, ALU.mult))
                    nc.vector.scalar_tensor_tensor(
                        r4[:, :, 1, :], b4[:, :, 0, :], scale, sc[:, 0, t, :].unsqueeze(1).broadcast_to((P, FH, 16)),
                        ALU.mult, ALU.mult).then_inc(read[kind], 1)
                    dv.wait_ge(read[kind], i + 1)
                    nc.vector.tensor_tensor(rot[:, n % 2, :], rot[:, n % 2, :], rot_b[:, n % 2, :],
                                            ALU.add).then_inc(rot_ready, 1)
                if kind == "s":
                    if i >= 2:
                        dv.wait_ge(made["t"], i - 1)
                    nc.vector.tensor_tensor(e[:, i % 2], bank((kind, i))[:, :].rearrange("p (h k) -> p h k", h=CH),
                                            m_full[:, t, :].unsqueeze(1).broadcast_to((P, CH, P)),
                                            ALU.add).then_inc(read[kind], 1)
                    dv.wait_ge(read[kind], i + 1)
                    nc.vector.tensor_reduce(nmax[:, i % 2, :], e[:, i % 2], AX.X, ALU.max, negate=True
                                            ).then_inc(fmax_ready, 1)
                if kind == "t":
                    if i >= 2:
                        dv.wait_ge(made["pv"], i - 1)
                    nc.vector.tensor_copy(p_t[:, i % 2].rearrange("p h k -> p (h k)"), bank((kind, i))[:, :]
                                          ).then_inc(read[kind], 1)
                if kind == "pv":
                    o = bank((kind, i))[:, 0:CH * FV].rearrange("p (h v) -> p h v", v=FV)
                    step(nc.vector.reciprocal(den[:, i % 2, :], o[:, :, FD]))
                    if c == 0 and t >= 2:
                        dv.wait_ge(made["ot"], t - 1)
                    nc.vector.tensor_tensor(o_n[:, t % 2, P * c:P * c + P].rearrange("p (h d) -> p h d", h=CH), o[:, :, 0:FD],
                                            den[:, i % 2, :].unsqueeze(2).broadcast_to((P, CH, FD)),
                                            ALU.mult).then_inc(read[kind], 1)
                if kind == "wo":
                    nc.vector.tensor_tensor(x1f[:, i, :], bank((kind, i))[:, :], xs[:, i, :], ALU.add
                                            ).then_inc(read[kind], 1)
                    dv.wait_ge(read[kind], i + 1)
                    nc.vector.tensor_tensor_reduce(junk[:, :], x1f[:, i, :], x1f[:, i, :], 1.0, 0.0, ALU.mult, ALU.add,
                                                   ss2[:, i:i + 1]).then_inc(ss2_ready, 1)
                    dv.wait_ge(ss2_ready, i + 1)
                if kind == "th":
                    nc.vector.tensor_tensor(h2_t[:, :, P * i:P * i + P],
                                            bank((kind, i))[:, :].rearrange("p (c k) -> p c k", c=DC),
                                            l2[:, :].unsqueeze(2).broadcast_to((P, DC, P)), ALU.mult
                                            ).then_inc(read[kind], 1)
                if kind == "w2":
                    nc.vector.tensor_tensor(x1f[:, i, :], bank((kind, i))[:, :], x1f[:, i, :], ALU.add
                                            ).then_inc(read[kind], 1)
                    dv.wait_ge(read[kind], i + 1)
                    dv.wait_ge(rows_in, 16 * NT)
                    nc.vector.scalar_tensor_tensor(fin[:, i, :], x1f[:, i, :], w_sel[:, i:i + 1], fin[:, i, :], ALU.mult,
                                                   ALU.add).then_inc(fin_ready, 1)

        @block.tensor
        def _(pe):
            pe.wait_ge(const, N_CONST_MADE)
            for kind, i in plan:
                before = RINGS[kind, i][2]
                if before:
                    pe.wait_ge(read[before[0]], before[1] + 1)
                to = bank((kind, i))
                t, c = divmod(i, DC) if kind in ("s", "t", "pv") else (i, 0)
                tok = slice(P * i, P * i + P)
                if kind == "info":
                    for n in range(NT):
                        ins = nc.tensor.transpose(to[:, 3 * n:3 * n + 3], info_t[:, P * n:P * n + P], ident[0:3, 0:3])
                if kind == "mask":
                    for n in range(NT):
                        cols = slice(P * n, P * n + P)
                        for k in range(TT):
                            ins = nc.tensor.matmul(to[:, cols], mask_rows[:, k, cols], picked[:, k, cols],
                                                   start=(k == 0), stop=(k == TT - 1))
                if kind == "xs":
                    for n in range(DC):
                        ins = nc.tensor.transpose(to[:, P * n:P * n + P], xsel_t[:, n, tok], ident[:, :])
                if kind in ("q", "k", "v"):
                    pe.wait_ge(ht_ready, DC)
                    for n in range(DC):
                        ins = nc.tensor.matmul(to[:, :], h_t[:, n, tok], w4[:, "qkv".index(kind), n, :],
                                               start=(n == 0), stop=(n == DC - 1))
                if kind in ("tq", "tk"):
                    n = 2 * i + (kind == "tk")
                    pe.wait_ge(rot_ready, n + 1)
                    for k in range(DC):
                        ins = nc.tensor.transpose(to[:, P * k:P * k + P], rot[:, n % 2, P * k:P * k + P], ident[:, :])
                if kind == "s":
                    pe.wait_ge(read["tq"], t + 1)
                    pe.wait_ge(read["tk"], t + 1)
                    ins = nc.tensor.matmul(to[:, :], q_t[:, t % 2, c, :], k_bd[:, t % 2, c].rearrange("p h k -> p (h k)"),
                                           start=True, stop=True)
                if kind == "t":
                    pe.wait_ge(exp_ready, i + 1)
                    for h in range(CH):
                        ins = nc.tensor.transpose(to[:, P * h:P * h + P], e[:, i % 2, h, :], ident[:, :])
                if kind == "pv":
                    pe.wait_ge(read["t"], i + 1)
                    pe.wait_ge(read["v"], t + 1)
                    for h in range(CH):
                        ins = nc.tensor.matmul(to[:, FV * h:FV * h + FV], p_t[:, i % 2, h, :],
                                               v_sb[:, t % 2, CH * c + h, :], start=True, stop=True)
                if kind == "ot":
                    pe.wait_ge(read["pv"], DC * (i + 1))
                    for n in range(DC):
                        ins = nc.tensor.transpose(to[:, P * n:P * n + P], o_n[:, i % 2, P * n:P * n + P], ident[:, :])
                if kind == "wo":
                    pe.wait_ge(read["ot"], i + 1)
                    for n in range(DC):
                        ins = nc.tensor.matmul(to[:, :], o_t[:, i % 2, n, :], w4[:, 3, n, :], start=(n == 0),
                                               stop=(n == DC - 1))
                if kind == "th":
                    pe.wait_ge(hn_ready, i + 1)
                    for n in range(DC):
                        ins = nc.tensor.transpose(to[:, P * n:P * n + P], hn[:, i % 2, P * n:P * n + P], ident[:, :])
                if kind == "w1":
                    pe.wait_ge(w1_in, 16)
                    pe.wait_ge(read["th"], NT)
                    for n in range(DC):
                        ins = nc.tensor.matmul(to[:, :], w1_sb[:, n, P * i:P * i + P], h2_t[:, n, :], start=(n == 0),
                                               stop=(n == DC - 1))
                if kind == "w2":
                    pe.wait_ge(w2_in, 16)
                    pe.wait_ge(read["w1"], FC)
                    for f in range(FC):
                        ins = nc.tensor.matmul(to[:, :], g_t[:, f // DC, f % DC, tok], w2_sb[:, f, :], start=(f == 0),
                                               stop=(f == FC - 1))
                ins.then_inc(made[kind], 1)


def pre_ln_decoder_layer(nc, x, ctx_1024, mask_1x1xSxS2_fk0, L0_attn_norm_w, L0_attn_w_q, L0_attn_w_k, L0_attn_w_v,
                         L0_attn_w_out, L0_attn_scorer_w, L0_attn_scorer_b, L0_xattn_Wq, L0_xattn_Wk, L0_xattn_Wv,
                         L0_ffn_attention_mask, L0_ffn_position_ids, L0_ffn_router_w, L0_ffn_router_b, L0_ffn_wq,
                         L0_ffn_wk, L0_ffn_wv, L0_ffn_wo, L0_ffn_w1, L0_ffn_w2, L0_ffn_ln1, L0_ffn_ln2, out):
    x1 = nc.dram_tensor("x1", [B, S, D], F32, kind="Internal").ap()
    self_attention(nc, x, L0_attn_norm_w, L0_attn_w_q, L0_attn_w_k, L0_attn_w_v, L0_attn_w_out, L0_attn_scorer_w,
                   L0_attn_scorer_b, x1)
    with ExitStack() as ctx:
        def sb(name, shape):
            return ctx.enter_context(nc.sbuf_tensor(name, shape, F32))

        xsel_t, info_t = sb("xsel_t", [P, DC, NSEL]), sb("info_t", [3, NSEL])
        picked, mask_rows = sb("picked", [P, TT, NSEL]), sb("mask_rows", [P, TT, NSEL])
        w4 = sb("w4", [P, 4, DC, D])
        later = [(w4[:, k], w.rearrange("(c p) d -> p c d", p=P))
                 for k, w in enumerate((L0_ffn_wq, L0_ffn_wk, L0_ffn_wv, L0_ffn_wo))]
        cross_and_router(nc, x1, ctx_1024, mask_1x1xSxS2_fk0, L0_xattn_Wq, L0_xattn_Wk, L0_xattn_Wv,
                         L0_ffn_attention_mask, L0_ffn_position_ids, L0_ffn_router_w, L0_ffn_router_b, out,
                         xsel_t, info_t, picked, mask_rows, later)
        routed_block(nc, xsel_t, info_t, picked, mask_rows, w4, L0_ffn_ln1, L0_ffn_ln2, L0_ffn_w1, L0_ffn_w2, out)


_INS = ["x", "ctx_1024", "mask_1x1xSxS2_fk0", "L0_attn_norm_w", "L0_attn_w_q", "L0_attn_w_k", "L0_attn_w_v",
        "L0_attn_w_out", "L0_attn_scorer_w", "L0_attn_scorer_b", "L0_xattn_Wq", "L0_xattn_Wk", "L0_xattn_Wv",
        "L0_ffn_attention_mask", "L0_ffn_position_ids", "L0_ffn_router_w", "L0_ffn_router_b", "L0_ffn_wq",
        "L0_ffn_wk", "L0_ffn_wv", "L0_ffn_wo", "L0_ffn_w1", "L0_ffn_w2", "L0_ffn_ln1", "L0_ffn_ln2"]


def kernel(**inputs):
    import numpy as _np
    import concourse.bacc as _bacc
    from concourse import mybir as _mybir
    from concourse.bass_utils import run_bass_kernel_spmd as _run

    nc = _bacc.Bacc("TRN2", target_bir_lowering=False, num_devices=1)
    arrays, args = {}, []
    for name in _INS:
        a = _np.ascontiguousarray(inputs[name])
        arrays[f"in_{name}"] = a
        args.append(nc.dram_tensor(f"in_{name}", a.shape, _mybir.dt.from_np(a.dtype), kind="ExternalInput").ap())
    args.append(nc.dram_tensor("out_0", (B, S, D), F32, kind="ExternalOutput").ap())
    pre_ln_decoder_layer(nc, *args)
    r = _run(nc, [arrays], core_ids=[0])
    return r.results[0]["out_0"]
```

```python
from contextlib import ExitStack, contextmanager

import numpy as np
import concourse.bass as bass
from concourse import mybir
from concourse.bass import IndirectOffsetOnAxis

F32 = mybir.dt.float32
F32R = mybir.dt.float32r
BF16 = mybir.dt.bfloat16
I8 = mybir.dt.int8
I32 = mybir.dt.int32
U32 = mybir.dt.uint32
ALU = mybir.AluOpType
ACT = mybir.ActivationFunctionType
AX = mybir.AxisListType

P = 128
B, S, D = 8, 512, 512
TT = S // P
DC = D // P
EPS_LN = 1e-5
EPS_RMS = 1e-6

H, HD = 16, 64
NPAIR = H // 2
TOPK = 128
NEG = -1e30
UNITS = 5
NU = NPAIR * UNITS
VW = HD + 1


class Tally:

    def __init__(self, sem):
        self.sem, self.start, self.round, self.n = sem, 0, 0, 0

    @contextmanager
    def loop(self, i, per, trips):
        self.start, self.round, self.n = self.start + self.n, i * per, 0
        yield
        assert self.n == per, (self.n, per)
        self.start, self.round, self.n = self.start + trips * per, 0, 0

    def mark(self, ins):
        ins.then_inc(self.sem, 1)
        self.n += 1

    def wait(self, eng):
        eng.wait_ge(self.sem, self.round + (self.start + self.n))


def unit_blocks(u):
    if u < 2:
        return [(u, 3, 0, 512)]
    if u < 4:
        return [(u - 2, 0, 0, 128), (u - 2, 2, 128, 384)]
    return [(0, 1, 0, 256), (1, 1, 256, 256)]


def attention_plan():
    plan = [("v", i) for i in range(2 * TT)] + [("q", 0), ("k", 0)]
    for g in range(NU + 7):
        p, u = divmod(g, UNITS)
        if g < NU:
            plan.append(("s", g))
            if p + 1 < NPAIR and u in (0, 2):
                plan.append(("q" if u == 0 else "k", p + 1))
        if 2 <= g < NU + 2:
            plan.append(("t", g - 2))
        if 3 <= g < NU + 3:
            plan.append(("pv", g - 3))
        if g == 3:
            plan.append(("stats", 0))
        if g == 14:
            plan.append(("dot", 0))
        if g == 18:
            plan.append(("score", 0))
        if g in (21, 23, 26, 28):
            plan.append(("rank", (21, 23, 26, 28).index(g)))
        if NU <= g < NU + DC:
            plan.append(("ht", g - NU))
        if g >= 9 and (g - 9) % UNITS == 0 and (g - 9) // UNITS < NPAIR - 1:
            plan.append(("ot", (g - 9) // UNITS))
    plan.append(("ot", NPAIR - 1))
    plan += [("out", t) for t in range(TT)]
    return plan


def bank_index(plan, kinds):
    return {s: i for i, s in enumerate([s for s in plan if s[0] in kinds])}


def self_attention(nc, x, norm_w, w_q, w_k, w_v, w_out, scorer_w, scorer_b, x1):
    plan = attention_plan()
    PROJ, PT = bank_index(plan, ("v", "q", "k", "out")), bank_index(plan, ("t", "score", "ht", "ot"))
    with ExitStack() as ctx:
        def sb(name, shape, dt=F32):
            return ctx.enter_context(nc.sbuf_tensor(name, shape, dt))

        def bank(name):
            return ctx.enter_context(nc.psum_tensor(name, [P, 512], F32))

        def sem(name):
            return ctx.enter_context(nc.semaphore(name))

        w_hi = {n: sb(f"w{n}_hi", [P, DC, H * HD], F32R) for n in "qkv"}
        w_lo = {n: sb(f"w{n}_lo", [P, DC, H * HD], F32R) for n in "qkv"}
        w_o = sb("w_o", [P, NPAIR, D])
        xb = sb("xb", [P, TT, D])
        ht_hi, ht_lo = sb("ht_hi", [P, DC, S], F32R), sb("ht_lo", [P, DC, S], F32R)
        vals = sb("vals", [P, TT, H, VW])
        q_hi, q_lo, k_hi, k_lo = (sb(n, [P, 2, S], F32R) for n in ("q_hi", "q_lo", "k_hi", "k_lo"))
        probs = sb("probs", [P, 2, 512])
        probs_t = sb("probs_t", [P, 2, 512])
        o_rden = sb("o_rden", [P, 2, 2])
        o_norm = sb("o_norm", [P, 2, TT, 2, HD])
        o_t = sb("o_t", [P, NPAIR, S])
        xr = sb("xr", [P, 2, D])
        ident = sb("ident", [P, P])
        ident_b = sb("ident_b", [P, P], BF16)
        causal_b = sb("causal_b", [P, P], BF16)
        before = sb("before", [P, S + P * (TT - 1)], I8)
        row_s = sb("row_s", [P, S])
        junk = sb("junk", [P, S], BF16)
        carrier = sb("carrier", [P, 4])
        nw = sb("nw", [P, DC])
        sw = sb("sw", [P, D])
        sbias = sb("sbias", [P, 1])
        bn = sb("bn", [P, TT, 6])
        mv = sb("mv", [P, TT, 2])
        half, ones, minus, eps_ln, eps_rms, idle = (
            sb(n, [P, TT]) for n in ("half", "ones", "minus", "eps_ln", "eps_rms", "idle"))
        st = sb("st", [P, 5, TT])
        RS, MS, S2, NM, NB = range(5)
        res_next, res_now = sb("res_next", [P, 2, TT]), sb("res_now", [P, 2, TT])
        score = sb("score", [P, TT])
        cnt = sb("cnt", [P, 2, TT])
        twice = sb("twice", [P, TT])
        nmax = sb("nmax", [P, 4, 2])

        s_bank = [bank(f"s_bank{i}") for i in range(2)]
        pt_bank = [bank(f"pt_bank{i}") for i in range(2)]
        pj_bank = [bank(f"pj_bank{i}") for i in range(2)]
        o_bank = [bank(f"o_bank{i}") for i in range(2)]

        w_loaded, split_hi, split_lo = [sem(f"w_loaded{i}") for i in range(2)], sem("split_hi"), sem("split_lo")
        small_in, wo_in, x_in = sem("small_in"), sem("wo_in"), sem("x_in")
        xr_in, x1_out = [sem(f"xr_in{i}") for i in range(2)], [sem(f"x1_out{i}") for i in range(2)]
        const_made, pool_step, dve_step = sem("const_made"), sem("pool_step"), sem("dve_step")
        sw_made, stats_ready, h_ready, score_ready, twice_ready = (
            sem(n) for n in ("sw_made", "stats_ready", "h_ready", "score_ready", "twice_ready"))
        ht_hi_ready, ht_lo_ready = sem("ht_hi_ready"), sem("ht_lo_ready")
        pj_ready, row_copied = sem("pj_ready"), sem("row_copied")
        v_ready, v_sum_ready, qk_hi, qk_lo = sem("v_ready"), sem("v_sum_ready"), sem("qk_hi"), sem("qk_lo")
        s_ready, s_half = sem("s_ready"), sem("s_half")
        max_ready, p_ready = sem("max_ready"), sem("p_ready")
        pt_ready = sem("pt_ready")
        ts_ready, pv_ready, o_copied = sem("ts_ready"), sem("pv_ready"), sem("o_copied")
        ot_ready = sem("ot_ready")
        xr_ready, y_ready = sem("xr_ready"), sem("y_ready")

        NPJ, NPT = len(PROJ), len(PT)
        PT0 = {("ht", c): c for c in range(DC)}
        PT0["score", 0] = DC
        NPT0 = len(PT0)
        W_ORDER = [("v", 0), ("v", 1), ("q", 0), ("k", 0), ("q", 1), ("k", 1)]
        N_CONST = 9
        assert NPJ % 2 == 0

        def pj(b, key):
            return PROJ[key] % 2, b * NPJ + PROJ[key] + 1

        def pt(b, key):
            if b is None:
                return PT0[key] % 2, PT0[key] + 1
            return PT[key] % 2, b * NPT + (PT[key] + 1 + NPT0)

        def taken(eng, b, key):
            kind, i = key
            if kind == "v":
                eng.wait_ge(v_ready, b * (2 * TT) + i + 1)
            elif kind in ("q", "k"):
                eng.wait_ge(qk_lo, b * (2 * NPAIR) + 2 * i + (1 if kind == "q" else 2))
            elif kind == "out":
                eng.wait_ge(y_ready, b * TT + i + 2)
            elif kind == "t":
                eng.wait_ge(ts_ready, b * NU + i + 1)
            elif kind == "ot":
                eng.wait_ge(ot_ready, b * NPAIR + i + 1)
            elif kind == "ht":
                eng.wait_ge(ht_lo_ready, (b + 1) * DC + i + 1)
            elif kind == "score":
                eng.wait_ge(row_copied, b + 2)

        def before_use(order, key):
            keys = list(order)
            return keys[order[key] - 2] if order[key] >= 2 else None

        x_rows = x.rearrange("b (t p) d -> b p t d", p=P)
        x1_rows = x1.rearrange("b (t p) d -> b p t d", p=P)
        w_dram = {n: w.rearrange("(c p) e -> p c e", p=P) for n, w in (("q", w_q), ("k", w_k), ("v", w_v))}

        block = ctx.enter_context(nc.Block())

        @block.sync
        def _(sp):
            sp.dma_start(xb[:, :, :], x_rows[0]).then_inc(x_in, 16)
            with nc.allow_non_contiguous_dma(reason="one column per chunk"):
                sp.dma_start(nw[:, :], norm_w.rearrange("(c p) -> p c", p=P)).then_inc(small_in, 16)
            sp.dma_start(sw[:, :], scorer_w.rearrange("d o -> o d").broadcast_to((P, D))).then_inc(small_in, 16)
            sp.dma_start(row_s[:, :], norm_w.rearrange("(o d) -> o d", o=1).broadcast_to((P, D))).then_inc(small_in, 16)
            sp.dma_start(sbias[:, :], scorer_b.rearrange("(o d) -> o d", o=1).broadcast_to((P, 1))).then_inc(small_in, 16)
            for i, (n, hw) in enumerate(W_ORDER):
                if i >= 2:
                    sp.wait_ge(split_lo, i - 1)
                sp.dma_start(o_t[:, DC * (i % 2):DC * (i % 2) + DC, :],
                             w_dram[n][:, :, 512 * hw:512 * hw + 512]).then_inc(w_loaded[i % 2], 16)
            sp.dma_start(w_o[:, :, :], w_out.rearrange("(c p) d -> p c d", p=P)).then_inc(wo_in, 16)

            def results(b):
                for t in range(TT + 1):
                    if t < TT:
                        sp.wait_ge(x1_out[t % 2], b * (16 * TT // 2) + 16 * (t // 2) + 1)
                        sp.dma_start(xr[:, t % 2, :], x_rows[b][:, t, :]).then_inc(xr_in[t % 2], 16)
                    if t:
                        sp.wait_ge(y_ready, b * TT + t + 1)
                        sp.dma_start(x1_rows[b][:, t - 1, :], xr[:, (t - 1) % 2, :]).then_inc(x1_out[(t - 1) % 2], 16)

            with sp.Fori(0, B - 1) as b:
                sp.wait_ge(ht_lo_ready, b * DC + DC)
                sp.dma_start(xb[:, :, :], x_rows[b + 1]).then_inc(x_in, 16)
                results(b)
            sp.wait_ge(ht_lo_ready, DC * B)
            sp.dma_start(xb[:, :, :], x_rows[0]).then_inc(x_in, 16)
            results(B - 1)
            for half_done in x1_out:
                sp.wait_ge(half_done, 16 * B * TT // 2 + 1)

        @block.gpsimd
        def _(pl):
            done = Tally(pool_step)
            done.mark(nc.gpsimd.memset(ident[:, :], 0.0))
            done.mark(nc.gpsimd.memset(causal_b[:, :], 0.0))
            done.mark(nc.gpsimd.memset(before[:, :], 1.0))
            for tile, value in ((half, -0.5), (ones, 1.0), (minus, -1.0), (eps_ln, EPS_LN), (eps_rms, EPS_RMS)):
                nc.gpsimd.memset(tile[:, :], value).then_inc(const_made, 1)
            done.wait(pl)
            done.mark(nc.gpsimd.affine_select(out=ident[:, :], in_=ident[:, :], compare_op=ALU.not_equal, fill=1.0,
                                              base=0, pattern=[[-1, P]], channel_multiplier=1))
            nc.gpsimd.affine_select(out=causal_b[:, :], in_=causal_b[:, :], compare_op=ALU.is_ge, fill=NEG,
                                    base=0, pattern=[[-1, P]], channel_multiplier=1).then_inc(const_made, 1)
            nc.gpsimd.affine_select(out=before[:, :], in_=before[:, :], compare_op=ALU.is_gt, fill=0.0,
                                    base=P * (TT - 1), pattern=[[-1, S + P * (TT - 1)]],
                                    channel_multiplier=1).then_inc(const_made, 1)
            done.wait(pl)
            nc.gpsimd.tensor_copy(ident_b[:, :], ident[:, :]).then_inc(const_made, 1)
            nc.gpsimd.memset(junk[:, :], 0.0).then_inc(const_made, 1)
            pl.wait_ge(const_made, N_CONST)

            def step(ins):
                done.mark(ins)
                done.wait(pl)

            def carry():
                done.wait(pl)
                done.mark(nc.gpsimd.tensor_tensor(idle[:, :], ones[:, :], ones[:, :], ALU.mult))

            def stats(n):
                pl.wait_ge(stats_ready, n + 1)
                m, v = mv[:, :, 0], mv[:, :, 1]
                step(nc.gpsimd.tensor_tensor(st[:, RS], v, eps_ln[:, :], ALU.add))
                step(nc.gpsimd.tensor_tensor(st[:, RS], st[:, RS], half[:, :], ALU.pow))
                step(nc.gpsimd.tensor_tensor(st[:, MS], st[:, RS], st[:, RS], ALU.mult))
                step(nc.gpsimd.tensor_tensor(st[:, MS], st[:, MS], v, ALU.mult))
                step(nc.gpsimd.tensor_tensor(st[:, MS], st[:, MS], eps_rms[:, :], ALU.add))
                step(nc.gpsimd.tensor_tensor(st[:, S2], st[:, MS], half[:, :], ALU.pow))
                step(nc.gpsimd.tensor_tensor(st[:, S2], st[:, S2], st[:, RS], ALU.mult))
                step(nc.gpsimd.tensor_tensor(st[:, NM], minus[:, :], m, ALU.mult))
                step(nc.gpsimd.tensor_tensor(st[:, NB], st[:, S2], st[:, NM], ALU.mult))
                step(nc.gpsimd.tensor_tensor(res_next[:, 0], st[:, RS], ones[:, :], ALU.add))
                step(nc.gpsimd.tensor_tensor(res_next[:, 1], st[:, RS], st[:, NM], ALU.mult))
                pl.wait_ge(x_in, n * 16 + 16)
                carry()
                for t in range(TT):
                    nc.gpsimd.tensor_scalar(xb[:, t, :], xb[:, t, :], st[:, S2, t:t + 1], st[:, NB, t:t + 1],
                                            ALU.mult, ALU.add).then_inc(h_ready, 1)

            stats(0)
            with pl.Fori(0, B) as b, done.loop(b, 14 + TT, B):
                for r in range(2):
                    step(nc.gpsimd.tensor_tensor(res_now[:, r], res_next[:, r], ones[:, :], ALU.mult))
                for kind, i in plan:
                    if kind == "stats":
                        pl.wait_ge(h_ready, b * TT + TT)
                        stats(b + 1)
                    if kind == "out":
                        pl.wait_ge(xr_in[i % 2], b * (16 * TT // 2) + 16 * (i // 2 + 1))
                        carry()
                        nc.gpsimd.tensor_scalar(xr[:, i % 2, :], xr[:, i % 2, :], res_now[:, 0, i:i + 1],
                                                res_now[:, 1, i:i + 1], ALU.mult, ALU.add).then_inc(xr_ready, 1)
                pl.wait_ge(xr_ready, b * TT + TT)

        @block.scalar
        def _(act):
            def normed(b, n, c):
                slot, ready = pt(b, ("ht", c))
                act.wait_ge(pt_ready, ready)
                nc.scalar.activation(ht_hi[:, c, :], pt_bank[slot][:, :], ACT.Copy,
                                     scale=nw[:, c:c + 1]).then_inc(ht_hi_ready, 1)

            for i, (n, hw) in enumerate(W_ORDER):
                act.wait_ge(w_loaded[i % 2], 16 * (i // 2 + 1))
                nc.scalar.copy(w_hi[n][:, :, 512 * hw:512 * hw + 512],
                               o_t[:, DC * (i % 2):DC * (i % 2) + DC, :]).then_inc(split_hi, 1)
                if i == 1:
                    act.wait_ge(small_in, 64)
                    for c in range(DC):
                        normed(None, 0, c)
            act.wait_ge(split_lo, len(W_ORDER))
            with act.Fori(0, B) as b:
                for kind, i in plan:
                    if kind == "v":
                        t, hw = divmod(i, 2)
                        slot, ready = pj(b, (kind, i))
                        act.wait_ge(pj_ready, ready)
                        if i == 0:
                            act.wait_ge(twice_ready, b + 1)
                        nc.scalar.activation(vals[:, t, 8 * hw:8 * hw + 8, 0:HD],
                                             pj_bank[slot][:, :].rearrange("p (h d) -> p h d", d=HD), ACT.Copy,
                                             scale=twice[:, t:t + 1]).then_inc(v_ready, 1)
                    if kind in ("q", "k"):
                        slot, ready = pj(b, (kind, i))
                        act.wait_ge(pj_ready, ready)
                        hi = q_hi if kind == "q" else k_hi
                        nc.scalar.activation(hi[:, i % 2, :], pj_bank[slot][:, :], ACT.Copy,
                                             scale=HD ** -0.5 if kind == "q" else 1.0).then_inc(qk_hi, 1)
                    if kind == "s":
                        act.wait_ge(max_ready, b * NU + i + 1)
                        if i >= 2:
                            act.wait_ge(pt_ready, pt(b, ("t", i - 2))[1])
                        for n, (_, _, c0, nk) in enumerate(unit_blocks(i % UNITS)):
                            ins = nc.scalar.activation(probs[:, i % 2, c0:c0 + nk], s_bank[i % 2][:, c0:c0 + nk],
                                                       ACT.Exp, bias=nmax[:, i % 4, n:n + 1])
                        ins.then_inc(p_ready, 1)
                    if kind == "ht":
                        normed(b, b + 1, i)
                    if kind == "ot":
                        slot, ready = pt(b, (kind, i))
                        act.wait_ge(pt_ready, ready)
                        nc.scalar.copy(o_t[:, i, :], pt_bank[slot][:, :]).then_inc(ot_ready, 1)

        @block.vector
        def _(dv):
            done = Tally(dve_step)

            def step(ins):
                done.mark(ins)
                done.wait(dv)

            def stats(n):
                dv.wait_ge(x_in, n * 16 + 16)
                for t in range(TT):
                    done.mark(nc.vector.bn_stats(bn[:, t, :], xb[:, t, :]))
                done.wait(dv)
                nc.vector.memset(carrier[:, 0:1], 0.0)
                for t in range(TT):
                    ins = nc.vector.bn_aggr(mv[:, t, :], bn[:, t, :])
                ins.then_inc(stats_ready, 1)

            def dot(n):
                dv.wait_ge(h_ready, n * TT + TT)
                for t in range(TT):
                    step(nc.vector.tensor_tensor_reduce(junk[:, :], xb[:, t, :], sw[:, :], 1.0, 0.0, ALU.mult,
                                                             ALU.add, score[:, t:t + 1]))
                done.wait(dv)
                nc.vector.tensor_scalar(score[:, :], score[:, :], sbias[:, 0:1], None, ALU.add).then_inc(score_ready, 1)

            def score_row(b, n):
                slot, ready = pt(b, ("score", 0))
                dv.wait_ge(pt_ready, ready)
                nc.vector.tensor_copy(row_s[:, :], pt_bank[slot][:, :]).then_inc(row_copied, 1)

            def rank(b, n, t):
                if t == 0:
                    dv.wait_ge(row_copied, n + 1)
                step(nc.vector.tensor_scalar(junk[:, :], row_s[:, :], score[:, t:t + 1], None, ALU.is_gt, ALU.add,
                                                  accum_out=cnt[:, 0, t:t + 1]))
                y0 = P * (TT - 1 - t)
                step(nc.vector.scalar_tensor_tensor(junk[:, :], row_s[:, :], score[:, t:t + 1],
                                                         before[:, y0:y0 + S], ALU.is_equal, ALU.mult,
                                                         accum_out=cnt[:, 1, t:t + 1]))
                if t == TT - 1:
                    done.wait(dv)
                    step(nc.vector.tensor_tensor(cnt[:, 0, :], cnt[:, 0, :], cnt[:, 1, :], ALU.add))
                    if b is not None:
                        dv.wait_ge(v_ready, n * (2 * TT))
                    nc.vector.tensor_scalar(twice[:, :], cnt[:, 0, :], TOPK - 0.5, 1.0, ALU.is_lt,
                                            ALU.add).then_inc(twice_ready, 1)

            def normed(b, n, c):
                slot, _ = pt(b, ("ht", c))
                dv.wait_ge(ht_hi_ready, n * DC + c + 1)
                nc.vector.scalar_tensor_tensor(ht_lo[:, c, :], pt_bank[slot][:, :], nw[:, c:c + 1],
                                               ht_hi[:, c, :].bitcast(F32), ALU.mult,
                                               ALU.subtract).then_inc(ht_lo_ready, 1)

            def split(i):
                n, hw = W_ORDER[i]
                dv.wait_ge(split_hi, i + 1)
                cols = slice(512 * hw, 512 * hw + 512)
                nc.vector.tensor_tensor(w_lo[n][:, :, cols], o_t[:, DC * (i % 2):DC * (i % 2) + DC, :],
                                        w_hi[n][:, :, cols].bitcast(F32), ALU.subtract).then_inc(split_lo, 1)

            dv.wait_ge(const_made, N_CONST)
            for i, at_one in enumerate((y_ready, *x1_out)):
                nc.vector.memset(carrier[:, 1 + i:2 + i], 0.0).then_inc(at_one, 1)
            stats(0)
            dv.wait_ge(small_in, 64)
            nc.vector.tensor_tensor(sw[:, :], sw[:, :], row_s[:, :], ALU.mult).then_inc(sw_made, 1)
            dv.wait_ge(sw_made, 1)
            split(0)
            split(1)
            for c in range(DC):
                normed(None, 0, c)
            dot(0)
            score_row(None, 0)
            for t in range(TT):
                rank(None, 0, t)
            for i in range(2, len(W_ORDER)):
                split(i)
            with dv.Fori(0, B) as b, done.loop(b, 2 * TT + 2 * TT + 1 + NU, B):
                for kind, i in plan:
                    if kind == "v" and i == 0:
                        dv.wait_ge(twice_ready, b + 1)
                        dv.wait_ge(pj_ready, pj(b, (kind, 0))[1])
                        nc.vector.tensor_copy(vals[:, :, :, HD], twice[:, :].unsqueeze(2).broadcast_to((P, TT, H))
                                              ).then_inc(v_sum_ready, 1)
                    if kind in ("q", "k"):
                        slot, _ = pj(b, (kind, i))
                        dv.wait_ge(qk_hi, b * (2 * NPAIR) + 2 * i + (1 if kind == "q" else 2))
                        if kind == "q":
                            ins = nc.vector.scalar_tensor_tensor(q_lo[:, i % 2, :], pj_bank[slot][:, :], HD ** -0.5,
                                                                 q_hi[:, i % 2, :].bitcast(F32), ALU.mult,
                                                                 ALU.subtract)
                        else:
                            ins = nc.vector.tensor_tensor(k_lo[:, i % 2, :], pj_bank[slot][:, :],
                                                          k_hi[:, i % 2, :].bitcast(F32), ALU.subtract)
                        ins.then_inc(qk_lo, 1)
                    if kind == "s":
                        dv.wait_ge(s_ready, b * NU + i + 1)
                        blocks = unit_blocks(i % UNITS)
                        if i % UNITS == UNITS - 1:
                            ins = nc.vector.tensor_reduce(nmax[:, i % 4, :],
                                                          s_bank[i % 2][:, :].rearrange("p (h k) -> p h k", h=2),
                                                          AX.X, ALU.max, negate=True)
                        else:
                            for n, (_, _, c0, nk) in enumerate(blocks):
                                ins = nc.vector.tensor_reduce(nmax[:, i % 4, n:n + 1], s_bank[i % 2][:, c0:c0 + nk],
                                                              AX.X, ALU.max, negate=True)
                        ins.then_inc(max_ready, 1)
                    if kind == "t":
                        slot, ready = pt(b, (kind, i))
                        dv.wait_ge(pt_ready, ready)
                        if i >= 2:
                            dv.wait_ge(pv_ready, b * NU + i - 1)
                        nc.vector.tensor_copy(probs_t[:, i % 2, :], pt_bank[slot][:, :]).then_inc(ts_ready, 1)
                    if kind == "pv":
                        p, u = divmod(i, UNITS)
                        dv.wait_ge(pv_ready, b * NU + i + 1)
                        if u == 0 and p >= 2:
                            dv.wait_ge(pt_ready, pt(b, ("ot", p - 2))[1])
                        n = len(unit_blocks(u))
                        src = o_bank[i % 2][:, 0:n * VW].rearrange("p (n v) -> p n v", n=n)
                        if u < 2:
                            dst = o_norm[:, p % 2, 3:4, u, :]
                        elif u < 4:
                            dst = o_norm[:, p % 2, 0:3:2, u - 2, :]
                        else:
                            dst = o_norm[:, p % 2, 1, :, :]
                        step(nc.vector.reciprocal(o_rden[:, i % 2, 0:n], src[:, :, HD]))
                        nc.vector.tensor_tensor(dst, src[:, :, 0:HD], o_rden[:, i % 2, 0:n].unsqueeze(2).broadcast_to((P, n, HD)),
                                                ALU.mult).then_inc(o_copied, 1)
                    if kind == "stats":
                        stats(b + 1)
                    if kind == "dot":
                        dot(b + 1)
                    if kind == "score":
                        score_row(b, b + 1)
                    if kind == "rank":
                        rank(b, b + 1, i)
                    if kind == "ht":
                        normed(b, b + 1, i)
                    if kind == "out":
                        slot, ready = pj(b, (kind, i))
                        dv.wait_ge(pj_ready, ready)
                        dv.wait_ge(xr_ready, b * TT + i + 1)
                        nc.vector.tensor_tensor(xr[:, i % 2, :], pj_bank[slot][:, :], xr[:, i % 2, :],
                                                ALU.add).then_inc(y_ready, 1)

        @block.tensor
        def _(pe):
            def product(out, lhs_hi, lhs_lo, rhs_hi, rhs_lo, start, stop):
                nc.tensor.matmul(out, lhs_hi, rhs_hi, start=start, stop=False)
                nc.tensor.matmul(out, lhs_lo, rhs_hi, start=False, stop=False)
                return nc.tensor.matmul(out, lhs_hi, rhs_lo, start=False, stop=stop)

            def pt_empty(b, key):
                if b is None:
                    if PT0[key] >= 2:
                        pe.wait_ge(ht_lo_ready, PT0[key] - 1)
                elif before_use(PT, key):
                    taken(pe, b, before_use(PT, key))
                else:
                    pe.wait_ge(ht_lo_ready, b * DC + DC)
                    pe.wait_ge(row_copied, b + 1)

            def pj_empty(b, key):
                if before_use(PROJ, key):
                    taken(pe, b, before_use(PROJ, key))
                else:
                    pe.wait_ge(y_ready, b * TT + 1)

            def transposed(b, n, c):
                slot, _ = pt(b, ("ht", c))
                if c == 0:
                    pe.wait_ge(h_ready, n * TT + TT)
                pt_empty(b, ("ht", c))
                for t in range(TT):
                    ins = nc.tensor.transpose(pt_bank[slot][:, P * t:P * t + P], xb[:, t, P * c:P * c + P], ident[:, :])
                ins.then_inc(pt_ready, 1)

            def score_rows(b, n):
                slot, _ = pt(b, ("score", 0))
                pe.wait_ge(score_ready, n + 1)
                pt_empty(b, ("score", 0))
                for t in range(TT):
                    ins = nc.tensor.transpose(pt_bank[slot][:, P * t:P * t + P],
                                              score[:, t:t + 1].broadcast_to((P, P)), ident[:, :])
                ins.then_inc(pt_ready, 1)

            pe.wait_ge(const_made, N_CONST)
            for c in range(DC):
                transposed(None, 0, c)
            score_rows(None, 0)
            with pe.Fori(0, B) as b:
                for kind, i in plan:
                    if kind == "v":
                        t, hw = divmod(i, 2)
                        slot, _ = pj(b, (kind, i))
                        if i == 0:
                            pe.wait_ge(ht_lo_ready, b * DC + DC)
                        if i < 2:
                            pe.wait_ge(split_lo, 1 + i)
                        pj_empty(b, (kind, i))
                        for c in range(DC):
                            ins = product(pj_bank[slot][:, :], ht_hi[:, c, P * t:P * t + P], ht_lo[:, c, P * t:P * t + P],
                                          w_hi["v"][:, c, 512 * hw:512 * hw + 512],
                                          w_lo["v"][:, c, 512 * hw:512 * hw + 512], c == 0, c == DC - 1)
                        ins.then_inc(pj_ready, 1)
                    if kind in ("q", "k"):
                        slot, _ = pj(b, (kind, i))
                        pe.wait_ge(split_lo, 4 if i < NPAIR // 2 else 6)
                        pj_empty(b, (kind, i))
                        for c in range(DC):
                            ins = product(pj_bank[slot][:, :], w_hi[kind][:, c, P * i:P * i + P],
                                          w_lo[kind][:, c, P * i:P * i + P], ht_hi[:, c, :], ht_lo[:, c, :],
                                          c == 0, c == DC - 1)
                        ins.then_inc(pj_ready, 1)
                    if kind == "s":
                        p, u = divmod(i, UNITS)
                        slot = i % 2
                        if u == 0:
                            pe.wait_ge(qk_lo, b * (2 * NPAIR) + 2 * p + 2)
                        if i >= 2:
                            pe.wait_ge(p_ready, b * NU + i - 1)
                        for h, t, c0, nk in unit_blocks(u):
                            if u == UNITS - 1 and h == 1:
                                ins.then_inc(s_half, 1)
                                pe.wait_ge(s_half, b * NPAIR + p + 1)
                            rows = slice(HD * h, HD * h + HD)
                            product(s_bank[slot][:, c0:c0 + nk],
                                    q_hi[rows, p % 2, P * t:P * t + P], q_lo[rows, p % 2, P * t:P * t + P],
                                    k_hi[rows, p % 2, 0:nk], k_lo[rows, p % 2, 0:nk], True, False)
                            ins = nc.tensor.matmul(s_bank[slot][:, c0 + nk - P:c0 + nk], ident_b[:, :], causal_b[:, :],
                                                   start=False, stop=True)
                        ins.then_inc(s_ready, 1)
                    if kind == "t":
                        slot, _ = pt(b, (kind, i))
                        pe.wait_ge(p_ready, b * NU + i + 1)
                        pt_empty(b, (kind, i))
                        for j in range(4):
                            ins = nc.tensor.transpose(pt_bank[slot][:, P * j:P * j + P], probs[:, i % 2, P * j:P * j + P],
                                                      ident[:, :])
                        ins.then_inc(pt_ready, 1)
                    if kind == "pv":
                        p, u = divmod(i, UNITS)
                        slot = i % 2
                        if i == 0:
                            pe.wait_ge(v_ready, b * (2 * TT) + 2 * TT)
                            pe.wait_ge(v_sum_ready, b + 1)
                        pe.wait_ge(ts_ready, b * NU + i + 1)
                        if i >= 2:
                            pe.wait_ge(o_copied, b * NU + i - 1)
                        for n, (h, t, c0, nk) in enumerate(unit_blocks(u)):
                            o0 = n * VW
                            for kt in range(nk // P):
                                ins = nc.tensor.matmul(o_bank[slot][:, o0:o0 + VW],
                                                       probs_t[:, i % 2, c0 + P * kt:c0 + P * kt + P],
                                                       vals[:, kt, 2 * p + h, :], start=(kt == 0), stop=(kt == nk // P - 1))
                        ins.then_inc(pv_ready, 1)
                    if kind == "ot":
                        slot, _ = pt(b, (kind, i))
                        pe.wait_ge(o_copied, b * NU + UNITS * (i + 1))
                        pt_empty(b, (kind, i))
                        for t in range(TT):
                            ins = nc.tensor.transpose(pt_bank[slot][:, P * t:P * t + P], o_norm[:, i % 2, t, :, :].rearrange("p h d -> p (h d)"), ident[:, :])
                        ins.then_inc(pt_ready, 1)
                    if kind == "score":
                        score_rows(b, b + 1)
                    if kind == "ht":
                        transposed(b, b + 1, i)
                    if kind == "out":
                        slot, _ = pj(b, (kind, i))
                        if i == 0:
                            pe.wait_ge(ot_ready, b * NPAIR + NPAIR)
                            pe.wait_ge(wo_in, 16)
                        pj_empty(b, (kind, i))
                        for c in range(NPAIR):
                            ins = nc.tensor.matmul(pj_bank[slot][:, :], o_t[:, c, P * i:P * i + P], w_o[:, c, :],
                                                   start=(c == 0), stop=(c == NPAIR - 1))
                        ins.then_inc(pj_ready, 1)


SK = 77
XH, XD = 16, 32
CH = P // XD
VX = XD + 1
FILL = -1e20
KEEP = 64
NSEL = B * KEEP


SLOTS = 2 * TT


class Batch:

    def __init__(self, j, k):
        self.j, self.k = j, k

    def ahead(self, off):
        return Batch(self.j, self.k + off)

    def count(self, per, more):
        return (2 * self.j + self.k) * per + more if isinstance(self.j, int) else self.j * (2 * per) + (self.k * per + more)

    @property
    def index(self):
        return self.count(1, 0)

    @property
    def par(self):
        return self.k % 2

    @property
    def had(self):
        return self.j + self.k // 2


def cross_plan():
    at = [("e", s, s) for s in range(SLOTS)]
    at += [("turn", t, 2 * t - 1) for t in range(TT)]
    for kind, lag in (("max", 1), ("t", 2), ("pv", 3)):
        at += [(kind, s, s + lag) for s in range(SLOTS)]
    at += [("xl", t, 2 * t - 2) for t in range(TT)]
    at += [("stats", 0, -3)] + [("ctx", i, i - 5) for i in range(4)]
    at += [("norm", t, 2 * t + 5) for t in range(TT)] + [("xl2", 0, 12), ("xs_take", 0, 19), ("a1_take", 0, 20)]
    at += [("dot", 0, 12), ("row", 0, 12)] + [("rank", t, 13 + t) for t in range(TT)] + [("pick", 0, 16)]
    at += [("xs", c, 17 + c // 2) for c in range(DC)] + [("base", t, 17 + t // 2) for t in range(TT)]
    at += [("a1", c, 18 + (c + 1) // 3) for c in range(TT)]
    order = ("pv", "t", "max", "xs_take", "a1_take", "turn", "xl", "ctx", "stats", "norm", "xl2", "dot", "row", "rank",
             "pick", "e", "base", "xs", "a1")
    at.sort(key=lambda a: (a[2] % SLOTS, order.index(a[0]), a[1]))
    return [(kind, i, -(slot // SLOTS)) for kind, i, slot in at]


def cross_and_router(nc, x1, ctx_in, mask, wq, wk, wv, amask, pos, router_w, router_b, base,
                     xsel_t, info_t, picked, mask_rows, later):
    with ExitStack() as ctx:
        def sb(name, shape, dt=F32):
            return ctx.enter_context(nc.sbuf_tensor(name, shape, dt))

        def banks(name, n=1):
            return ctx.enter_context(nc.psum_tensor(name, [P, n, 512] if n > 1 else [P, 512], F32))

        def sem(name):
            return ctx.enter_context(nc.semaphore(name))

        xt = sb("xt", [P, 2, TT, D])
        x2 = sb("x2", [P, 2, TT, D])
        xl = sb("xl", [P, 2, D])
        xl_t = sb("xl_t", [P, 2, D])
        e = sb("e", [P, 4, 2 * CH, SK])
        fill = sb("fill", [P, 2, 2 * CH, SK])
        mk = sb("mk", [P, TT, SK])
        e_max = sb("e_max", [P, 2, 2 * CH])
        p_t = sb("p_t", [SK, 2, 2, 512])
        att_den = sb("att_den", [P, 2, 2 * CH])
        att = sb("att", [P, 2, 2 * CH, XD])
        cx = sb("cx", [SK, D])
        cx_t = sb("cx_t", [P, DC, SK])
        key_t = sb("key_t", [P, DC, SK])
        qk_bd = sb("qk_bd", [P, 2, DC, CH, SK])
        vx = sb("vx", [SK, 2, XH, VX])
        w_bd = sb("w_bd", [P, 3, P])
        wq_bt = sb("wq_bt", [P, P])
        ident = sb("x_ident", [P, P])
        rw = sb("rw", [P, D])
        rb = sb("rb", [P, 1])
        am = sb("am", [P, TT, S])
        pos_i = sb("pos_i", [P, TT], I32)
        xl2 = sb("xl2", [P, TT, D])
        row_s = sb("x_row_s", [P, S])
        junk = sb("x_junk", [P, S], BF16)
        before = sb("x_before", [P, S + P * (TT - 1)], I8)
        slots = sb("slots", [P, KEEP])
        bn, mv = sb("x_bn", [P, 2, TT, 6]), sb("x_mv", [P, 2, TT, 2])
        half, minus, eps_ln, ones, idle = (sb(n, [P, TT]) for n in ("x_half", "x_minus", "x_eps", "x_ones", "x_idle"))
        scales = sb("scales", [P, 2, 3, TT])
        RS, NM, NB = range(3)
        info = sb("info", [P, TT, 3])
        cnt = sb("x_cnt", [P, 3, TT])
        stay = sb("stay", [P, TT])
        sel = sb("sel", [P, TT, KEEP])

        e_bank, pt_bank = banks("e_bank", 2), [banks(f"x_pt_bank{i}") for i in range(2)]
        o_bank, t_bank, r_bank = banks("x_o_bank"), banks("t_bank"), [banks(f"r_bank{i}") for i in range(2)]

        x_in = [[sem(f"x_in{p}{t}") for t in range(TT)] for p in range(2)]
        base_out = [[sem(f"base_out{p}{t}") for t in range(TT)] for p in range(2)]
        cx_in, am_in, pos_in, const_in, later_in = (sem(n) for n in ("cx_in", "am_in", "pos_in", "x_const_in", "later_in"))
        idle_v = sb("idle_v", [P, 2])
        made, pool_step, dve_step = sem("x_made"), sem("x_pool_step"), sem("x_dve_step")
        wq_turned, wq_copied = sem("wq_turned"), sem("wq_copied")
        stats_ready, scales_ready, scales2_ready, xl_ready, turned, t_copied = (
            sem(n) for n in ("x_stats_ready", "scales_ready", "scales2_ready", "xl_ready", "turned", "t_copied"))
        e_ready, masked, fill_ready, filled, max_ready, shifted, p_ready = (
            sem(n) for n in ("e_ready", "masked", "fill_ready", "filled", "x_max_ready", "shifted", "x_p_ready"))
        pt_ready, pt_copied, pv_ready, att_ready, x2_ready = (
            sem(n) for n in ("x_pt_ready", "pt_copied", "x_pv_ready", "att_ready", "x2_ready"))
        stats2_ready, xl2_ready, info_ready, r_ready, row_copied, sel_ready, xs_copied, a1_copied, base_ready = (
            sem(n) for n in ("stats2_ready", "xl2_ready", "info_ready", "r_ready", "x_row_copied", "sel_ready",
                             "xs_copied", "a1_copied", "base_ready"))

        HALVES, RB = 2 * TT, 3
        x1_rows = x1.rearrange("b (t p) d -> b p t d", p=P)
        base_rows = base.rearrange("b (t p) d -> b p t d", p=P)
        N_MADE, CONST_IN, ROUNDS = 11, 16 * (3 + 3 * CH), (B - 2) // 2
        assert B == 2 * ROUNDS + 2 and amask.shape[0] <= 4

        def cols(i):
            return slice(256 * (i % 2), 256 * (i % 2) + 256)

        plan = cross_plan()
        in_t_bank = [p for p in plan if p[0] in ("ctx", "turn")]
        early = [p for p in in_t_bank if p[2] == 1]

        def t_count(kind, i, n):
            off = next(p[2] for p in plan if p[:2] == (kind, i))
            n = n.ahead(-off)
            if isinstance(n.j, int) and n.index < 0:
                return early.index((kind, i, off)) + 1
            return n.count(len(in_t_bank), len(early) + in_t_bank.index((kind, i, off)) + 1)

        def run(step, eng, tally=None, per=0):
            def period(n, least=-2, most=1):
                for kind, i, off in plan:
                    if least <= off <= most:
                        step(kind, i, n.ahead(off))

            period(Batch(0, -1), least=1)
            period(Batch(0, 0), least=0)
            period(Batch(0, 1), least=-1)
            with eng.Fori(0, ROUNDS) as j:
                if tally:
                    with tally.loop(j, per, ROUNDS):
                        period(Batch(j, 2))
                        period(Batch(j, 3))
                else:
                    period(Batch(j, 2))
                    period(Batch(j, 3))
            period(Batch(0, B), most=-1)
            period(Batch(0, B + 1), most=-2)

        def wait(eng, sem_, value):
            if not isinstance(value, int) or value > 0:
                eng.wait_ge(sem_, value)

        block = ctx.enter_context(nc.Block())

        @block.sync
        def _(sp):
            def load_x(n, source):
                for t in range(TT):
                    wait(sp, x2_ready, n.count(HALVES, 2 * t + 2 - 2 * HALVES))
                    sp.dma_start(xt[:, n.par, t, :], x1_rows[source][:, t, :]).then_inc(x_in[n.par][t], 16)

            def load_context(n, source):
                if not isinstance(n.j, int) or n.index > 0:
                    sp.wait_ge(turned, t_count("ctx", 0, n.ahead(-1)))
                sp.dma_start(cx[:, :], ctx_in[source]).then_inc(cx_in, 16)

            def store(n):
                for t in range(TT):
                    sp.wait_ge(base_ready, n.count(TT, t + 1))
                    sp.dma_start(base_rows[n.index][:, t, :], x2[:, n.par, t, :]).then_inc(base_out[n.par][t], 16)

            def load_router(n, m):
                wait(sp, info_ready, n.count(1, 0))
                with nc.allow_non_contiguous_dma(reason="512 numbers"):
                    sp.dma_start(pos_i[:, :], pos[m, 0:S].rearrange("(t p) -> p t", p=P)).then_inc(pos_in, 16)
                wait(sp, r_ready, n.count(RB, 0))
                sp.dma_start(am[:, :, :], amask[m, 0, 0:S, 0:S].rearrange("(t p) k -> p t k", p=P)).then_inc(am_in, 16)

            def period(n, m, source):
                store(n.ahead(-2))
                load_x(n.ahead(1), source)
                load_context(n.ahead(1), source)
                load_router(n.ahead(-1), m)

            last_m = amask.shape[0] - 1
            load_x(Batch(0, 0), 0)
            load_context(Batch(0, 0), 0)
            sp.dma_start(mk[:, :, :], mask[0, 0].rearrange("(t p) k -> p t k", p=P)).then_inc(const_in, 16)
            sp.dma_start(rw[:, :], router_w.rearrange("d o -> o d").broadcast_to((P, D))).then_inc(const_in, 16)
            sp.dma_start(rb[:, :], router_b.rearrange("(o d) -> o d", o=1).broadcast_to((P, 1))).then_inc(const_in, 16)
            sp.wait_ge(made, N_MADE)
            for k, w in enumerate((wq, wk, wv)):
                for h in range(CH):
                    rows = slice(XD * h, XD * h + XD)
                    sp.dma_start(w_bd[rows, k, rows], w[:, :]).then_inc(const_in, 16)
            load_x(Batch(0, 1), 1)
            load_context(Batch(0, 1), 1)
            load_router(Batch(0, 0), 0)
            load_x(Batch(0, 2), 2)
            load_context(Batch(0, 2), 2)
            for k in (2, 3):
                period(Batch(0, k), min(k - 1, last_m), k + 1)
            for dst, src in later:
                sp.dma_start(dst, src).then_inc(later_in, 16)
            with sp.Fori(1, ROUNDS - 1) as j:
                period(Batch(j, 2), last_m, Batch(j, 3).index)
                period(Batch(j, 3), last_m, Batch(j, 4).index)
            period(Batch(0, B - 2), last_m, B - 1)
            period(Batch(0, B - 1), last_m, 0)
            store(Batch(0, B - 2))
            load_router(Batch(0, B - 1), last_m)
            store(Batch(0, B - 1))
            for par in range(2):
                for t in range(TT):
                    sp.wait_ge(base_out[par][t], 16 * B // 2)
            sp.wait_ge(later_in, 16 * len(later))

        @block.gpsimd
        def _(pl):
            done = Tally(pool_step)
            done.mark(nc.gpsimd.memset(ident[:, :], 0.0))
            done.mark(nc.gpsimd.memset(before[:, :], 1.0))
            for tile, value in ((half, -0.5), (minus, -1.0), (eps_ln, EPS_LN), (ones, 1.0)):
                nc.gpsimd.memset(tile[:, :], value).then_inc(made, 1)
            nc.gpsimd.memset(w_bd[:, :, :], 0.0).then_inc(made, 1)
            nc.gpsimd.memset(qk_bd[:, :, :, :, :], 0.0).then_inc(made, 1)
            nc.gpsimd.memset(vx[:, :, :, XD:VX], 1.0).then_inc(made, 1)
            nc.gpsimd.iota(slots[:, :], [[1, KEEP]], base=0, channel_multiplier=0,
                           allow_small_or_imprecise_dtypes=True).then_inc(made, 1)
            nc.gpsimd.iota(info[:, :, 2:3], [[P, TT]], base=0, channel_multiplier=1,
                           allow_small_or_imprecise_dtypes=True).then_inc(made, 1)
            done.wait(pl)
            nc.gpsimd.affine_select(out=ident[:, :], in_=ident[:, :], compare_op=ALU.not_equal, fill=1.0, base=0,
                                    pattern=[[-1, P]], channel_multiplier=1).then_inc(made, 1)
            nc.gpsimd.affine_select(out=before[:, :], in_=before[:, :], compare_op=ALU.is_gt, fill=0.0,
                                    base=P * (TT - 1), pattern=[[-1, S + P * (TT - 1)]],
                                    channel_multiplier=1).then_inc(made, 1)
            pl.wait_ge(made, N_MADE)

            def step(ins):
                done.mark(ins)
                done.wait(pl)

            def scale(r, ready):
                step(nc.gpsimd.tensor_tensor(scales[:, r, RS], mv[:, r, :, 1], eps_ln[:, :], ALU.add))
                step(nc.gpsimd.tensor_tensor(scales[:, r, RS], scales[:, r, RS], half[:, :], ALU.pow))
                step(nc.gpsimd.tensor_tensor(scales[:, r, NM], minus[:, :], mv[:, r, :, 0], ALU.mult))
                nc.gpsimd.tensor_tensor(scales[:, r, NB], scales[:, r, NM], scales[:, r, RS], ALU.mult).then_inc(ready, 1)

            def work(kind, i, n):
                if kind == "stats":
                    pl.wait_ge(stats_ready, n.count(1, 1))
                    scale(0, scales_ready)
                if kind == "e":
                    pl.wait_ge(fill_ready, n.count(HALVES, i + 1))
                    nc.gpsimd.tensor_tensor(e[:, i % 4], e[:, i % 4], fill[:, i % 2], ALU.add).then_inc(filled, 1)
                if kind == "max":
                    pl.wait_ge(max_ready, n.count(HALVES, i + 1))
                    nc.gpsimd.tensor_tensor(e[:, i % 4], e[:, i % 4],
                                            e_max[:, i % 2].unsqueeze(2).broadcast_to((P, 2 * CH, SK)),
                                            ALU.add).then_inc(shifted, 1)
                if kind == "pv":
                    pl.wait_ge(att_ready, n.count(HALVES, i + 1))
                    if not isinstance(n.had, int) or n.had > 0:
                        pl.wait_ge(base_out[n.par][i // 2], n.had * 16)
                    nc.gpsimd.tensor_tensor(x2[:, n.par, i // 2, cols(i)], xt[:, n.par, i // 2, cols(i)],
                                            att[:, i % 2].rearrange("p h d -> p (h d)"), ALU.add).then_inc(x2_ready, 1)
                if kind == "norm" and i == TT - 1:
                    pl.wait_ge(stats2_ready, n.count(1, 1))
                    scale(1, scales2_ready)

            run(work, pl, done, 2 * 6)

        @block.scalar
        def _(act):
            act.wait_ge(wq_turned, 1)
            nc.scalar.copy(wq_bt[:, :], t_bank[:, 0:P]).then_inc(wq_copied, 1)
            act.wait_ge(made, N_MADE)

            def work(kind, i, n):
                if kind == "ctx":
                    act.wait_ge(turned, t_count(kind, i, n))
                    chunks = t_bank[:, 0:DC * SK].rearrange("p (c k) -> p c k", c=DC)
                    if i == 0:
                        ins = nc.scalar.copy(cx_t[:, :, :], chunks)
                    elif i == 1:
                        ins = nc.scalar.copy(key_t[:, :, :], chunks)
                    elif i == 2:
                        for h in range(CH):
                            rows = slice(XD * h, XD * h + XD)
                            ins = nc.scalar.copy(qk_bd[rows, n.par, :, h, :], chunks[rows])
                    else:
                        ins = nc.scalar.copy(vx[:, n.par, :, 0:XD], t_bank[0:SK, :].rearrange("p (h d) -> p h d", d=XD))
                    ins.then_inc(t_copied, 1)
                if kind == "xl":
                    act.wait_ge(scales_ready, n.count(1, 1))
                    if i >= 2:
                        act.wait_ge(turned, t_count("turn", i - 2, n))
                    elif not isinstance(n.j, int) or n.index > 0:
                        act.wait_ge(turned, t_count("turn", i + 2, n.ahead(-1)))
                    nc.scalar.activation(xl[:, i % 2, :], xt[:, n.par, i, :], ACT.Identity, bias=scales[:, 0, NB, i:i + 1],
                                         scale=scales[:, 0, RS, i:i + 1]).then_inc(xl_ready, 1)
                if kind == "turn":
                    act.wait_ge(turned, t_count(kind, i, n))
                    wait(act, e_ready, n.count(HALVES, 2 * i - 2))
                    nc.scalar.copy(xl_t[:, i % 2, :], t_bank[:, :]).then_inc(t_copied, 1)
                if kind == "max":
                    act.wait_ge(shifted, n.count(HALVES, i + 1))
                    nc.scalar.activation(e[:, i % 4], e[:, i % 4], ACT.Exp).then_inc(p_ready, 1)
                if kind == "t":
                    act.wait_ge(pt_ready, n.count(HALVES, i + 1))
                    wait(act, pv_ready, n.count(HALVES, i - 1))
                    for h in range(2):
                        ins = nc.scalar.copy(p_t[:, i % 2, h, :], pt_bank[h][0:SK, :])
                    ins.then_inc(pt_copied, 1)
                if kind == "xl2":
                    act.wait_ge(scales2_ready, n.count(1, 1))
                    wait(act, base_ready, n.count(TT, 0))
                    wait(act, r_ready, n.count(RB, -1))
                    for t in range(TT):
                        nc.scalar.activation(xl2[:, t, :], x2[:, n.par, t, :], ACT.Identity,
                                             bias=scales[:, 1, NB, t:t + 1], scale=scales[:, 1, RS, t:t + 1]
                                             ).then_inc(xl2_ready, 1)

            run(work, act)

        @block.vector
        def _(dv):
            done = Tally(dve_step)

            def step(ins):
                done.mark(ins)
                done.wait(dv)

            def aggregate(r, ready):
                done.wait(dv)
                nc.vector.memset(idle_v[:, r:r + 1], 0.0)
                for t in range(TT):
                    ins = nc.vector.bn_aggr(mv[:, r, t, :], bn[:, r, t, :])
                ins.then_inc(ready, 1)

            def work(kind, i, n):
                if kind == "stats":
                    wait(dv, xl_ready, n.count(TT, 0))
                    for t in range(TT):
                        dv.wait_ge(x_in[n.par][t], n.had * 16 + 16)
                        done.mark(nc.vector.bn_stats(bn[:, 0, t, :], xt[:, n.par, t, :]))
                    aggregate(0, stats_ready)
                if kind == "e":
                    four = (P, 2, CH, SK)
                    dv.wait_ge(e_ready, n.count(HALVES, i + 1))
                    wait(dv, pt_ready, n.count(HALVES, i - 3))
                    nc.vector.tensor_tensor(e[:, i % 4].rearrange("p (c h) k -> p c h k", c=2),
                                            e_bank[:, :, 0:CH * SK].rearrange("p c (h k) -> p c h k", h=CH),
                                            mk[:, i // 2, :].unsqueeze(1).unsqueeze(1).broadcast_to(four),
                                            ALU.mult).then_inc(masked, 1)
                    dv.wait_ge(masked, n.count(HALVES, i + 1))
                    wait(dv, filled, n.count(HALVES, i - 1))
                    nc.vector.tensor_scalar(fill[:, i % 2], e[:, i % 4], 0.0, FILL, ALU.is_equal,
                                            ALU.mult).then_inc(fill_ready, 1)
                if kind == "max":
                    dv.wait_ge(filled, n.count(HALVES, i + 1))
                    wait(dv, shifted, n.count(HALVES, i - 1))
                    nc.vector.tensor_reduce(e_max[:, i % 2], e[:, i % 4], AX.X, ALU.max,
                                            negate=True).then_inc(max_ready, 1)
                if kind == "pv":
                    dv.wait_ge(pv_ready, n.count(HALVES, i + 1))
                    o = o_bank[:, 0:2 * CH * VX].rearrange("p (h v) -> p h v", v=VX)
                    step(nc.vector.reciprocal(att_den[:, i % 2], o[:, :, XD]))
                    wait(dv, x2_ready, n.count(HALVES, i - 1))
                    nc.vector.tensor_tensor(att[:, i % 2], o[:, :, 0:XD],
                                            att_den[:, i % 2].unsqueeze(2).broadcast_to((P, 2 * CH, XD)),
                                            ALU.mult).then_inc(att_ready, 1)

                batch = bass.ts(n.index, KEEP)
                if kind == "norm":
                    dv.wait_ge(x2_ready, n.count(HALVES, 2 * i + 2))
                    done.mark(nc.vector.bn_stats(bn[:, 1, i, :], x2[:, n.par, i, :]))
                    if i == TT - 1:
                        aggregate(1, stats2_ready)
                if kind == "dot":
                    dv.wait_ge(xl2_ready, n.count(TT, TT))
                    for t in range(TT):
                        step(nc.vector.tensor_tensor_reduce(junk[:, :], xl2[:, t, :], rw[:, :], 1.0, 0.0, ALU.mult,
                                                            ALU.add, info[:, t, 0:1]))
                    step(nc.vector.tensor_scalar(info[:, :, 0], info[:, :, 0], rb[:, 0:1], None, ALU.add))
                    dv.wait_ge(pos_in, n.count(16, 16))
                    nc.vector.tensor_copy(info[:, :, 1], pos_i[:, :]).then_inc(info_ready, 1)
                if kind == "row":
                    dv.wait_ge(r_ready, n.count(RB, 1))
                    nc.vector.tensor_copy(row_s[:, :], r_bank[0][:, :]).then_inc(row_copied, 1)
                    dv.wait_ge(row_copied, n.count(1, 1))
                if kind == "rank":
                    w = info[:, i, 0:1]
                    y0 = P * (TT - 1 - i)
                    step(nc.vector.tensor_scalar(junk[:, :], row_s[:, :], w, None, ALU.is_gt, ALU.add,
                                                 accum_out=cnt[:, 0, i:i + 1]))
                    step(nc.vector.scalar_tensor_tensor(junk[:, :], row_s[:, :], w, before[:, y0:y0 + S],
                                                        ALU.is_equal, ALU.mult, accum_out=cnt[:, 1, i:i + 1]))
                    step(nc.vector.tensor_scalar(junk[:, :], row_s[:, :], w, None, ALU.is_ge, ALU.add,
                                                 accum_out=cnt[:, 2, i:i + 1]))
                if kind == "pick":
                    step(nc.vector.tensor_tensor(cnt[:, 0, :], cnt[:, 0, :], cnt[:, 1, :], ALU.add))
                    step(nc.vector.tensor_scalar(stay[:, :], cnt[:, 2, :], KEEP - 0.5, None, ALU.is_gt))
                    for t in range(TT):
                        ins = nc.vector.tensor_scalar(sel[:, t, :], slots[:, :], cnt[:, 0, t:t + 1], None, ALU.is_equal)
                    ins.then_inc(sel_ready, 1)
                    dv.wait_ge(sel_ready, n.count(1, 1))
                    nc.vector.tensor_scalar(picked[:, :, batch], sel[:, :, :], 1.0, None, ALU.mult)
                if kind == "xs_take":
                    dv.wait_ge(r_ready, n.count(RB, 2))
                    nc.vector.tensor_scalar(xsel_t[:, :, batch],
                                            r_bank[1][:, 0:DC * KEEP].rearrange("p (c s) -> p c s", c=DC), 1.0, None,
                                            ALU.mult)
                    nc.vector.tensor_scalar(info_t[0:3, batch], r_bank[1][0:3, DC * KEEP:DC * KEEP + KEEP], 1.0, None,
                                            ALU.mult).then_inc(xs_copied, 1)
                if kind == "a1_take":
                    dv.wait_ge(r_ready, n.count(RB, 3))
                    nc.vector.tensor_scalar(mask_rows[:, :, batch],
                                            r_bank[0][:, 0:TT * KEEP].rearrange("p (c s) -> p c s", c=TT), 1.0, None,
                                            ALU.mult).then_inc(a1_copied, 1)
                if kind == "base":
                    rows = x2[:, n.par, i, :]
                    nc.vector.scalar_tensor_tensor(rows, xl2[:, i, :], stay[:, i:i + 1], rows, ALU.mult,
                                                   ALU.add).then_inc(base_ready, 1)

            dv.wait_ge(made, N_MADE)
            dv.wait_ge(const_in, CONST_IN)
            run(work, dv, done, 2 * (TT + HALVES + TT + TT + 1 + 3 * TT + 2))

        @block.tensor
        def _(pe):
            pe.wait_ge(made, N_MADE)
            pe.wait_ge(const_in, CONST_IN)
            nc.tensor.transpose(t_bank[:, 0:P], w_bd[:, 0, :], ident[:, :]).then_inc(wq_turned, 1)
            pe.wait_ge(wq_copied, 1)

            def work(kind, i, n):
                if kind == "ctx":
                    if i == 0:
                        pe.wait_ge(cx_in, n.count(16, 16))
                    wait(pe, t_copied, t_count(kind, i, n) - 1)
                    if i == 0:
                        for c in range(DC):
                            ins = nc.tensor.transpose(t_bank[:, SK * c:SK * c + SK], cx[:, P * c:P * c + P],
                                                      ident[0:SK, 0:SK])
                    elif i == 1:
                        ins = nc.tensor.matmul(t_bank[:, 0:DC * SK], w_bd[:, 1, :],
                                               cx_t[:, :, :].rearrange("p c k -> p (c k)"), start=True, stop=True)
                    elif i == 2:
                        ins = nc.tensor.matmul(t_bank[:, 0:DC * SK], wq_bt[:, :],
                                               key_t[:, :, :].rearrange("p c k -> p (c k)"), start=True, stop=True)
                    else:
                        for c in range(DC):
                            ins = nc.tensor.matmul(t_bank[0:SK, P * c:P * c + P], cx_t[:, c, :], w_bd[:, 2, :],
                                                   start=True, stop=True)
                    ins.then_inc(turned, 1)
                if kind == "turn":
                    pe.wait_ge(xl_ready, n.count(TT, i + 1))
                    pe.wait_ge(t_copied, t_count(kind, i, n) - 1)
                    for c in range(DC):
                        ins = nc.tensor.transpose(t_bank[:, P * c:P * c + P], xl[:, i % 2, P * c:P * c + P], ident[:, :])
                    ins.then_inc(turned, 1)
                if kind == "e":
                    pe.wait_ge(t_copied, t_count("turn", i // 2, n))
                    wait(pe, masked, n.count(HALVES, i))
                    for c in range(2):
                        k = 2 * (i % 2) + c
                        ins = nc.tensor.matmul(e_bank[:, c, 0:CH * SK], xl_t[:, (i // 2) % 2, P * k:P * k + P],
                                               qk_bd[:, n.par, k].rearrange("p h k -> p (h k)"), start=True, stop=True)
                    ins.then_inc(e_ready, 1)
                if kind == "t":
                    pe.wait_ge(p_ready, n.count(HALVES, i + 1))
                    wait(pe, pt_copied, n.count(HALVES, i))
                    for h in range(2 * CH):
                        ins = nc.tensor.transpose(pt_bank[h // CH][0:SK, P * (h % CH):P * (h % CH) + P], e[:, i % 4, h, :],
                                                  ident[:, :])
                    ins.then_inc(pt_ready, 1)
                if kind == "pv":
                    pe.wait_ge(pt_copied, n.count(HALVES, i + 1))
                    wait(pe, att_ready, n.count(HALVES, i))
                    for h in range(2 * CH):
                        ins = nc.tensor.matmul(o_bank[:, VX * h:VX * h + VX],
                                               p_t[:, i % 2, h // CH, P * (h % CH):P * (h % CH) + P],
                                               vx[:, n.par, 2 * CH * (i % 2) + h, :], start=True, stop=True)
                    ins.then_inc(pv_ready, 1)

                if kind == "row":
                    pe.wait_ge(info_ready, n.count(1, 1))
                    for t in range(TT):
                        ins = nc.tensor.transpose(r_bank[0][:, P * t:P * t + P], info[:, t, 0:1].broadcast_to((P, P)),
                                                  ident[:, :])
                    ins.then_inc(r_ready, 1)
                if kind == "xs":
                    if i == 0:
                        pe.wait_ge(sel_ready, n.count(1, 1))
                    for t in range(TT):
                        ins = nc.tensor.matmul(r_bank[1][:, KEEP * i:KEEP * i + KEEP], xl2[:, t, P * i:P * i + P],
                                               sel[:, t, :], start=(t == 0), stop=(t == TT - 1))
                    if i == DC - 1:
                        for t in range(TT):
                            ins = nc.tensor.matmul(r_bank[1][0:3, DC * KEEP:DC * KEEP + KEEP], info[:, t, :], sel[:, t, :],
                                                   start=(t == 0), stop=(t == TT - 1))
                        ins.then_inc(r_ready, 1)
                if kind == "a1":
                    if i == 0:
                        pe.wait_ge(am_in, n.count(16, 16))
                    for t in range(TT):
                        ins = nc.tensor.matmul(r_bank[0][:, KEEP * i:KEEP * i + KEEP], am[:, t, P * i:P * i + P],
                                               sel[:, t, :], start=(t == 0), stop=(t == TT - 1))
                    if i == TT - 1:
                        ins.then_inc(r_ready, 1)

            run(work, pe)


FH, FD = 16, 32
FF = 2048
FC = FF // P
FV = FD + 1
ROPE_BASE = 10000.0
TURN = 2 * np.pi
TURN_PARTS = (6.28125, 1.93500518798828125e-3, 3.0199159795074593e-7)
ROUNDING = 1.5 * 2.0 ** 23
HALF_TURN = float(np.nextafter(np.float32(np.pi), np.float32(0)))
NT = NSEL // P


def routed_plan():
    plan = [("info", 0), ("mask", 0)] + [("xs", t) for t in range(NT)]
    plan += [(k, 0) for k in ("q", "k", "v", "tq", "tk")] + [(k, 1) for k in ("q", "k", "v")]
    units = NT * DC
    for s in range(units + 8):
        if s < units:
            plan.append(("s", s))
            t, c = divmod(s, DC)
            if c == 0 and 1 <= t < NT - 1:
                plan += [(k, t + 1) for k in ("q", "k")]
            if c == 1 and t + 1 < NT:
                plan += [("tq", t + 1), ("tk", t + 1)]
            if c == 2 and 1 <= t < NT - 1:
                plan.append(("v", t + 1))
        if 1 <= s < units + 1:
            plan.append(("t", s - 1))
        if 2 <= s < units + 2:
            plan.append(("pv", s - 2))
        if s >= DC + 2 and (s - DC - 2) % DC == 0 and (s - DC - 2) // DC < NT:
            plan.append(("ot", (s - DC - 2) // DC))
        if s >= DC + 3 and (s - DC - 3) % DC == 0 and (s - DC - 3) // DC < NT:
            plan.append(("wo", (s - DC - 3) // DC))
        if s >= DC + 5 and (s - DC - 5) % DC == 0 and (s - DC - 5) // DC < NT:
            plan.append(("th", (s - DC - 5) // DC))
    plan += [("th", t) for t in range(NT) if ("th", t) not in plan]
    return plan + [("w1", f) for f in range(FC)] + [("w2", t) for t in range(NT)]


def routed_block(nc, xsel_t, info_t, picked, mask_rows, w4, ln1, ln2, w1, w2, out):
    plan = routed_plan()
    RINGS = {}
    for name, kinds in (("big", ("q", "k", "v", "wo", "w1", "w2")), ("turn", ("xs", "tq", "tk", "t", "ot", "th")),
                        ("score", ("s",)), ("small", ("info", "mask", "pv"))):
        keys = [s for s in plan if s[0] in kinds]
        for n, key in enumerate(keys):
            RINGS[key] = (name, n % 2, keys[n - 2] if n >= 2 else None)
    KINDS = sorted({s[0] for s in plan})
    with ExitStack() as ctx:
        def sb(name, shape, dt=F32):
            return ctx.enter_context(nc.sbuf_tensor(name, shape, dt))

        def sem(name):
            return ctx.enter_context(nc.semaphore(name))

        w1_sb, w2_sb = sb("w1_sb", [P, DC, FF]), sb("w2_sb", [P, FC, D])
        xs = sb("xs", [P, NT, D])
        x1f = sb("x1f", [P, NT, D])
        h_t = xsel_t
        h2_t = mask_rows
        g_t = w4
        rot, rot_b = sb("rot", [P, 2, D]), sb("rot_b", [P, 2, D])
        q_t = sb("q_t", [P, 2, DC, P])
        k_bd = sb("k_bd", [P, 2, DC, CH, P])
        v_sb = sb("v_sb", [P, 2, FH, FV])
        e = sb("f_e", [P, 2, CH, P])
        p_t = sb("f_p_t", [P, 2, CH, P])
        o_n = sb("f_o_n", [P, 2, D])
        o_t = sb("f_o_t", [P, 2, DC, P])
        hn = sb("hn", [P, 2, D])
        m_full = sb("m_full", [P, NT, P])
        m_slot = sb("m_slot", [P, P])
        fin = picked
        junk = sb("f_junk", [P, D], BF16)
        ident = sb("f_ident", [P, P])
        l1, l2 = sb("l1", [P, DC]), sb("l2", [P, DC])
        info = sb("f_info", [P, NT, 3])
        idx = sb("idx", [P, NT], U32)
        first_row, live, inv = sb("first_row", [P, NT]), sb("live", [P, 1]), sb("inv", [P, FD // 2])
        half = sb("f_half", [P, NT])
        w_sel = sb("w_sel", [P, NT])
        ang, turns, sc = sb("ang", [P, NT, 16]), sb("turns", [P, 2, NT, 16]), sb("sc", [P, 2, NT, 16])
        minus_sin = sb("minus_sin", [P, NT, 16])
        ss, ss2 = sb("ss", [P, NT]), sb("ss2", [P, NT])
        r1, rq, r2 = sb("r1", [P, 2, NT]), sb("rq", [P, NT]), sb("r2", [P, 2, NT])
        nmax, den = sb("f_nmax", [P, 2, CH]), sb("f_den", [P, 2, CH])

        banks = {n: [ctx.enter_context(nc.psum_tensor(f"{n}_bank{i}", [P, 512], F32)) for i in range(2)]
                 for n in ("big", "turn", "score", "small")}
        made = {k: sem(f"{k}_made") for k in KINDS}
        read = {k: sem(f"{k}_read") for k in KINDS}
        w1_in, w2_in, ln_in, idx_ready, rows_in, out_done = (
            sem(n) for n in ("w1_in", "w2_in", "ln_in", "idx_ready", "rows_in", "out_done"))
        const, pool_step, dve_step, act_step = (sem(n) for n in ("f_const", "f_pool_step", "f_dve_step", "f_act_step"))
        ht_ready, angles_ready, sincos_ready, ss_ready, r1_ready = (
            sem(n) for n in ("ht_ready", "angles_ready", "sincos_ready", "ss_ready", "r1_ready"))
        rot_ready, fmax_ready, exp_ready, ss2_ready, hn_ready, fin_ready = (
            sem(n) for n in ("rot_ready", "fmax_ready", "exp_ready", "ss2_ready", "hn_ready", "fin_ready"))

        def bank(key):
            name, slot, _ = RINGS[key]
            return banks[name][slot]

        N_CONST_MADE = 1
        out_rows = out.rearrange("b s d -> (b s) d")
        block = ctx.enter_context(nc.Block())

        @block.sync
        def _(sp):
            with nc.allow_non_contiguous_dma(reason="one column per chunk"):
                for dst, src in ((l1, ln1), (l2, ln2)):
                    sp.dma_start(dst[:, :], src.rearrange("(c p) -> p c", p=P)).then_inc(ln_in, 16)
            sp.dma_start(w1_sb[:, :, :], w1.rearrange("(c p) f -> p c f", p=P)).then_inc(w1_in, 16)
            sp.dma_start(w2_sb[:, :, :], w2.rearrange("(c p) d -> p c d", p=P)).then_inc(w2_in, 16)

        @block.gpsimd
        def _(pl):
            done = Tally(pool_step)

            def step(ins):
                done.mark(ins)
                done.wait(pl)

            for t in range(NT):
                for b in range(2):
                    step(nc.gpsimd.memset(first_row[KEEP * b:KEEP * b + KEEP, t:t + 1], float(S * (2 * t + b))))
            step(nc.gpsimd.memset(half[:, :], -0.5))
            step(nc.gpsimd.memset(ident[:, :], 0.0))
            step(nc.gpsimd.affine_select(out=ident[:, :], in_=ident[:, :], compare_op=ALU.not_equal, fill=1.0, base=0,
                                         pattern=[[-1, P]], channel_multiplier=1))
            for j in range(FD // 2):
                step(nc.gpsimd.memset(inv[:, j:j + 1], float(np.float32(1.0) / np.float32(ROPE_BASE)
                                                           ** np.float32(2 * j / FD))))
            step(nc.gpsimd.memset(m_slot[:, :], 0.0))
            step(nc.gpsimd.memset(m_slot[0:KEEP, KEEP:P], NEG))
            step(nc.gpsimd.memset(m_slot[KEEP:P, 0:KEEP], NEG))
            step(nc.gpsimd.memset(m_slot[:, KEEP - 1:KEEP], NEG))
            step(nc.gpsimd.memset(m_slot[:, P - 1:P], NEG))
            step(nc.gpsimd.memset(live[:, :], 1.0))
            for last in (KEEP - 1, P - 1):
                step(nc.gpsimd.affine_select(out=live[:, :], in_=live[:, :], compare_op=ALU.not_equal, fill=0.0,
                                             base=-last, pattern=[[0, 1]], channel_multiplier=1))
            step(nc.gpsimd.memset(v_sb[:, :, :, FD:FV], 1.0))
            nc.gpsimd.memset(k_bd[:, :, :, :, :], 0.0).then_inc(const, 1)
            pl.wait_ge(made["mask"], 1)
            pl.wait_ge(idx_ready, 1)
            for t in range(NT):
                nc.gpsimd.indirect_dma_start(fin[:, t, :], None, out_rows, IndirectOffsetOnAxis(ap=idx[:, t:t + 1], axis=0)
                                             ).then_inc(rows_in, 16)
            pl.wait_ge(ss_ready, NT)
            step(nc.gpsimd.tensor_scalar(r1[:, 0], ss[:, :], 1.0 / D, EPS_RMS, ALU.mult, ALU.add))
            step(nc.gpsimd.tensor_tensor(r1[:, 1], r1[:, 0], half[:, :], ALU.pow))
            nc.gpsimd.tensor_scalar(rq[:, :], r1[:, 1], FD ** -0.5, 1.0, ALU.mult, ALU.mult).then_inc(r1_ready, 1)
            for t in range(NT):
                pl.wait_ge(ss2_ready, t + 1)
                step(nc.gpsimd.tensor_scalar(r2[:, 0, t:t + 1], ss2[:, t:t + 1], 1.0 / D, EPS_RMS, ALU.mult, ALU.add))
                step(nc.gpsimd.tensor_tensor(r2[:, 1, t:t + 1], r2[:, 0, t:t + 1], half[:, 0:1], ALU.pow))
                if t >= 2:
                    pl.wait_ge(made["th"], t - 1)
                nc.gpsimd.tensor_scalar(hn[:, t % 2, :], x1f[:, t, :], r2[:, 1, t:t + 1], 1.0, ALU.mult,
                                        ALU.mult).then_inc(hn_ready, 1)
            for t in range(NT):
                pl.wait_ge(fin_ready, t + 1)
                nc.gpsimd.indirect_dma_start(out_rows, IndirectOffsetOnAxis(ap=idx[:, t:t + 1], axis=0), fin[:, t, :], None
                                             ).then_inc(out_done, 16)
            pl.wait_ge(out_done, 16 * NT)

        @block.scalar
        def _(act):
            for kind, i in plan:
                t, c = divmod(i, DC) if kind in ("s", "t", "pv") else (i, 0)
                if kind == "xs":
                    act.wait_ge(made[kind], i + 1)
                    nc.scalar.copy(xs[:, i, :], bank((kind, i))[:, :]).then_inc(read[kind], 1)
                    if i == NT - 1:
                        act.wait_ge(ln_in, 32)
                        for n in range(DC):
                            nc.scalar.activation(h_t[:, n, :], h_t[:, n, :], ACT.Copy,
                                                 scale=l1[:, n:n + 1]).then_inc(ht_ready, 1)
                        act.wait_ge(angles_ready, 1)
                        nc.scalar.activation(sc[:, :, :, :], turns[:, :, :, :], ACT.Sin).then_inc(sincos_ready, 1)
                if kind == "v":
                    act.wait_ge(made[kind], i + 1)
                    act.wait_ge(r1_ready, 1)
                    act.wait_ge(const, N_CONST_MADE)
                    if i >= 2:
                        act.wait_ge(made["pv"], DC * (i - 1))
                    nc.scalar.activation(v_sb[:, i % 2, :, 0:FD], bank((kind, i))[:, :].rearrange("p (h d) -> p h d", d=FD),
                                         ACT.Copy, scale=r1[:, 1, i:i + 1]).then_inc(read[kind], 1)
                if kind == "tq":
                    act.wait_ge(made[kind], i + 1)
                    if i >= 2:
                        act.wait_ge(made["s"], DC * (i - 1))
                    nc.scalar.copy(q_t[:, i % 2].rearrange("p c k -> p (c k)"), bank((kind, i))[:, :]).then_inc(read[kind], 1)
                if kind == "tk":
                    act.wait_ge(made[kind], i + 1)
                    for h in range(CH):
                        rows = slice(FD * h, FD * h + FD)
                        ins = nc.scalar.copy(k_bd[rows, i % 2, :, h, :],
                                             bank((kind, i))[rows, :].rearrange("p (c k) -> p c k", c=DC))
                    ins.then_inc(read[kind], 1)
                if kind == "s":
                    act.wait_ge(fmax_ready, i + 1)
                    for h in range(CH):
                        ins = nc.scalar.activation(e[:, i % 2, h, :], e[:, i % 2, h, :], ACT.Exp,
                                                   bias=nmax[:, i % 2, h:h + 1])
                    ins.then_inc(exp_ready, 1)
                if kind == "ot":
                    act.wait_ge(made[kind], i + 1)
                    if i >= 2:
                        act.wait_ge(made["wo"], i - 1)
                    nc.scalar.copy(o_t[:, i % 2].rearrange("p c k -> p (c k)"), bank((kind, i))[:, :]).then_inc(read[kind], 1)
                if kind == "w1":
                    act.wait_ge(made[kind], i + 1)
                    if i == 0:
                        act.wait_ge(made["wo"], NT)
                    nc.scalar.activation(g_t[:, i // DC, i % DC, :], bank((kind, i))[:, :],
                                         ACT.Gelu_apprx_tanh).then_inc(read[kind], 1)

        @block.vector
        def _(dv):
            done = Tally(dve_step)

            def step(ins):
                done.mark(ins)
                done.wait(dv)

            dv.wait_ge(const, N_CONST_MADE)
            for kind, i in plan:
                t, c = divmod(i, DC) if kind in ("s", "t", "pv") else (i, 0)
                if kind in ("info", "mask", "q", "k", "t", "pv", "wo", "th", "w2", "s"):
                    dv.wait_ge(made[kind], i + 1)
                if kind == "info":
                    nc.vector.tensor_copy(info[:, :, :], bank((kind, i))[:, 0:3 * NT].rearrange("p (t k) -> p t k", k=3)
                                          ).then_inc(read[kind], 1)
                    dv.wait_ge(read[kind], 1)
                    nc.vector.tensor_tensor(idx[:, :], info[:, :, 2], first_row[:, :], ALU.add).then_inc(idx_ready, 1)
                    nc.vector.tensor_scalar(w_sel[:, :], info[:, :, 0], live[:, 0:1], None, ALU.mult)
                    shape = (P, NT, FD // 2)
                    step(nc.vector.tensor_tensor(ang[:, :, :], info[:, :, 1].unsqueeze(2).broadcast_to(shape),
                                                 inv[:, :].unsqueeze(1).broadcast_to(shape), ALU.mult))
                    for n in range(2):
                        step(nc.vector.tensor_scalar(sc[:, n], ang[:, :, :], 1 / TURN, 0.25 * n, ALU.mult, ALU.add))
                        step(nc.vector.tensor_scalar(sc[:, n], sc[:, n], ROUNDING, None, ALU.add))
                        step(nc.vector.tensor_scalar(sc[:, n], sc[:, n], -ROUNDING, None, ALU.add))
                        src = ang[:, :, :]
                        for part in TURN_PARTS:
                            step(nc.vector.scalar_tensor_tensor(turns[:, n], sc[:, n], -part, src, ALU.mult, ALU.add))
                            src = turns[:, n]
                        if n:
                            step(nc.vector.tensor_scalar(turns[:, n], turns[:, n], TURN / 4, None, ALU.add))
                        ins = nc.vector.tensor_scalar(turns[:, n], turns[:, n], HALF_TURN, -HALF_TURN, ALU.min, ALU.max)
                    ins.then_inc(angles_ready, 1)
                if kind == "mask":
                    nc.vector.tensor_tensor(m_full[:, :, :], bank((kind, i))[:, :].rearrange("p (t k) -> p t k", t=NT),
                                            m_slot[:, :].unsqueeze(1).broadcast_to((P, NT, P)), ALU.add
                                            ).then_inc(read[kind], 1)
                if kind == "xs":
                    dv.wait_ge(read["xs"], i + 1)
                    nc.vector.tensor_tensor_reduce(junk[:, :], xs[:, i, :], xs[:, i, :], 1.0, 0.0, ALU.mult, ALU.add,
                                                   ss[:, i:i + 1]).then_inc(ss_ready, 1)
                    dv.wait_ge(ss_ready, i + 1)
                    if i == NT - 1:
                        dv.wait_ge(sincos_ready, 1)
                        step(nc.vector.tensor_scalar(minus_sin[:, :, :], sc[:, 0], -1.0, None, ALU.mult))
                        dv.wait_ge(r1_ready, 1)
                if kind in ("q", "k"):
                    n = 2 * t + (kind == "k")
                    scale = rq[:, t:t + 1] if kind == "q" else r1[:, 1, t:t + 1]
                    b4 = bank((kind, i))[:, :].rearrange("p (h m j) -> p h m j", h=FH, m=2)
                    r4 = rot_b[:, n % 2, :].rearrange("p (h m j) -> p h m j", h=FH, m=2)
                    if n >= 2:
                        dv.wait_ge(made["tq" if kind == "q" else "tk"], t)
                    done.mark(nc.vector.scalar_tensor_tensor(
                        rot[:, n % 2, :].rearrange("p (r j) -> p r j", j=16),
                        bank((kind, i))[:, :].rearrange("p (r j) -> p r j", j=16), scale,
                        sc[:, 1, t, :].unsqueeze(1).broadcast_to((P, 2 * FH, 16)), ALU.mult, ALU.mult))
                    done.mark(nc.vector.scalar_tensor_tensor(
                        r4[:, :, 0, :], b4[:, :, 1, :], scale, minus_sin[:, t, :].unsqueeze(1).broadcast_to((P, FH, 16)),
                        ALU.mult, ALU.mult))
                    nc.vector.scalar_tensor_tensor(
                        r4[:, :, 1, :], b4[:, :, 0, :], scale, sc[:, 0, t, :].unsqueeze(1).broadcast_to((P, FH, 16)),
                        ALU.mult, ALU.mult).then_inc(read[kind], 1)
                    dv.wait_ge(read[kind], i + 1)
                    nc.vector.tensor_tensor(rot[:, n % 2, :], rot[:, n % 2, :], rot_b[:, n % 2, :],
                                            ALU.add).then_inc(rot_ready, 1)
                if kind == "s":
                    if i >= 2:
                        dv.wait_ge(made["t"], i - 1)
                    nc.vector.tensor_tensor(e[:, i % 2], bank((kind, i))[:, :].rearrange("p (h k) -> p h k", h=CH),
                                            m_full[:, t, :].unsqueeze(1).broadcast_to((P, CH, P)),
                                            ALU.add).then_inc(read[kind], 1)
                    dv.wait_ge(read[kind], i + 1)
                    nc.vector.tensor_reduce(nmax[:, i % 2, :], e[:, i % 2], AX.X, ALU.max, negate=True
                                            ).then_inc(fmax_ready, 1)
                if kind == "t":
                    if i >= 2:
                        dv.wait_ge(made["pv"], i - 1)
                    nc.vector.tensor_copy(p_t[:, i % 2].rearrange("p h k -> p (h k)"), bank((kind, i))[:, :]
                                          ).then_inc(read[kind], 1)
                if kind == "pv":
                    o = bank((kind, i))[:, 0:CH * FV].rearrange("p (h v) -> p h v", v=FV)
                    step(nc.vector.reciprocal(den[:, i % 2, :], o[:, :, FD]))
                    if c == 0 and t >= 2:
                        dv.wait_ge(made["ot"], t - 1)
                    nc.vector.tensor_tensor(o_n[:, t % 2, P * c:P * c + P].rearrange("p (h d) -> p h d", h=CH), o[:, :, 0:FD],
                                            den[:, i % 2, :].unsqueeze(2).broadcast_to((P, CH, FD)),
                                            ALU.mult).then_inc(read[kind], 1)
                if kind == "wo":
                    nc.vector.tensor_tensor(x1f[:, i, :], bank((kind, i))[:, :], xs[:, i, :], ALU.add
                                            ).then_inc(read[kind], 1)
                    dv.wait_ge(read[kind], i + 1)
                    nc.vector.tensor_tensor_reduce(junk[:, :], x1f[:, i, :], x1f[:, i, :], 1.0, 0.0, ALU.mult, ALU.add,
                                                   ss2[:, i:i + 1]).then_inc(ss2_ready, 1)
                    dv.wait_ge(ss2_ready, i + 1)
                if kind == "th":
                    nc.vector.tensor_tensor(h2_t[:, :, P * i:P * i + P],
                                            bank((kind, i))[:, :].rearrange("p (c k) -> p c k", c=DC),
                                            l2[:, :].unsqueeze(2).broadcast_to((P, DC, P)), ALU.mult
                                            ).then_inc(read[kind], 1)
                if kind == "w2":
                    nc.vector.tensor_tensor(x1f[:, i, :], bank((kind, i))[:, :], x1f[:, i, :], ALU.add
                                            ).then_inc(read[kind], 1)
                    dv.wait_ge(read[kind], i + 1)
                    dv.wait_ge(rows_in, 16 * NT)
                    nc.vector.scalar_tensor_tensor(fin[:, i, :], x1f[:, i, :], w_sel[:, i:i + 1], fin[:, i, :], ALU.mult,
                                                   ALU.add).then_inc(fin_ready, 1)

        @block.tensor
        def _(pe):
            pe.wait_ge(const, N_CONST_MADE)
            for kind, i in plan:
                before = RINGS[kind, i][2]
                if before:
                    pe.wait_ge(read[before[0]], before[1] + 1)
                to = bank((kind, i))
                t, c = divmod(i, DC) if kind in ("s", "t", "pv") else (i, 0)
                tok = slice(P * i, P * i + P)
                if kind == "info":
                    for n in range(NT):
                        ins = nc.tensor.transpose(to[:, 3 * n:3 * n + 3], info_t[:, P * n:P * n + P], ident[0:3, 0:3])
                if kind == "mask":
                    for n in range(NT):
                        cols = slice(P * n, P * n + P)
                        for k in range(TT):
                            ins = nc.tensor.matmul(to[:, cols], mask_rows[:, k, cols], picked[:, k, cols],
                                                   start=(k == 0), stop=(k == TT - 1))
                if kind == "xs":
                    for n in range(DC):
                        ins = nc.tensor.transpose(to[:, P * n:P * n + P], xsel_t[:, n, tok], ident[:, :])
                if kind in ("q", "k", "v"):
                    pe.wait_ge(ht_ready, DC)
                    for n in range(DC):
                        ins = nc.tensor.matmul(to[:, :], h_t[:, n, tok], w4[:, "qkv".index(kind), n, :],
                                               start=(n == 0), stop=(n == DC - 1))
                if kind in ("tq", "tk"):
                    n = 2 * i + (kind == "tk")
                    pe.wait_ge(rot_ready, n + 1)
                    for k in range(DC):
                        ins = nc.tensor.transpose(to[:, P * k:P * k + P], rot[:, n % 2, P * k:P * k + P], ident[:, :])
                if kind == "s":
                    pe.wait_ge(read["tq"], t + 1)
                    pe.wait_ge(read["tk"], t + 1)
                    ins = nc.tensor.matmul(to[:, :], q_t[:, t % 2, c, :], k_bd[:, t % 2, c].rearrange("p h k -> p (h k)"),
                                           start=True, stop=True)
                if kind == "t":
                    pe.wait_ge(exp_ready, i + 1)
                    for h in range(CH):
                        ins = nc.tensor.transpose(to[:, P * h:P * h + P], e[:, i % 2, h, :], ident[:, :])
                if kind == "pv":
                    pe.wait_ge(read["t"], i + 1)
                    pe.wait_ge(read["v"], t + 1)
                    for h in range(CH):
                        ins = nc.tensor.matmul(to[:, FV * h:FV * h + FV], p_t[:, i % 2, h, :],
                                               v_sb[:, t % 2, CH * c + h, :], start=True, stop=True)
                if kind == "ot":
                    pe.wait_ge(read["pv"], DC * (i + 1))
                    for n in range(DC):
                        ins = nc.tensor.transpose(to[:, P * n:P * n + P], o_n[:, i % 2, P * n:P * n + P], ident[:, :])
                if kind == "wo":
                    pe.wait_ge(read["ot"], i + 1)
                    for n in range(DC):
                        ins = nc.tensor.matmul(to[:, :], o_t[:, i % 2, n, :], w4[:, 3, n, :], start=(n == 0),
                                               stop=(n == DC - 1))
                if kind == "th":
                    pe.wait_ge(hn_ready, i + 1)
                    for n in range(DC):
                        ins = nc.tensor.transpose(to[:, P * n:P * n + P], hn[:, i % 2, P * n:P * n + P], ident[:, :])
                if kind == "w1":
                    pe.wait_ge(w1_in, 16)
                    pe.wait_ge(read["th"], NT)
                    for n in range(DC):
                        ins = nc.tensor.matmul(to[:, :], w1_sb[:, n, P * i:P * i + P], h2_t[:, n, :], start=(n == 0),
                                               stop=(n == DC - 1))
                if kind == "w2":
                    pe.wait_ge(w2_in, 16)
                    pe.wait_ge(read["w1"], FC)
                    for f in range(FC):
                        ins = nc.tensor.matmul(to[:, :], g_t[:, f // DC, f % DC, tok], w2_sb[:, f, :], start=(f == 0),
                                               stop=(f == FC - 1))
                ins.then_inc(made[kind], 1)


def pre_ln_decoder_layer(nc, x, ctx_1024, mask_1x1xSxS2_fk0, L0_attn_norm_w, L0_attn_w_q, L0_attn_w_k, L0_attn_w_v,
                         L0_attn_w_out, L0_attn_scorer_w, L0_attn_scorer_b, L0_xattn_Wq, L0_xattn_Wk, L0_xattn_Wv,
                         L0_ffn_attention_mask, L0_ffn_position_ids, L0_ffn_router_w, L0_ffn_router_b, L0_ffn_wq,
                         L0_ffn_wk, L0_ffn_wv, L0_ffn_wo, L0_ffn_w1, L0_ffn_w2, L0_ffn_ln1, L0_ffn_ln2, out):
    x1 = nc.dram_tensor("x1", [B, S, D], F32, kind="Internal").ap()
    self_attention(nc, x, L0_attn_norm_w, L0_attn_w_q, L0_attn_w_k, L0_attn_w_v, L0_attn_w_out, L0_attn_scorer_w,
                   L0_attn_scorer_b, x1)
    with ExitStack() as ctx:
        def sb(name, shape):
            return ctx.enter_context(nc.sbuf_tensor(name, shape, F32))

        xsel_t, info_t = sb("xsel_t", [P, DC, NSEL]), sb("info_t", [3, NSEL])
        picked, mask_rows = sb("picked", [P, TT, NSEL]), sb("mask_rows", [P, TT, NSEL])
        w4 = sb("w4", [P, 4, DC, D])
        later = [(w4[:, k], w.rearrange("(c p) d -> p c d", p=P))
                 for k, w in enumerate((L0_ffn_wq, L0_ffn_wk, L0_ffn_wv, L0_ffn_wo))]
        cross_and_router(nc, x1, ctx_1024, mask_1x1xSxS2_fk0, L0_xattn_Wq, L0_xattn_Wk, L0_xattn_Wv,
                         L0_ffn_attention_mask, L0_ffn_position_ids, L0_ffn_router_w, L0_ffn_router_b, out,
                         xsel_t, info_t, picked, mask_rows, later)
        routed_block(nc, xsel_t, info_t, picked, mask_rows, w4, L0_ffn_ln1, L0_ffn_ln2, L0_ffn_w1, L0_ffn_w2, out)


_INS = ["x", "ctx_1024", "mask_1x1xSxS2_fk0", "L0_attn_norm_w", "L0_attn_w_q", "L0_attn_w_k", "L0_attn_w_v",
        "L0_attn_w_out", "L0_attn_scorer_w", "L0_attn_scorer_b", "L0_xattn_Wq", "L0_xattn_Wk", "L0_xattn_Wv",
        "L0_ffn_attention_mask", "L0_ffn_position_ids", "L0_ffn_router_w", "L0_ffn_router_b", "L0_ffn_wq",
        "L0_ffn_wk", "L0_ffn_wv", "L0_ffn_wo", "L0_ffn_w1", "L0_ffn_w2", "L0_ffn_ln1", "L0_ffn_ln2"]


def kernel(**inputs):
    import numpy as _np
    import concourse.bacc as _bacc
    from concourse import mybir as _mybir
    from concourse.bass_utils import run_bass_kernel_spmd as _run

    nc = _bacc.Bacc("TRN2", target_bir_lowering=False, num_devices=1)
    arrays, args = {}, []
    for name in _INS:
        a = _np.ascontiguousarray(inputs[name])
        arrays[f"in_{name}"] = a
        args.append(nc.dram_tensor(f"in_{name}", a.shape, _mybir.dt.from_np(a.dtype), kind="ExternalInput").ap())
    args.append(nc.dram_tensor("out_0", (B, S, D), F32, kind="ExternalOutput").ap())
    pre_ln_decoder_layer(nc, *args)
    r = _run(nc, [arrays], core_ids=[0])
    return r.results[0]["out_0"]
```

```python
from contextlib import ExitStack, contextmanager

import numpy as np
import concourse.bass as bass
from concourse import mybir
from concourse.bass import IndirectOffsetOnAxis

F32 = mybir.dt.float32
F32R = mybir.dt.float32r
BF16 = mybir.dt.bfloat16
I8 = mybir.dt.int8
I32 = mybir.dt.int32
U32 = mybir.dt.uint32
ALU = mybir.AluOpType
ACT = mybir.ActivationFunctionType
AX = mybir.AxisListType

P = 128
B, S, D = 8, 512, 512
TT = S // P
DC = D // P
EPS_LN = 1e-5
EPS_RMS = 1e-6

H, HD = 16, 64
NPAIR = H // 2
TOPK = 128
NEG = -1e30
UNITS = 5
NU = NPAIR * UNITS
VW = HD + 1


class Tally:

    def __init__(self, sem):
        self.sem, self.start, self.round, self.n = sem, 0, 0, 0

    @contextmanager
    def loop(self, i, per, trips):
        self.start, self.round, self.n = self.start + self.n, i * per, 0
        yield
        assert self.n == per, (self.n, per)
        self.start, self.round, self.n = self.start + trips * per, 0, 0

    def mark(self, ins):
        ins.then_inc(self.sem, 1)
        self.n += 1

    def wait(self, eng):
        eng.wait_ge(self.sem, self.round + (self.start + self.n))


RANK_AT = (22, 24, 27, 29)


def unit_blocks(u):
    if u < 2:
        return [(u, 3, 0, 512)]
    if u < 4:
        return [(u - 2, 0, 0, 128), (u - 2, 2, 128, 384)]
    return [(0, 1, 0, 256), (1, 1, 256, 256)]


def head_rows(h):
    return slice(HD * h, HD * h + HD)


def attention_plan():
    plan = [("v", i) for i in range(2 * TT - 2)] + [("q", 0), ("q_lo", 0), ("k", 0), ("k_lo", 0)]
    plan += [("v", i) for i in range(2 * TT - 2, 2 * TT)]
    for g in range(NU + 7):
        p, u = divmod(g, UNITS)
        if g < NU:
            plan.append(("s", g))
        if 2 <= g < NU + 2:
            plan.append(("t", g - 2))
        if 3 <= g < NU + 3:
            plan.append(("pv", g - 3))
        if g < NU and p + 1 < NPAIR and u < 4:
            plan.append((("q", "q_lo", "k", "k_lo")[u], p + 1))
        if g == 5:
            plan.append(("stats", 0))
        if g == 14:
            plan.append(("dot", 0))
        if g == 18:
            plan.append(("score", 0))
        if g in RANK_AT:
            plan.append(("rank", RANK_AT.index(g)))
        if NU <= g < NU + DC:
            plan.append(("ht", g - NU))
        if g >= 9 and (g - 9) % UNITS == 0 and (g - 9) // UNITS < NPAIR - 1:
            plan.append(("ot", (g - 9) // UNITS))
    plan.append(("ot", NPAIR - 1))
    plan += [("out", t) for t in range(TT)]
    return plan


def bank_index(plan, kinds):
    return {s: i for i, s in enumerate([s for s in plan if s[0] in kinds])}


def self_attention(nc, x, norm_w, w_q, w_k, w_v, w_out, scorer_w, scorer_b, x1):
    plan = attention_plan()
    PROJ, PT = bank_index(plan, ("v", "q", "k", "out")), bank_index(plan, ("t", "score", "ht", "ot"))
    with ExitStack() as ctx:
        def sb(name, shape, dt=F32):
            return ctx.enter_context(nc.sbuf_tensor(name, shape, dt))

        def bank(name):
            return ctx.enter_context(nc.psum_tensor(name, [P, 512], F32))

        def sem(name):
            return ctx.enter_context(nc.semaphore(name))

        w_hi = {n: sb(f"w{n}_hi", [P, DC, H * HD], F32R) for n in "qkv"}
        w_lo = {n: sb(f"w{n}_lo", [P, DC, H * HD], F32R) for n in "qkv"}
        w_o = sb("w_o", [P, NPAIR, D])
        xb = sb("xb", [P, TT, D])
        ht_hi, ht_lo = sb("ht_hi", [P, DC, S], F32R), sb("ht_lo", [P, DC, S], F32R)
        vals = sb("vals", [P, TT, H, VW])
        q_both, k_twice = sb("q_both", [P, 2, 2, S], F32R), sb("k_twice", [P, 2, 2, S], F32R)
        k_lo = sb("k_lo", [P, 2, S], F32R)
        probs = sb("probs", [P, 2, 512])
        probs_t = sb("probs_t", [P, 2, 512])
        o_rden = sb("o_rden", [P, 2, 2])
        o_norm = sb("o_norm", [P, 2, TT, 2, HD])
        o_t = sb("o_t", [P, NPAIR, S])
        xr = probs
        ident = sb("ident", [P, P])
        ident_b = sb("ident_b", [P, P], BF16)
        causal_b = sb("causal_b", [P, P], BF16)
        before = sb("before", [P, S + P * (TT - 1)], I8)
        row_s = sb("row_s", [P, S])
        junk = sb("junk", [P, S], BF16)
        carrier = sb("carrier", [P, 4])
        nw = sb("nw", [P, DC])
        sw = sb("sw", [P, D])
        sbias = sb("sbias", [P, 1])
        bn = sb("bn", [P, TT, 6])
        mv = sb("mv", [P, TT, 2])
        half, ones, minus, eps_ln, eps_rms, idle = (
            sb(n, [P, TT]) for n in ("half", "ones", "minus", "eps_ln", "eps_rms", "idle"))
        st = sb("st", [P, 5, TT])
        RS, MS, S2, NM, NB = range(5)
        res_next, res_now = sb("res_next", [P, 2, TT]), sb("res_now", [P, 2, TT])
        score = sb("score", [P, TT])
        cnt = sb("cnt", [P, 2, TT])
        twice = sb("twice", [P, TT])
        nmax = sb("nmax", [P, 4, 2])

        s_bank = [bank(f"s_bank{i}") for i in range(2)]
        pt_bank = [bank(f"pt_bank{i}") for i in range(2)]
        pj_bank = [bank(f"pj_bank{i}") for i in range(2)]
        o_bank = [bank(f"o_bank{i}") for i in range(2)]

        w_loaded, split_hi, split_lo = [sem(f"w_loaded{i}") for i in range(2)], sem("split_hi"), sem("split_lo")
        small_in, wo_in, x_in = sem("small_in"), sem("wo_in"), sem("x_in")
        xr_in, x1_out = [sem(f"xr_in{i}") for i in range(2)], [sem(f"x1_out{i}") for i in range(2)]
        const_made, pool_step, dve_step = sem("const_made"), sem("pool_step"), sem("dve_step")
        sw_made, stats_ready, h_ready, score_ready, twice_ready = (
            sem(n) for n in ("sw_made", "stats_ready", "h_ready", "score_ready", "twice_ready"))
        ht_hi_ready, ht_lo_ready = sem("ht_hi_ready"), sem("ht_lo_ready")
        pj_ready, row_copied = sem("pj_ready"), sem("row_copied")
        v_ready, v_sum_ready, qk_hi, qk_lo = sem("v_ready"), sem("v_sum_ready"), sem("qk_hi"), sem("qk_lo")
        s_ready, s_half = sem("s_ready"), sem("s_half")
        max_ready, p_ready = sem("max_ready"), sem("p_ready")
        pt_ready = sem("pt_ready")
        ts_ready, pv_ready, o_copied = sem("ts_ready"), sem("pv_ready"), sem("o_copied")
        ot_ready = sem("ot_ready")
        xr_ready, y_ready = sem("xr_ready"), sem("y_ready")

        NPJ, NPT = len(PROJ), len(PT)
        PT0 = {("ht", c): c for c in range(DC)}
        PT0["score", 0] = DC
        NPT0 = len(PT0)
        W_ORDER = [("v", 0), ("v", 1), ("q", 0), ("k", 0), ("q", 1), ("k", 1)]
        N_CONST = 9
        assert NPJ % 2 == 0

        def pj(b, key):
            return PROJ[key] % 2, b * NPJ + PROJ[key] + 1

        def pt(b, key):
            if b is None:
                return PT0[key] % 2, PT0[key] + 1
            return PT[key] % 2, b * NPT + (PT[key] + 1 + NPT0)

        def taken(eng, b, key):
            kind, i = key
            if kind == "v":
                eng.wait_ge(v_ready, b * (2 * TT) + i + 1)
            elif kind in ("q", "k"):
                eng.wait_ge(qk_lo, b * (2 * NPAIR) + 2 * i + (1 if kind == "q" else 2))
            elif kind == "out":
                eng.wait_ge(y_ready, b * TT + i + 2)
            elif kind == "t":
                eng.wait_ge(ts_ready, b * NU + i + 1)
            elif kind == "ot":
                eng.wait_ge(ot_ready, b * NPAIR + i + 1)
            elif kind == "ht":
                eng.wait_ge(ht_lo_ready, (b + 1) * DC + i + 1)
            elif kind == "score":
                eng.wait_ge(row_copied, b + 2)

        def before_use(order, key):
            keys = list(order)
            return keys[order[key] - 2] if order[key] >= 2 else None

        x_rows = x.rearrange("b (t p) d -> b p t d", p=P)
        x1_rows = x1.rearrange("b (t p) d -> b p t d", p=P)
        w_dram = {n: w.rearrange("(c p) e -> p c e", p=P) for n, w in (("q", w_q), ("k", w_k), ("v", w_v))}

        block = ctx.enter_context(nc.Block())

        @block.sync
        def _(sp):
            sp.dma_start(xb[:, :, :], x_rows[0]).then_inc(x_in, 16)
            with nc.allow_non_contiguous_dma(reason="one column per chunk"):
                sp.dma_start(nw[:, :], norm_w.rearrange("(c p) -> p c", p=P)).then_inc(small_in, 16)
            sp.dma_start(sw[:, :], scorer_w.rearrange("d o -> o d").broadcast_to((P, D))).then_inc(small_in, 16)
            sp.dma_start(row_s[:, :], norm_w.rearrange("(o d) -> o d", o=1).broadcast_to((P, D))).then_inc(small_in, 16)
            sp.dma_start(sbias[:, :], scorer_b.rearrange("(o d) -> o d", o=1).broadcast_to((P, 1))
                         ).then_inc(small_in, 16)
            for i, (n, hw) in enumerate(W_ORDER):
                if i >= 2:
                    sp.wait_ge(split_lo, i - 1)
                sp.dma_start(o_t[:, DC * (i % 2):DC * (i % 2) + DC, :],
                             w_dram[n][:, :, 512 * hw:512 * hw + 512]).then_inc(w_loaded[i % 2], 16)
            sp.dma_start(w_o[:, :, :], w_out.rearrange("(c p) d -> p c d", p=P)).then_inc(wo_in, 16)

            def results(b):
                for t in range(TT + 1):
                    if t < TT:
                        if t < 2:
                            sp.wait_ge(pt_ready, pt(b, ("t", NU - 1))[1])
                        else:
                            sp.wait_ge(x1_out[t % 2], b * (16 * TT // 2) + 16 * (t // 2) + 1)
                        sp.dma_start(xr[:, t % 2, :], x_rows[b][:, t, :]).then_inc(xr_in[t % 2], 16)
                    if t:
                        sp.wait_ge(y_ready, b * TT + t + 1)
                        sp.dma_start(x1_rows[b][:, t - 1, :], xr[:, (t - 1) % 2, :]).then_inc(x1_out[(t - 1) % 2], 16)

            with sp.Fori(0, B - 1) as b:
                sp.wait_ge(ht_lo_ready, b * DC + DC)
                sp.dma_start(xb[:, :, :], x_rows[b + 1]).then_inc(x_in, 16)
                results(b)
            sp.wait_ge(ht_lo_ready, DC * B)
            sp.dma_start(xb[:, :, :], x_rows[0]).then_inc(x_in, 16)
            results(B - 1)
            for half_done in x1_out:
                sp.wait_ge(half_done, 16 * B * TT // 2 + 1)

        @block.gpsimd
        def _(pl):
            done = Tally(pool_step)
            done.mark(nc.gpsimd.memset(ident[:, :], 0.0))
            done.mark(nc.gpsimd.memset(causal_b[:, :], 0.0))
            done.mark(nc.gpsimd.memset(before[:, :], 1.0))
            for tile, value in ((half, -0.5), (ones, 1.0), (minus, -1.0), (eps_ln, EPS_LN), (eps_rms, EPS_RMS)):
                nc.gpsimd.memset(tile[:, :], value).then_inc(const_made, 1)
            done.wait(pl)
            done.mark(nc.gpsimd.affine_select(out=ident[:, :], in_=ident[:, :], compare_op=ALU.not_equal, fill=1.0,
                                              base=0, pattern=[[-1, P]], channel_multiplier=1))
            nc.gpsimd.affine_select(out=causal_b[:, :], in_=causal_b[:, :], compare_op=ALU.is_ge, fill=NEG,
                                    base=0, pattern=[[-1, P]], channel_multiplier=1).then_inc(const_made, 1)
            nc.gpsimd.affine_select(out=before[:, :], in_=before[:, :], compare_op=ALU.is_gt, fill=0.0,
                                    base=P * (TT - 1), pattern=[[-1, S + P * (TT - 1)]],
                                    channel_multiplier=1).then_inc(const_made, 1)
            done.wait(pl)
            nc.gpsimd.tensor_copy(ident_b[:, :], ident[:, :]).then_inc(const_made, 1)
            nc.gpsimd.memset(junk[:, :], 0.0).then_inc(const_made, 1)
            pl.wait_ge(const_made, N_CONST)

            def step(ins):
                done.mark(ins)
                done.wait(pl)

            def carry():
                done.wait(pl)
                done.mark(nc.gpsimd.tensor_tensor(idle[:, :], ones[:, :], ones[:, :], ALU.mult))

            def stats(n):
                pl.wait_ge(stats_ready, n + 1)
                m, v = mv[:, :, 0], mv[:, :, 1]
                step(nc.gpsimd.tensor_tensor(st[:, RS], v, eps_ln[:, :], ALU.add))
                step(nc.gpsimd.tensor_tensor(st[:, RS], st[:, RS], half[:, :], ALU.pow))
                step(nc.gpsimd.tensor_tensor(st[:, MS], st[:, RS], st[:, RS], ALU.mult))
                step(nc.gpsimd.tensor_tensor(st[:, MS], st[:, MS], v, ALU.mult))
                step(nc.gpsimd.tensor_tensor(st[:, MS], st[:, MS], eps_rms[:, :], ALU.add))
                step(nc.gpsimd.tensor_tensor(st[:, S2], st[:, MS], half[:, :], ALU.pow))
                step(nc.gpsimd.tensor_tensor(st[:, S2], st[:, S2], st[:, RS], ALU.mult))
                step(nc.gpsimd.tensor_tensor(st[:, NM], minus[:, :], m, ALU.mult))
                step(nc.gpsimd.tensor_tensor(st[:, NB], st[:, S2], st[:, NM], ALU.mult))
                step(nc.gpsimd.tensor_tensor(res_next[:, 0], st[:, RS], ones[:, :], ALU.add))
                step(nc.gpsimd.tensor_tensor(res_next[:, 1], st[:, RS], st[:, NM], ALU.mult))
                pl.wait_ge(x_in, n * 16 + 16)
                carry()
                for t in range(TT):
                    nc.gpsimd.tensor_scalar(xb[:, t, :], xb[:, t, :], st[:, S2, t:t + 1], st[:, NB, t:t + 1],
                                            ALU.mult, ALU.add).then_inc(h_ready, 1)

            stats(0)
            with pl.Fori(0, B) as b, done.loop(b, 14 + TT, B):
                for r in range(2):
                    step(nc.gpsimd.tensor_tensor(res_now[:, r], res_next[:, r], ones[:, :], ALU.mult))
                for kind, i in plan:
                    if kind == "stats":
                        pl.wait_ge(h_ready, b * TT + TT)
                        stats(b + 1)
                    if kind == "out":
                        pl.wait_ge(xr_in[i % 2], b * (16 * TT // 2) + 16 * (i // 2 + 1))
                        carry()
                        nc.gpsimd.tensor_scalar(xr[:, i % 2, :], xr[:, i % 2, :], res_now[:, 0, i:i + 1],
                                                res_now[:, 1, i:i + 1], ALU.mult, ALU.add).then_inc(xr_ready, 1)
                pl.wait_ge(xr_ready, b * TT + TT)

        @block.scalar
        def _(act):
            def normed(b, n, c):
                slot, ready = pt(b, ("ht", c))
                act.wait_ge(pt_ready, ready)
                nc.scalar.activation(ht_hi[:, c, :], pt_bank[slot][:, :], ACT.Copy,
                                     scale=nw[:, c:c + 1]).then_inc(ht_hi_ready, 1)

            for i, (n, hw) in enumerate(W_ORDER):
                act.wait_ge(w_loaded[i % 2], 16 * (i // 2 + 1))
                nc.scalar.copy(w_hi[n][:, :, 512 * hw:512 * hw + 512],
                               o_t[:, DC * (i % 2):DC * (i % 2) + DC, :]).then_inc(split_hi, 1)
                if i == 1:
                    act.wait_ge(small_in, 64)
                    for c in range(DC):
                        normed(None, 0, c)
            act.wait_ge(split_lo, len(W_ORDER))
            with act.Fori(0, B) as b:
                for kind, i in plan:
                    if kind == "v":
                        t, hw = divmod(i, 2)
                        slot, ready = pj(b, (kind, i))
                        act.wait_ge(pj_ready, ready)
                        if i == 0:
                            act.wait_ge(twice_ready, b + 1)
                        nc.scalar.activation(vals[:, t, 8 * hw:8 * hw + 8, 0:HD],
                                             pj_bank[slot][:, :].rearrange("p (h d) -> p h d", d=HD), ACT.Copy,
                                             scale=twice[:, t:t + 1]).then_inc(v_ready, 1)
                    if kind in ("q", "k"):
                        slot, ready = pj(b, (kind, i))
                        act.wait_ge(pj_ready, ready)
                        for h in range(2):
                            own, other = head_rows(h), head_rows(1 - h)
                            if kind == "q":
                                ins = nc.scalar.activation(q_both[own, i % 2, h, :], pj_bank[slot][own, :], ACT.Copy,
                                                           scale=HD ** -0.5)
                            else:
                                nc.scalar.copy(k_twice[own, i % 2, h, :], pj_bank[slot][own, :])
                                ins = nc.scalar.copy(k_twice[other, i % 2, h, :], pj_bank[slot][own, :])
                        ins.then_inc(qk_hi, 1)
                    if kind == "s":
                        act.wait_ge(max_ready, b * NU + i + 1)
                        if i < 2:
                            act.wait_ge(x1_out[i], b * (16 * TT // 2) + 1)
                        else:
                            act.wait_ge(pt_ready, pt(b, ("t", i - 2))[1])
                        for n, (_, _, c0, nk) in enumerate(unit_blocks(i % UNITS)):
                            ins = nc.scalar.activation(probs[:, i % 2, c0:c0 + nk], s_bank[i % 2][:, c0:c0 + nk],
                                                       ACT.Exp, bias=nmax[:, i % 4, n:n + 1])
                        ins.then_inc(p_ready, 1)
                    if kind == "ht":
                        normed(b, b + 1, i)
                    if kind == "ot":
                        slot, ready = pt(b, (kind, i))
                        act.wait_ge(pt_ready, ready)
                        nc.scalar.copy(o_t[:, i, :], pt_bank[slot][:, :]).then_inc(ot_ready, 1)

        @block.vector
        def _(dv):
            done = Tally(dve_step)

            def step(ins):
                done.mark(ins)
                done.wait(dv)

            def stats(n):
                dv.wait_ge(x_in, n * 16 + 16)
                for t in range(TT):
                    done.mark(nc.vector.bn_stats(bn[:, t, :], xb[:, t, :]))
                done.wait(dv)
                nc.vector.memset(carrier[:, 0:1], 0.0)
                for t in range(TT):
                    ins = nc.vector.bn_aggr(mv[:, t, :], bn[:, t, :])
                ins.then_inc(stats_ready, 1)

            def dot(n):
                dv.wait_ge(h_ready, n * TT + TT)
                for t in range(TT):
                    step(nc.vector.tensor_tensor_reduce(junk[:, :], xb[:, t, :], sw[:, :], 1.0, 0.0, ALU.mult,
                                                             ALU.add, score[:, t:t + 1]))
                done.wait(dv)
                nc.vector.tensor_scalar(score[:, :], score[:, :], sbias[:, 0:1], None, ALU.add).then_inc(score_ready, 1)

            def score_row(b, n):
                slot, ready = pt(b, ("score", 0))
                dv.wait_ge(pt_ready, ready)
                nc.vector.tensor_copy(row_s[:, :], pt_bank[slot][:, :]).then_inc(row_copied, 1)

            def rank(b, n, t):
                if t == 0:
                    dv.wait_ge(row_copied, n + 1)
                step(nc.vector.tensor_scalar(junk[:, :], row_s[:, :], score[:, t:t + 1], None, ALU.is_gt, ALU.add,
                                                  accum_out=cnt[:, 0, t:t + 1]))
                y0 = P * (TT - 1 - t)
                step(nc.vector.scalar_tensor_tensor(junk[:, :], row_s[:, :], score[:, t:t + 1],
                                                         before[:, y0:y0 + S], ALU.is_equal, ALU.mult,
                                                         accum_out=cnt[:, 1, t:t + 1]))
                if t == TT - 1:
                    done.wait(dv)
                    step(nc.vector.tensor_tensor(cnt[:, 0, :], cnt[:, 0, :], cnt[:, 1, :], ALU.add))
                    if b is not None:
                        dv.wait_ge(v_ready, n * (2 * TT))
                    nc.vector.tensor_scalar(twice[:, :], cnt[:, 0, :], TOPK - 0.5, 1.0, ALU.is_lt,
                                            ALU.add).then_inc(twice_ready, 1)

            def normed(b, n, c):
                slot, _ = pt(b, ("ht", c))
                dv.wait_ge(ht_hi_ready, n * DC + c + 1)
                nc.vector.scalar_tensor_tensor(ht_lo[:, c, :], pt_bank[slot][:, :], nw[:, c:c + 1],
                                               ht_hi[:, c, :].bitcast(F32), ALU.mult,
                                               ALU.subtract).then_inc(ht_lo_ready, 1)

            def split(i):
                n, hw = W_ORDER[i]
                dv.wait_ge(split_hi, i + 1)
                cols = slice(512 * hw, 512 * hw + 512)
                nc.vector.tensor_tensor(w_lo[n][:, :, cols], o_t[:, DC * (i % 2):DC * (i % 2) + DC, :],
                                        w_hi[n][:, :, cols].bitcast(F32), ALU.subtract).then_inc(split_lo, 1)

            dv.wait_ge(const_made, N_CONST)
            for i, at_one in enumerate((y_ready, *x1_out)):
                nc.vector.memset(carrier[:, 1 + i:2 + i], 0.0).then_inc(at_one, 1)
            stats(0)
            dv.wait_ge(small_in, 64)
            nc.vector.tensor_tensor(sw[:, :], sw[:, :], row_s[:, :], ALU.mult).then_inc(sw_made, 1)
            dv.wait_ge(sw_made, 1)
            split(0)
            split(1)
            for c in range(DC):
                normed(None, 0, c)
            dot(0)
            split(2)
            score_row(None, 0)
            split(3)
            for t in range(TT):
                rank(None, 0, t)
                if t in (1, 3):
                    split(4 + t // 2)
            with dv.Fori(0, B) as b, done.loop(b, 2 * TT + 2 * TT + 1 + NU, B):
                for kind, i in plan:
                    if kind == "v" and i == 0:
                        dv.wait_ge(twice_ready, b + 1)
                        dv.wait_ge(pj_ready, pj(b, (kind, 0))[1])
                        nc.vector.tensor_copy(vals[:, :, :, HD], twice[:, :].unsqueeze(2).broadcast_to((P, TT, H))
                                              ).then_inc(v_sum_ready, 1)
                    if kind in ("q_lo", "k_lo"):
                        slot, _ = pj(b, (kind[0], i))
                        dv.wait_ge(qk_hi, b * (2 * NPAIR) + 2 * i + (1 if kind == "q_lo" else 2))
                        for h in range(2):
                            own, other = head_rows(h), head_rows(1 - h)
                            if kind == "q_lo":
                                ins = nc.vector.scalar_tensor_tensor(q_both[other, i % 2, h, :], pj_bank[slot][own, :],
                                                                     HD ** -0.5, q_both[own, i % 2, h, :].bitcast(F32),
                                                                     ALU.mult, ALU.subtract)
                            else:
                                ins = nc.vector.tensor_tensor(k_lo[own, i % 2, :], pj_bank[slot][own, :],
                                                              k_twice[own, i % 2, h, :].bitcast(F32), ALU.subtract)
                        ins.then_inc(qk_lo, 1)
                    if kind == "s":
                        dv.wait_ge(s_ready, b * NU + i + 1)
                        blocks = unit_blocks(i % UNITS)
                        if i % UNITS == UNITS - 1:
                            ins = nc.vector.tensor_reduce(nmax[:, i % 4, :],
                                                          s_bank[i % 2][:, :].rearrange("p (h k) -> p h k", h=2),
                                                          AX.X, ALU.max, negate=True)
                        else:
                            for n, (_, _, c0, nk) in enumerate(blocks):
                                ins = nc.vector.tensor_reduce(nmax[:, i % 4, n:n + 1], s_bank[i % 2][:, c0:c0 + nk],
                                                              AX.X, ALU.max, negate=True)
                        ins.then_inc(max_ready, 1)
                    if kind == "t":
                        slot, ready = pt(b, (kind, i))
                        dv.wait_ge(pt_ready, ready)
                        if i >= 2:
                            dv.wait_ge(pv_ready, b * NU + i - 1)
                        nc.vector.tensor_copy(probs_t[:, i % 2, :], pt_bank[slot][:, :]).then_inc(ts_ready, 1)
                    if kind == "pv":
                        p, u = divmod(i, UNITS)
                        dv.wait_ge(pv_ready, b * NU + i + 1)
                        if u == 0 and p >= 2:
                            dv.wait_ge(pt_ready, pt(b, ("ot", p - 2))[1])
                        n = len(unit_blocks(u))
                        src = o_bank[i % 2][:, 0:n * VW].rearrange("p (n v) -> p n v", n=n)
                        if u < 2:
                            dst = o_norm[:, p % 2, 3:4, u, :]
                        elif u < 4:
                            dst = o_norm[:, p % 2, 0:3:2, u - 2, :]
                        else:
                            dst = o_norm[:, p % 2, 1, :, :]
                        step(nc.vector.reciprocal(o_rden[:, i % 2, 0:n], src[:, :, HD]))
                        nc.vector.tensor_tensor(dst, src[:, :, 0:HD],
                                                o_rden[:, i % 2, 0:n].unsqueeze(2).broadcast_to((P, n, HD)),
                                                ALU.mult).then_inc(o_copied, 1)
                    if kind == "stats":
                        stats(b + 1)
                    if kind == "dot":
                        dot(b + 1)
                    if kind == "score":
                        score_row(b, b + 1)
                    if kind == "rank":
                        rank(b, b + 1, i)
                    if kind == "ht":
                        normed(b, b + 1, i)
                    if kind == "out":
                        slot, ready = pj(b, (kind, i))
                        dv.wait_ge(pj_ready, ready)
                        dv.wait_ge(xr_ready, b * TT + i + 1)
                        nc.vector.tensor_tensor(xr[:, i % 2, :], pj_bank[slot][:, :], xr[:, i % 2, :],
                                                ALU.add).then_inc(y_ready, 1)

        @block.tensor
        def _(pe):
            def product(out, lhs_hi, lhs_lo, rhs_hi, rhs_lo, start, stop):
                nc.tensor.matmul(out, lhs_hi, rhs_hi, start=start, stop=False)
                nc.tensor.matmul(out, lhs_lo, rhs_hi, start=False, stop=False)
                return nc.tensor.matmul(out, lhs_hi, rhs_lo, start=False, stop=stop)

            def pt_empty(b, key):
                if b is None:
                    if PT0[key] >= 2:
                        pe.wait_ge(ht_lo_ready, PT0[key] - 1)
                elif before_use(PT, key):
                    taken(pe, b, before_use(PT, key))
                else:
                    pe.wait_ge(ht_lo_ready, b * DC + DC)
                    pe.wait_ge(row_copied, b + 1)

            def pj_empty(b, key):
                if before_use(PROJ, key):
                    taken(pe, b, before_use(PROJ, key))
                else:
                    pe.wait_ge(y_ready, b * TT + 1)

            def transposed(b, n, c):
                slot, _ = pt(b, ("ht", c))
                if c == 0:
                    pe.wait_ge(h_ready, n * TT + TT)
                pt_empty(b, ("ht", c))
                for t in range(TT):
                    ins = nc.tensor.transpose(pt_bank[slot][:, P * t:P * t + P], xb[:, t, P * c:P * c + P], ident[:, :])
                ins.then_inc(pt_ready, 1)

            def score_rows(b, n):
                slot, _ = pt(b, ("score", 0))
                pe.wait_ge(score_ready, n + 1)
                pt_empty(b, ("score", 0))
                for t in range(TT):
                    ins = nc.tensor.transpose(pt_bank[slot][:, P * t:P * t + P],
                                              score[:, t:t + 1].broadcast_to((P, P)), ident[:, :])
                ins.then_inc(pt_ready, 1)

            pe.wait_ge(const_made, N_CONST)
            for c in range(DC):
                transposed(None, 0, c)
            score_rows(None, 0)
            with pe.Fori(0, B) as b:
                for kind, i in plan:
                    if kind == "v":
                        t, hw = divmod(i, 2)
                        slot, _ = pj(b, (kind, i))
                        if i == 0:
                            pe.wait_ge(ht_lo_ready, b * DC + DC)
                        if i < 2:
                            pe.wait_ge(split_lo, 1 + i)
                        pj_empty(b, (kind, i))
                        for c in range(DC):
                            ins = product(pj_bank[slot][:, :], ht_hi[:, c, P * t:P * t + P], ht_lo[:, c, P * t:P * t + P],
                                          w_hi["v"][:, c, 512 * hw:512 * hw + 512],
                                          w_lo["v"][:, c, 512 * hw:512 * hw + 512], c == 0, c == DC - 1)
                        ins.then_inc(pj_ready, 1)
                    if kind in ("q", "k"):
                        slot, _ = pj(b, (kind, i))
                        pe.wait_ge(split_lo, 4 if i < NPAIR // 2 else 6)
                        pj_empty(b, (kind, i))
                        for c in range(DC):
                            ins = product(pj_bank[slot][:, :], w_hi[kind][:, c, P * i:P * i + P],
                                          w_lo[kind][:, c, P * i:P * i + P], ht_hi[:, c, :], ht_lo[:, c, :],
                                          c == 0, c == DC - 1)
                        ins.then_inc(pj_ready, 1)
                    if kind == "s":
                        p, u = divmod(i, UNITS)
                        slot = i % 2
                        if u == 0:
                            pe.wait_ge(qk_lo, b * (2 * NPAIR) + 2 * p + 2)
                        if i >= 2:
                            pe.wait_ge(p_ready, b * NU + i - 1)
                        for h, t, c0, nk in unit_blocks(u):
                            queries, rows = slice(P * t, P * t + P), head_rows(h)
                            high = (q_both[:, p % 2, h, queries], k_twice[:, p % 2, h, 0:nk])
                            low = (q_both[rows, p % 2, h, queries], k_lo[rows, p % 2, 0:nk])
                            if u == UNITS - 1 and h == 0:
                                nc.tensor.matmul(s_bank[slot][:, c0:c0 + nk], *low, start=True, stop=False
                                                 ).then_inc(s_half, 1)
                                nc.tensor.matmul(s_bank[slot][:, c0:c0 + nk], *high, start=False, stop=False)
                            else:
                                nc.tensor.matmul(s_bank[slot][:, c0:c0 + nk], *high, start=True, stop=False)
                                if u == UNITS - 1:
                                    pe.wait_ge(s_half, b * NPAIR + p + 1)
                                nc.tensor.matmul(s_bank[slot][:, c0:c0 + nk], *low, start=False, stop=False)
                            ins = nc.tensor.matmul(s_bank[slot][:, c0 + nk - P:c0 + nk], ident_b[:, :], causal_b[:, :],
                                                   start=False, stop=True)
                        ins.then_inc(s_ready, 1)
                    if kind == "t":
                        slot, _ = pt(b, (kind, i))
                        pe.wait_ge(p_ready, b * NU + i + 1)
                        pt_empty(b, (kind, i))
                        for j in range(4):
                            ins = nc.tensor.transpose(pt_bank[slot][:, P * j:P * j + P], probs[:, i % 2, P * j:P * j + P],
                                                      ident[:, :])
                        ins.then_inc(pt_ready, 1)
                    if kind == "pv":
                        p, u = divmod(i, UNITS)
                        slot = i % 2
                        if i == 0:
                            pe.wait_ge(v_ready, b * (2 * TT) + 2 * TT)
                            pe.wait_ge(v_sum_ready, b + 1)
                        pe.wait_ge(ts_ready, b * NU + i + 1)
                        if i >= 2:
                            pe.wait_ge(o_copied, b * NU + i - 1)
                        for n, (h, t, c0, nk) in enumerate(unit_blocks(u)):
                            o0 = n * VW
                            for kt in range(nk // P):
                                ins = nc.tensor.matmul(o_bank[slot][:, o0:o0 + VW],
                                                       probs_t[:, i % 2, c0 + P * kt:c0 + P * kt + P],
                                                       vals[:, kt, 2 * p + h, :], start=(kt == 0), stop=(kt == nk // P - 1))
                        ins.then_inc(pv_ready, 1)
                    if kind == "ot":
                        slot, _ = pt(b, (kind, i))
                        pe.wait_ge(o_copied, b * NU + UNITS * (i + 1))
                        pt_empty(b, (kind, i))
                        for t in range(TT):
                            ins = nc.tensor.transpose(pt_bank[slot][:, P * t:P * t + P],
                                                      o_norm[:, i % 2, t, :, :].rearrange("p h d -> p (h d)"),
                                                      ident[:, :])
                        ins.then_inc(pt_ready, 1)
                    if kind == "score":
                        score_rows(b, b + 1)
                    if kind == "ht":
                        transposed(b, b + 1, i)
                    if kind == "out":
                        slot, _ = pj(b, (kind, i))
                        if i == 0:
                            pe.wait_ge(ot_ready, b * NPAIR + NPAIR)
                            pe.wait_ge(wo_in, 16)
                        pj_empty(b, (kind, i))
                        for c in range(NPAIR):
                            ins = nc.tensor.matmul(pj_bank[slot][:, :], o_t[:, c, P * i:P * i + P], w_o[:, c, :],
                                                   start=(c == 0), stop=(c == NPAIR - 1))
                        ins.then_inc(pj_ready, 1)


SK = 77
XH, XD = 16, 32
CH = P // XD
VX = XD + 1
FILL = -1e20
KEEP = 64
NSEL = B * KEEP
SLOTS = 2 * TT


class Batch:

    def __init__(self, j, k):
        self.j, self.k = j, k

    def ahead(self, off):
        return Batch(self.j, self.k + off)

    def count(self, per, more):
        if isinstance(self.j, int):
            return (2 * self.j + self.k) * per + more
        return self.j * (2 * per) + (self.k * per + more)

    @property
    def index(self):
        return self.count(1, 0)

    @property
    def par(self):
        return self.k % 2

    @property
    def had(self):
        return self.j + self.k // 2


def cross_plan():
    at = []
    for kind, lag in (("e", 0), ("e_take", 1), ("max", 2), ("t", 3), ("pv", 4), ("pv_take", 5)):
        at += [(kind, s, s + lag) for s in range(SLOTS)]
    at += [("turn", t, 2 * t - 1) for t in range(TT)] + [("xl", t, 2 * t - 2) for t in range(TT)]
    at += [("stats", 0, -3)] + [("ctx", i, i - 5) for i in range(4)]
    at += [("norm", t, 2 * t + 7) for t in range(TT)] + [("xl2", t, 2 * t + 8) for t in range(TT)]
    at += [("dot", t, 2 * t + 9) for t in range(TT)] + [("row", 0, 15), ("row_take", 0, 16)]
    at += [("rank", t, (16, 16, 17, 18)[t]) for t in range(TT)] + [("pick", 0, 18)]
    at += [("base", t, 19 + t // 2) for t in range(TT)] + [("xs", c, 19 + (c + 1) // 2) for c in range(DC)]
    at += [("a1", c, 21 + c // 2) for c in range(TT)] + [("xs_take", 0, 22), ("a1_take", 0, 23)]
    order = ("turn", "xl", "e_take", "pv_take", "t", "max", "xs_take", "norm", "xl2", "dot", "row_take",
             "rank", "pick", "e", "pv", "row", "ctx", "base", "xs", "a1", "a1_take", "stats")
    at.sort(key=lambda a: (a[2] % SLOTS, order.index(a[0]), a[1]))
    return [(kind, i, -(slot // SLOTS)) for kind, i, slot in at]


def cross_and_router(nc, x1, ctx_in, mask, wq, wk, wv, amask, pos, router_w, router_b, base,
                     xsel_t, info_t, picked, mask_rows, later):
    with ExitStack() as ctx:
        def sb(name, shape, dt=F32):
            return ctx.enter_context(nc.sbuf_tensor(name, shape, dt))

        def banks(name, n=1):
            return ctx.enter_context(nc.psum_tensor(name, [P, n, 512] if n > 1 else [P, 512], F32))

        def sem(name):
            return ctx.enter_context(nc.semaphore(name))

        xt = sb("xt", [P, 2, TT, D])
        x2 = sb("x2", [P, 2, TT, D])
        xl = sb("xl", [P, 2, D])
        xl_t = sb("xl_t", [P, 2, D])
        e = sb("e", [P, 4, 2 * CH, SK])
        fill = sb("fill", [P, 2, 2 * CH, SK])
        mk = sb("mk", [P, TT, SK])
        e_max = sb("e_max", [P, 2, 2 * CH])
        p_t = sb("p_t", [SK, 2, 2, 512])
        att_den = sb("att_den", [P, 2, 2 * CH])
        att = sb("att", [P, 2, 2 * CH, XD])
        cx = sb("cx", [SK, D])
        cx_t = sb("cx_t", [P, DC, SK])
        key_t = sb("key_t", [P, DC, SK])
        qk_bd = sb("qk_bd", [P, 2, DC, CH, SK])
        vx = sb("vx", [SK, 2, XH, VX])
        w_bd = sb("w_bd", [P, 3, P])
        wq_bt = sb("wq_bt", [P, P])
        ident = sb("x_ident", [P, P])
        rw = sb("rw", [P, D])
        rb = sb("rb", [P, 1])
        am = sb("am", [P, TT, S])
        pos_i = sb("pos_i", [P, TT], I32)
        xl2 = sb("xl2", [P, 2, TT, D])
        row_s = sb("x_row_s", [P, S])
        junk = sb("x_junk", [P, S], BF16)
        before = sb("x_before", [P, S + P * (TT - 1)], I8)
        slots = sb("slots", [P, KEEP])
        bn, mv = sb("x_bn", [P, 2, TT, 6]), sb("x_mv", [P, 2, TT, 2])
        half, minus, eps_ln = (sb(n, [P, TT]) for n in ("x_half", "x_minus", "x_eps"))
        idle_v, at_start = sb("idle_v", [P, 2]), sb("at_start", [P, 2 * TT])
        scales = sb("scales", [P, 2, 3, TT])
        RS, NM, NB = range(3)
        info = sb("info", [P, 2, TT, 3])
        cnt = sb("x_cnt", [P, 3, TT])
        stay = sb("stay", [P, TT])
        sel = sb("sel", [P, TT, KEEP])

        e_bank, pt_bank = banks("e_bank", 2), [banks(f"x_pt_bank{i}") for i in range(2)]
        o_bank, t_bank, r_bank = banks("x_o_bank"), banks("t_bank"), [banks(f"r_bank{i}") for i in range(2)]

        x_in = [[sem(f"x_in{p}{t}") for t in range(TT)] for p in range(2)]
        base_out = [[sem(f"base_out{p}{t}") for t in range(TT)] for p in range(2)]
        cx_in, am_in, pos_in, const_in, later_in = (
            sem(n) for n in ("cx_in", "am_in", "pos_in", "x_const_in", "later_in"))
        w_in, made, pool_step, dve_step = sem("w_in"), sem("x_made"), sem("x_pool_step"), sem("x_dve_step")
        wq_turned, wq_copied = sem("wq_turned"), sem("wq_copied")
        stats_ready, scales_ready, scales2_ready, xl_ready, turned, t_copied = (
            sem(n) for n in ("x_stats_ready", "scales_ready", "scales2_ready", "xl_ready", "turned", "t_copied"))
        e_ready, masked, fill_ready, filled, max_ready, shifted, p_ready = (
            sem(n) for n in ("e_ready", "masked", "fill_ready", "filled", "x_max_ready", "shifted", "x_p_ready"))
        pt_ready, pt_copied, pv_ready, att_ready, x2_ready = (
            sem(n) for n in ("x_pt_ready", "pt_copied", "x_pv_ready", "att_ready", "x2_ready"))
        stats2_ready, xl2_ready, info_ready, row_ready, row_copied, sel_ready = (
            sem(n) for n in ("stats2_ready", "xl2_ready", "info_ready", "row_ready", "x_row_copied", "sel_ready"))
        xs_ready, a1_ready, xs_copied, a1_copied, base_ready = (
            sem(n) for n in ("xs_ready", "a1_ready", "xs_copied", "a1_copied", "base_ready"))

        HALVES = 2 * TT
        x1_rows = x1.rearrange("b (t p) d -> b p t d", p=P)
        base_rows = base.rearrange("b (t p) d -> b p t d", p=P)
        N_MADE, CONST_IN, ROUNDS = 10, 16 * 3, (B - 2) // 2
        assert B == 2 * ROUNDS + 2 and amask.shape[0] <= 4

        def cols(i):
            return slice(256 * (i % 2), 256 * (i % 2) + 256)

        plan = cross_plan()
        in_t_bank = [p for p in plan if p[0] in ("ctx", "turn")]
        early = [p for p in in_t_bank if p[2] == 1]

        def t_count(kind, i, n):
            off = next(p[2] for p in plan if p[:2] == (kind, i))
            n = n.ahead(-off)
            if isinstance(n.j, int) and n.index < 0:
                return early.index((kind, i, off)) + 1
            return n.count(len(in_t_bank), len(early) + in_t_bank.index((kind, i, off)) + 1)

        def run(step, eng, tally=None, per=0):
            def period(n, least=-2, most=1):
                for kind, i, off in plan:
                    if least <= off <= most:
                        step(kind, i, n.ahead(off))

            period(Batch(0, -1), least=1)
            period(Batch(0, 0), least=0)
            period(Batch(0, 1), least=-1)
            with eng.Fori(0, ROUNDS) as j:
                if tally:
                    with tally.loop(j, per, ROUNDS):
                        period(Batch(j, 2))
                        period(Batch(j, 3))
                else:
                    period(Batch(j, 2))
                    period(Batch(j, 3))
            period(Batch(0, B), most=-1)
            period(Batch(0, B + 1), most=-2)

        def wait(eng, sem_, value):
            if not isinstance(value, int) or value > 0:
                eng.wait_ge(sem_, value)

        block = ctx.enter_context(nc.Block())

        @block.sync
        def _(sp):
            def load_x(n, source, tiles=range(TT)):
                for t in tiles:
                    wait(sp, x2_ready, n.count(HALVES, 2 * t + 2 - 2 * HALVES))
                    sp.dma_start(xt[:, n.par, t, :], x1_rows[source][:, t, :]).then_inc(x_in[n.par][t], 16)

            def load_context(n, source):
                if not isinstance(n.j, int) or n.index > 0:
                    sp.wait_ge(turned, t_count("ctx", 0, n.ahead(-1)))
                sp.dma_start(cx[:, :], ctx_in[source]).then_inc(cx_in, 16)

            def store(n, tiles=range(TT)):
                for t in tiles:
                    sp.wait_ge(base_ready, n.count(TT, t + 1))
                    sp.dma_start(base_rows[n.index][:, t, :], x2[:, n.par, t, :]).then_inc(base_out[n.par][t], 16)

            def load_router(n, m):
                wait(sp, info_ready, n.count(1, 0))
                with nc.allow_non_contiguous_dma(reason="512 numbers"):
                    sp.dma_start(pos_i[:, :], pos[m, 0:S].rearrange("(t p) -> p t", p=P)).then_inc(pos_in, 16)
                wait(sp, a1_ready, n.count(1, 0))
                sp.dma_start(am[:, :, :], amask[m, 0, 0:S, 0:S].rearrange("(t p) k -> p t k", p=P)).then_inc(am_in, 16)

            def period(n, m, source):
                load_context(n.ahead(1), source)
                load_x(n.ahead(1), source, range(TT - 1))
                store(n.ahead(-2), range(TT // 2))
                load_x(n.ahead(1), source, [TT - 1])
                store(n.ahead(-2), range(TT // 2, TT))
                load_router(n.ahead(-1), m)

            last_m = amask.shape[0] - 1
            load_x(Batch(0, 0), 0)
            sp.wait_ge(made, 1)
            for k, w in enumerate((wq, wk, wv)):
                for h in range(CH):
                    rows = slice(XD * h, XD * h + XD)
                    sp.dma_start(w_bd[rows, k, rows], w[:, :]).then_inc(w_in, 16)
            load_context(Batch(0, 0), 0)
            sp.dma_start(mk[:, :, :], mask[0, 0].rearrange("(t p) k -> p t k", p=P)).then_inc(const_in, 16)
            sp.dma_start(rw[:, :], router_w.rearrange("d o -> o d").broadcast_to((P, D))).then_inc(const_in, 16)
            sp.dma_start(rb[:, :], router_b.rearrange("(o d) -> o d", o=1).broadcast_to((P, 1))).then_inc(const_in, 16)
            load_x(Batch(0, 1), 1)
            load_context(Batch(0, 1), 1)
            load_router(Batch(0, 0), 0)
            load_context(Batch(0, 2), 2)
            load_x(Batch(0, 2), 2)
            for k in (2, 3):
                period(Batch(0, k), min(k - 1, last_m), k + 1)
            for dst, src in later:
                sp.dma_start(dst, src).then_inc(later_in, 16)
            with sp.Fori(1, ROUNDS - 1) as j:
                period(Batch(j, 2), last_m, Batch(j, 3).index)
                period(Batch(j, 3), last_m, Batch(j, 4).index)
            period(Batch(0, B - 2), last_m, B - 1)
            period(Batch(0, B - 1), last_m, 0)
            store(Batch(0, B - 2))
            load_router(Batch(0, B - 1), last_m)
            store(Batch(0, B - 1))
            for par in range(2):
                for t in range(TT):
                    sp.wait_ge(base_out[par][t], 16 * B // 2 + 1)
            sp.wait_ge(later_in, 16 * len(later))

        @block.gpsimd
        def _(pl):
            done = Tally(pool_step)
            nc.gpsimd.memset(w_bd[:, :, :], 0.0).then_inc(made, 1)
            done.mark(nc.gpsimd.memset(ident[:, :], 0.0))
            done.mark(nc.gpsimd.memset(before[:, :], 1.0))
            for tile, value in ((half, -0.5), (minus, -1.0), (eps_ln, EPS_LN)):
                nc.gpsimd.memset(tile[:, :], value).then_inc(made, 1)
            nc.gpsimd.memset(qk_bd[:, :, :, :, :], 0.0).then_inc(made, 1)
            nc.gpsimd.memset(vx[:, :, :, XD:VX], 1.0).then_inc(made, 1)
            nc.gpsimd.iota(slots[:, :], [[1, KEEP]], base=0, channel_multiplier=0,
                           allow_small_or_imprecise_dtypes=True).then_inc(made, 1)
            nc.gpsimd.iota(info[:, :, :, 2:3], [[0, 2], [P, TT]], base=0, channel_multiplier=1,
                           allow_small_or_imprecise_dtypes=True).then_inc(made, 1)
            done.wait(pl)
            nc.gpsimd.affine_select(out=ident[:, :], in_=ident[:, :], compare_op=ALU.not_equal, fill=1.0, base=0,
                                    pattern=[[-1, P]], channel_multiplier=1).then_inc(made, 1)
            nc.gpsimd.affine_select(out=before[:, :], in_=before[:, :], compare_op=ALU.is_gt, fill=0.0,
                                    base=P * (TT - 1), pattern=[[-1, S + P * (TT - 1)]],
                                    channel_multiplier=1).then_inc(made, 1)
            pl.wait_ge(made, N_MADE)

            def step(ins):
                done.mark(ins)
                done.wait(pl)

            def scale(r, tiles, ready):
                rs, nm, nb = (scales[:, r, k, tiles] for k in (RS, NM, NB))
                step(nc.gpsimd.tensor_tensor(rs, mv[:, r, tiles, 1], eps_ln[:, tiles], ALU.add))
                step(nc.gpsimd.tensor_tensor(rs, rs, half[:, tiles], ALU.pow))
                step(nc.gpsimd.tensor_tensor(nm, minus[:, tiles], mv[:, r, tiles, 0], ALU.mult))
                nc.gpsimd.tensor_tensor(nb, nm, rs, ALU.mult).then_inc(ready, 1)

            def work(kind, i, n):
                if kind == "stats":
                    pl.wait_ge(stats_ready, n.count(1, 1))
                    scale(0, slice(0, TT), scales_ready)
                if kind == "e_take":
                    pl.wait_ge(fill_ready, n.count(HALVES, i + 1))
                    nc.gpsimd.tensor_tensor(e[:, i % 4], e[:, i % 4], fill[:, i % 2], ALU.add).then_inc(filled, 1)
                if kind == "max":
                    pl.wait_ge(max_ready, n.count(HALVES, i + 1))
                    nc.gpsimd.tensor_tensor(e[:, i % 4], e[:, i % 4],
                                            e_max[:, i % 2].unsqueeze(2).broadcast_to((P, 2 * CH, SK)),
                                            ALU.add).then_inc(shifted, 1)
                if kind == "pv_take":
                    pl.wait_ge(att_ready, n.count(HALVES, i + 1))
                    pl.wait_ge(base_out[n.par][i // 2], n.had * 16 + 1)
                    nc.gpsimd.tensor_tensor(x2[:, n.par, i // 2, cols(i)], xt[:, n.par, i // 2, cols(i)],
                                            att[:, i % 2].rearrange("p h d -> p (h d)"), ALU.add).then_inc(x2_ready, 1)
                if kind == "norm":
                    pl.wait_ge(stats2_ready, n.count(TT, i + 1))
                    scale(1, slice(i, i + 1), scales2_ready)

            run(work, pl, done, 2 * 3 * (1 + TT))

        @block.scalar
        def _(act):
            act.wait_ge(wq_turned, 1)
            nc.scalar.copy(wq_bt[:, :], t_bank[:, 0:P]).then_inc(wq_copied, 1)
            act.wait_ge(made, N_MADE)

            def work(kind, i, n):
                if kind == "ctx":
                    act.wait_ge(turned, t_count(kind, i, n))
                    chunks = t_bank[:, 0:DC * SK].rearrange("p (c k) -> p c k", c=DC)
                    if i == 0:
                        ins = nc.scalar.copy(cx_t[:, :, :], chunks)
                    elif i == 1:
                        ins = nc.scalar.copy(key_t[:, :, :], chunks)
                    elif i == 2:
                        for h in range(CH):
                            rows = slice(XD * h, XD * h + XD)
                            ins = nc.scalar.copy(qk_bd[rows, n.par, :, h, :], chunks[rows])
                    else:
                        ins = nc.scalar.copy(vx[:, n.par, :, 0:XD], t_bank[0:SK, :].rearrange("p (h d) -> p h d", d=XD))
                    ins.then_inc(t_copied, 1)
                if kind == "xl":
                    act.wait_ge(scales_ready, n.count(1, 1))
                    if i >= 2:
                        act.wait_ge(turned, t_count("turn", i - 2, n))
                    elif not isinstance(n.j, int) or n.index > 0:
                        act.wait_ge(turned, t_count("turn", i + 2, n.ahead(-1)))
                    nc.scalar.activation(xl[:, i % 2, :], xt[:, n.par, i, :], ACT.Identity,
                                         bias=scales[:, 0, NB, i:i + 1], scale=scales[:, 0, RS, i:i + 1]
                                         ).then_inc(xl_ready, 1)
                if kind == "turn":
                    act.wait_ge(turned, t_count(kind, i, n))
                    wait(act, e_ready, n.count(HALVES, 2 * i - 2))
                    nc.scalar.copy(xl_t[:, i % 2, :], t_bank[:, :]).then_inc(t_copied, 1)
                if kind == "max":
                    act.wait_ge(shifted, n.count(HALVES, i + 1))
                    nc.scalar.activation(e[:, i % 4], e[:, i % 4], ACT.Exp).then_inc(p_ready, 1)
                if kind == "t":
                    act.wait_ge(pt_ready, n.count(HALVES, i + 1))
                    wait(act, pv_ready, n.count(HALVES, i - 1))
                    for h in range(2):
                        ins = nc.scalar.copy(p_t[:, i % 2, h, :], pt_bank[h][0:SK, :])
                    ins.then_inc(pt_copied, 1)
                if kind == "xl2":
                    act.wait_ge(scales2_ready, n.count(TT, i + 1))
                    nc.scalar.activation(xl2[:, n.par, i, :], x2[:, n.par, i, :], ACT.Identity,
                                         bias=scales[:, 1, NB, i:i + 1], scale=scales[:, 1, RS, i:i + 1]
                                         ).then_inc(xl2_ready, 1)

            run(work, act)

        @block.vector
        def _(dv):
            done = Tally(dve_step)

            def step(ins):
                done.mark(ins)
                done.wait(dv)

            def aggregate(r, tiles, ready):
                done.wait(dv)
                nc.vector.memset(idle_v[:, r:r + 1], 0.0)
                for t in tiles:
                    ins = nc.vector.bn_aggr(mv[:, r, t, :], bn[:, r, t, :])
                ins.then_inc(ready, 1)

            def work(kind, i, n):
                if kind == "stats":
                    wait(dv, xl_ready, n.count(TT, 0))
                    for t in range(TT):
                        dv.wait_ge(x_in[n.par][t], n.had * 16 + 16)
                        done.mark(nc.vector.bn_stats(bn[:, 0, t, :], xt[:, n.par, t, :]))
                    aggregate(0, range(TT), stats_ready)
                if kind == "e_take":
                    four = (P, 2, CH, SK)
                    if isinstance(n.j, int) and n.index == i == 0:
                        dv.wait_ge(made, N_MADE)
                        dv.wait_ge(const_in, CONST_IN)
                    dv.wait_ge(e_ready, n.count(HALVES, i + 1))
                    wait(dv, pt_ready, n.count(HALVES, i - 3))
                    nc.vector.tensor_tensor(e[:, i % 4].rearrange("p (c h) k -> p c h k", c=2),
                                            e_bank[:, :, 0:CH * SK].rearrange("p c (h k) -> p c h k", h=CH),
                                            mk[:, i // 2, :].unsqueeze(1).unsqueeze(1).broadcast_to(four),
                                            ALU.mult).then_inc(masked, 1)
                    dv.wait_ge(masked, n.count(HALVES, i + 1))
                    wait(dv, filled, n.count(HALVES, i - 1))
                    nc.vector.tensor_scalar(fill[:, i % 2], e[:, i % 4], 0.0, FILL, ALU.is_equal,
                                            ALU.mult).then_inc(fill_ready, 1)
                if kind == "max":
                    dv.wait_ge(filled, n.count(HALVES, i + 1))
                    wait(dv, shifted, n.count(HALVES, i - 1))
                    nc.vector.tensor_reduce(e_max[:, i % 2], e[:, i % 4], AX.X, ALU.max,
                                            negate=True).then_inc(max_ready, 1)
                if kind == "pv_take":
                    dv.wait_ge(pv_ready, n.count(HALVES, i + 1))
                    o = o_bank[:, 0:2 * CH * VX].rearrange("p (h v) -> p h v", v=VX)
                    step(nc.vector.reciprocal(att_den[:, i % 2], o[:, :, XD]))
                    wait(dv, x2_ready, n.count(HALVES, i - 1))
                    nc.vector.tensor_tensor(att[:, i % 2], o[:, :, 0:XD],
                                            att_den[:, i % 2].unsqueeze(2).broadcast_to((P, 2 * CH, XD)),
                                            ALU.mult).then_inc(att_ready, 1)

                batch = bass.ts(n.index, KEEP)
                if kind == "norm":
                    dv.wait_ge(x2_ready, n.count(HALVES, 2 * i + 2))
                    done.mark(nc.vector.bn_stats(bn[:, 1, i, :], x2[:, n.par, i, :]))
                    aggregate(1, [i], stats2_ready)
                if kind == "dot":
                    weights = info[:, n.par, :, 0]
                    dv.wait_ge(xl2_ready, n.count(TT, i + 1))
                    done.wait(dv)
                    done.mark(nc.vector.tensor_tensor_reduce(junk[:, :], xl2[:, n.par, i, :], rw[:, :], 1.0, 0.0,
                                                             ALU.mult, ALU.add, info[:, n.par, i, 0:1]))
                    if i == TT - 1:
                        done.wait(dv)
                        step(nc.vector.tensor_scalar(weights, weights, rb[:, 0:1], None, ALU.add))
                        dv.wait_ge(pos_in, n.count(16, 16))
                        nc.vector.tensor_copy(info[:, n.par, :, 1], pos_i[:, :]).then_inc(info_ready, 1)
                if kind == "row_take":
                    dv.wait_ge(row_ready, n.count(1, 1))
                    nc.vector.tensor_copy(row_s[:, :], r_bank[1][:, :]).then_inc(row_copied, 1)
                    dv.wait_ge(row_copied, n.count(1, 1))
                if kind == "rank":
                    w = info[:, n.par, i, 0:1]
                    done.wait(dv)
                    y0 = P * (TT - 1 - i)
                    step(nc.vector.tensor_scalar(junk[:, :], row_s[:, :], w, None, ALU.is_gt, ALU.add,
                                                 accum_out=cnt[:, 0, i:i + 1]))
                    step(nc.vector.scalar_tensor_tensor(junk[:, :], row_s[:, :], w, before[:, y0:y0 + S],
                                                        ALU.is_equal, ALU.mult, accum_out=cnt[:, 1, i:i + 1]))
                    step(nc.vector.tensor_scalar(junk[:, :], row_s[:, :], w, None, ALU.is_ge, ALU.add,
                                                 accum_out=cnt[:, 2, i:i + 1]))
                if kind == "pick":
                    step(nc.vector.tensor_tensor(cnt[:, 0, :], cnt[:, 0, :], cnt[:, 1, :], ALU.add))
                    step(nc.vector.tensor_scalar(stay[:, :], cnt[:, 2, :], KEEP - 0.5, None, ALU.is_gt))
                    for t in range(TT):
                        ins = nc.vector.tensor_scalar(sel[:, t, :], slots[:, :], cnt[:, 0, t:t + 1], None, ALU.is_equal)
                    ins.then_inc(sel_ready, 1)
                    dv.wait_ge(sel_ready, n.count(1, 1))
                    nc.vector.tensor_scalar(picked[:, :, batch], sel[:, :, :], 1.0, None, ALU.mult)
                if kind == "xs_take":
                    dv.wait_ge(xs_ready, n.count(1, 1))
                    nc.vector.tensor_scalar(xsel_t[:, :, batch],
                                            r_bank[1][:, 0:DC * KEEP].rearrange("p (c s) -> p c s", c=DC), 1.0, None,
                                            ALU.mult)
                    nc.vector.tensor_scalar(info_t[0:3, batch], r_bank[1][0:3, DC * KEEP:DC * KEEP + KEEP], 1.0, None,
                                            ALU.mult).then_inc(xs_copied, 1)
                if kind == "a1_take":
                    dv.wait_ge(a1_ready, n.count(1, 1))
                    nc.vector.tensor_scalar(mask_rows[:, :, batch],
                                            r_bank[0][:, 0:TT * KEEP].rearrange("p (c s) -> p c s", c=TT), 1.0, None,
                                            ALU.mult).then_inc(a1_copied, 1)
                if kind == "base":
                    rows = x2[:, n.par, i, :]
                    nc.vector.scalar_tensor_tensor(rows, xl2[:, n.par, i, :], stay[:, i:i + 1], rows, ALU.mult,
                                                   ALU.add).then_inc(base_ready, 1)

            for k, at_one in enumerate((*base_out[0], *base_out[1])):
                nc.vector.memset(at_start[:, k:k + 1], 0.0).then_inc(at_one, 1)
            run(work, dv, done, 2 * (TT + HALVES + TT + TT + 1 + 3 * TT + 2))

        @block.tensor
        def _(pe):
            pe.wait_ge(made, N_MADE)
            pe.wait_ge(w_in, 16 * 3 * CH)
            nc.tensor.transpose(t_bank[:, 0:P], w_bd[:, 0, :], ident[:, :]).then_inc(wq_turned, 1)
            pe.wait_ge(wq_copied, 1)

            def work(kind, i, n):
                if kind == "ctx":
                    if i == 0:
                        pe.wait_ge(cx_in, n.count(16, 16))
                    wait(pe, t_copied, t_count(kind, i, n) - 1)
                    if i == 0:
                        for c in range(DC):
                            ins = nc.tensor.transpose(t_bank[:, SK * c:SK * c + SK], cx[:, P * c:P * c + P],
                                                      ident[0:SK, 0:SK])
                    elif i == 1:
                        ins = nc.tensor.matmul(t_bank[:, 0:DC * SK], w_bd[:, 1, :],
                                               cx_t[:, :, :].rearrange("p c k -> p (c k)"), start=True, stop=True)
                    elif i == 2:
                        ins = nc.tensor.matmul(t_bank[:, 0:DC * SK], wq_bt[:, :],
                                               key_t[:, :, :].rearrange("p c k -> p (c k)"), start=True, stop=True)
                    else:
                        for c in range(DC):
                            ins = nc.tensor.matmul(t_bank[0:SK, P * c:P * c + P], cx_t[:, c, :], w_bd[:, 2, :],
                                                   start=True, stop=True)
                    ins.then_inc(turned, 1)
                if kind == "turn":
                    pe.wait_ge(xl_ready, n.count(TT, i + 1))
                    pe.wait_ge(t_copied, t_count(kind, i, n) - 1)
                    for c in range(DC):
                        ins = nc.tensor.transpose(t_bank[:, P * c:P * c + P], xl[:, i % 2, P * c:P * c + P], ident[:, :])
                    ins.then_inc(turned, 1)
                if kind == "e":
                    pe.wait_ge(t_copied, t_count("turn", i // 2, n))
                    wait(pe, masked, n.count(HALVES, i))
                    for c in range(2):
                        k = 2 * (i % 2) + c
                        ins = nc.tensor.matmul(e_bank[:, c, 0:CH * SK], xl_t[:, (i // 2) % 2, P * k:P * k + P],
                                               qk_bd[:, n.par, k].rearrange("p h k -> p (h k)"), start=True, stop=True)
                    ins.then_inc(e_ready, 1)
                if kind == "t":
                    pe.wait_ge(p_ready, n.count(HALVES, i + 1))
                    wait(pe, pt_copied, n.count(HALVES, i))
                    for h in range(2 * CH):
                        ins = nc.tensor.transpose(pt_bank[h // CH][0:SK, P * (h % CH):P * (h % CH) + P],
                                                  e[:, i % 4, h, :], ident[:, :])
                    ins.then_inc(pt_ready, 1)
                if kind == "pv":
                    pe.wait_ge(pt_copied, n.count(HALVES, i + 1))
                    wait(pe, att_ready, n.count(HALVES, i))
                    for h in range(2 * CH):
                        ins = nc.tensor.matmul(o_bank[:, VX * h:VX * h + VX],
                                               p_t[:, i % 2, h // CH, P * (h % CH):P * (h % CH) + P],
                                               vx[:, n.par, 2 * CH * (i % 2) + h, :], start=True, stop=True)
                    ins.then_inc(pv_ready, 1)

                if kind == "row":
                    pe.wait_ge(info_ready, n.count(1, 1))
                    for t in range(TT):
                        ins = nc.tensor.transpose(r_bank[1][:, P * t:P * t + P],
                                                  info[:, n.par, t, 0:1].broadcast_to((P, P)), ident[:, :])
                    ins.then_inc(row_ready, 1)
                if kind == "xs":
                    if i == 0:
                        pe.wait_ge(sel_ready, n.count(1, 1))
                    for t in range(TT):
                        ins = nc.tensor.matmul(r_bank[1][:, KEEP * i:KEEP * i + KEEP],
                                               xl2[:, n.par, t, P * i:P * i + P], sel[:, t, :], start=(t == 0),
                                               stop=(t == TT - 1))
                    if i == DC - 1:
                        for t in range(TT):
                            ins = nc.tensor.matmul(r_bank[1][0:3, DC * KEEP:DC * KEEP + KEEP],
                                                   info[:, n.par, t, :], sel[:, t, :], start=(t == 0),
                                                   stop=(t == TT - 1))
                        ins.then_inc(xs_ready, 1)
                if kind == "a1":
                    if i == 0:
                        pe.wait_ge(am_in, n.count(16, 16))
                    for t in range(TT):
                        ins = nc.tensor.matmul(r_bank[0][:, KEEP * i:KEEP * i + KEEP], am[:, t, P * i:P * i + P],
                                               sel[:, t, :], start=(t == 0), stop=(t == TT - 1))
                    if i == TT - 1:
                        ins.then_inc(a1_ready, 1)

            run(work, pe)


FH, FD = 16, 32
FF = 2048
FC = FF // P
FV = FD + 1
ROPE_BASE = 10000.0
TURN = 2 * np.pi
TURN_PARTS = (6.28125, 1.93500518798828125e-3, 3.0199159795074593e-7)
ROUNDING = 1.5 * 2.0 ** 23
HALF_TURN = float(np.nextafter(np.float32(np.pi), np.float32(0)))
NT = NSEL // P


def routed_plan():
    plan = [("info", 0), ("mask", 0)] + [("xs", t) for t in range(NT)]
    plan += [(k, 0) for k in ("q", "k", "v", "tq", "tk")] + [(k, 1) for k in ("q", "k", "v")]
    units = NT * DC
    for s in range(units + 8):
        if s < units:
            plan.append(("s", s))
            t, c = divmod(s, DC)
            if c == 0 and 1 <= t < NT - 1:
                plan += [(k, t + 1) for k in ("q", "k")]
            if c == 1 and t + 1 < NT:
                plan += [("tq", t + 1), ("tk", t + 1)]
            if c == 2 and 1 <= t < NT - 1:
                plan.append(("v", t + 1))
        if 1 <= s < units + 1:
            plan.append(("t", s - 1))
        if 2 <= s < units + 2:
            plan.append(("pv", s - 2))
        if s >= DC + 2 and (s - DC - 2) % DC == 0 and (s - DC - 2) // DC < NT:
            plan.append(("ot", (s - DC - 2) // DC))
        if s >= DC + 3 and (s - DC - 3) % DC == 0 and (s - DC - 3) // DC < NT:
            plan.append(("wo", (s - DC - 3) // DC))
        if s >= DC + 5 and (s - DC - 5) % DC == 0 and (s - DC - 5) // DC < NT:
            plan.append(("th", (s - DC - 5) // DC))
    plan += [("th", t) for t in range(NT) if ("th", t) not in plan]
    return plan + [("w1", f) for f in range(FC)] + [("w2", t) for t in range(NT)]


def routed_block(nc, xsel_t, info_t, picked, mask_rows, w4, ln1, ln2, w1, w2, out):
    plan = routed_plan()
    RINGS = {}
    for name, kinds in (("big", ("q", "k", "v", "wo", "w1", "w2")), ("turn", ("xs", "tq", "tk", "t", "ot", "th")),
                        ("score", ("s",)), ("small", ("info", "mask", "pv"))):
        keys = [s for s in plan if s[0] in kinds]
        for n, key in enumerate(keys):
            RINGS[key] = (name, n % 2, keys[n - 2] if n >= 2 else None)
    KINDS = sorted({s[0] for s in plan})
    with ExitStack() as ctx:
        def sb(name, shape, dt=F32):
            return ctx.enter_context(nc.sbuf_tensor(name, shape, dt))

        def sem(name):
            return ctx.enter_context(nc.semaphore(name))

        w1_sb, w2_sb = sb("w1_sb", [P, DC, FF]), sb("w2_sb", [P, FC, D])
        xs = sb("xs", [P, NT, D])
        x1f = sb("x1f", [P, NT, D])
        h_t = xsel_t
        h2_t = mask_rows
        g_t = w4
        rot, rot_b = sb("rot", [P, 2, D]), sb("rot_b", [P, 2, D])
        q_t = sb("q_t", [P, 2, DC, P])
        k_bd = sb("k_bd", [P, 2, DC, CH, P])
        v_sb = sb("v_sb", [P, 2, FH, FV])
        e = sb("f_e", [P, 2, CH, P])
        p_t = sb("f_p_t", [P, 2, CH, P])
        o_n = sb("f_o_n", [P, 2, D])
        o_t = sb("f_o_t", [P, 2, DC, P])
        hn = sb("hn", [P, 2, D])
        m_full = sb("m_full", [P, NT, P])
        m_slot = sb("m_slot", [P, P])
        fin = picked
        junk = sb("f_junk", [P, D], BF16)
        ident = sb("f_ident", [P, P])
        l1, l2 = sb("l1", [P, DC]), sb("l2", [P, DC])
        info = sb("f_info", [P, NT, 3])
        idx = sb("idx", [P, NT], U32)
        first_row, live, inv = sb("first_row", [P, NT]), sb("live", [P, 1]), sb("inv", [P, FD // 2])
        half = sb("f_half", [P, NT])
        w_sel = sb("w_sel", [P, NT])
        ang, turns, sc = sb("ang", [P, NT, 16]), sb("turns", [P, 2, NT, 16]), sb("sc", [P, 2, NT, 16])
        minus_sin = sb("minus_sin", [P, NT, 16])
        ss, ss2 = sb("ss", [P, NT]), sb("ss2", [P, NT])
        r1, rq, r2 = sb("r1", [P, 2, NT]), sb("rq", [P, NT]), sb("r2", [P, 2, NT])
        nmax, den = sb("f_nmax", [P, 2, CH]), sb("f_den", [P, 2, CH])

        banks = {n: [ctx.enter_context(nc.psum_tensor(f"{n}_bank{i}", [P, 512], F32)) for i in range(2)]
                 for n in ("big", "turn", "score", "small")}
        made = {k: sem(f"{k}_made") for k in KINDS}
        read = {k: sem(f"{k}_read") for k in KINDS}
        w1_in, w2_in, ln_in, idx_ready, rows_in, out_done = (
            sem(n) for n in ("w1_in", "w2_in", "ln_in", "idx_ready", "rows_in", "out_done"))
        ident_made, const_made, pool_step, dve_step = (
            sem(n) for n in ("f_ident_made", "f_const_made", "f_pool_step", "f_dve_step"))
        ht_ready, angles_ready, sincos_ready, ss_ready, r1_ready = (
            sem(n) for n in ("ht_ready", "angles_ready", "sincos_ready", "ss_ready", "r1_ready"))
        rot_ready, fmax_ready, exp_ready, ss2_ready, hn_ready, fin_ready = (
            sem(n) for n in ("rot_ready", "fmax_ready", "exp_ready", "ss2_ready", "hn_ready", "fin_ready"))

        def bank(key):
            name, slot, _ = RINGS[key]
            return banks[name][slot]

        out_rows = out.rearrange("b s d -> (b s) d")
        block = ctx.enter_context(nc.Block())

        @block.sync
        def _(sp):
            with nc.allow_non_contiguous_dma(reason="one column per chunk"):
                for dst, src in ((l1, ln1), (l2, ln2)):
                    sp.dma_start(dst[:, :], src.rearrange("(c p) -> p c", p=P)).then_inc(ln_in, 16)
            sp.dma_start(w1_sb[:, :, :], w1.rearrange("(c p) f -> p c f", p=P)).then_inc(w1_in, 16)
            sp.dma_start(w2_sb[:, :, :], w2.rearrange("(c p) d -> p c d", p=P)).then_inc(w2_in, 16)

        @block.gpsimd
        def _(pl):
            done = Tally(pool_step)

            def step(ins):
                done.mark(ins)
                done.wait(pl)

            step(nc.gpsimd.memset(ident[:, :], 0.0))
            nc.gpsimd.affine_select(out=ident[:, :], in_=ident[:, :], compare_op=ALU.not_equal, fill=1.0, base=0,
                                    pattern=[[-1, P]], channel_multiplier=1).then_inc(ident_made, 1)
            pl.wait_ge(ident_made, 1)
            for t in range(NT):
                for b in range(2):
                    step(nc.gpsimd.memset(first_row[KEEP * b:KEEP * b + KEEP, t:t + 1], float(S * (2 * t + b))))
            step(nc.gpsimd.memset(half[:, :], -0.5))
            for j in range(FD // 2):
                step(nc.gpsimd.memset(inv[:, j:j + 1], float(np.float32(1.0) / np.float32(ROPE_BASE)
                                                           ** np.float32(2 * j / FD))))
            step(nc.gpsimd.memset(m_slot[:, :], 0.0))
            step(nc.gpsimd.memset(m_slot[0:KEEP, KEEP:P], NEG))
            step(nc.gpsimd.memset(m_slot[KEEP:P, 0:KEEP], NEG))
            step(nc.gpsimd.memset(m_slot[:, KEEP - 1:KEEP], NEG))
            step(nc.gpsimd.memset(m_slot[:, P - 1:P], NEG))
            step(nc.gpsimd.memset(live[:, :], 1.0))
            for last in (KEEP - 1, P - 1):
                step(nc.gpsimd.affine_select(out=live[:, :], in_=live[:, :], compare_op=ALU.not_equal, fill=0.0,
                                             base=-last, pattern=[[0, 1]], channel_multiplier=1))
            step(nc.gpsimd.memset(v_sb[:, :, :, FD:FV], 1.0))
            nc.gpsimd.memset(k_bd[:, :, :, :, :], 0.0).then_inc(const_made, 1)
            pl.wait_ge(made["mask"], 1)
            pl.wait_ge(idx_ready, 1)
            for t in range(NT):
                nc.gpsimd.indirect_dma_start(fin[:, t, :], None, out_rows,
                                             IndirectOffsetOnAxis(ap=idx[:, t:t + 1], axis=0)).then_inc(rows_in, 16)
            pl.wait_ge(ss_ready, NT)
            step(nc.gpsimd.tensor_scalar(r1[:, 0], ss[:, :], 1.0 / D, EPS_RMS, ALU.mult, ALU.add))
            step(nc.gpsimd.tensor_tensor(r1[:, 1], r1[:, 0], half[:, :], ALU.pow))
            nc.gpsimd.tensor_scalar(rq[:, :], r1[:, 1], FD ** -0.5, 1.0, ALU.mult, ALU.mult).then_inc(r1_ready, 1)
            for t in range(NT):
                pl.wait_ge(ss2_ready, t + 1)
                step(nc.gpsimd.tensor_scalar(r2[:, 0, t:t + 1], ss2[:, t:t + 1], 1.0 / D, EPS_RMS, ALU.mult, ALU.add))
                step(nc.gpsimd.tensor_tensor(r2[:, 1, t:t + 1], r2[:, 0, t:t + 1], half[:, 0:1], ALU.pow))
                if t >= 2:
                    pl.wait_ge(made["th"], t - 1)
                nc.gpsimd.tensor_scalar(hn[:, t % 2, :], x1f[:, t, :], r2[:, 1, t:t + 1], 1.0, ALU.mult,
                                        ALU.mult).then_inc(hn_ready, 1)
            for t in range(NT):
                pl.wait_ge(fin_ready, t + 1)
                nc.gpsimd.indirect_dma_start(out_rows, IndirectOffsetOnAxis(ap=idx[:, t:t + 1], axis=0),
                                             fin[:, t, :], None).then_inc(out_done, 16)
            pl.wait_ge(out_done, 16 * NT)

        @block.scalar
        def _(act):
            for kind, i in plan:
                if kind == "xs":
                    act.wait_ge(made[kind], i + 1)
                    nc.scalar.copy(xs[:, i, :], bank((kind, i))[:, :]).then_inc(read[kind], 1)
                    if i == NT - 1:
                        act.wait_ge(ln_in, 32)
                        for n in range(DC):
                            nc.scalar.activation(h_t[:, n, :], h_t[:, n, :], ACT.Copy,
                                                 scale=l1[:, n:n + 1]).then_inc(ht_ready, 1)
                        act.wait_ge(angles_ready, 1)
                        nc.scalar.activation(sc[:, :, :, :], turns[:, :, :, :], ACT.Sin).then_inc(sincos_ready, 1)
                if kind == "v":
                    act.wait_ge(made[kind], i + 1)
                    act.wait_ge(r1_ready, 1)
                    act.wait_ge(const_made, 1)
                    if i >= 2:
                        act.wait_ge(made["pv"], DC * (i - 1))
                    nc.scalar.activation(v_sb[:, i % 2, :, 0:FD], bank((kind, i))[:, :].rearrange("p (h d) -> p h d", d=FD),
                                         ACT.Copy, scale=r1[:, 1, i:i + 1]).then_inc(read[kind], 1)
                if kind == "tq":
                    act.wait_ge(made[kind], i + 1)
                    if i >= 2:
                        act.wait_ge(made["s"], DC * (i - 1))
                    nc.scalar.copy(q_t[:, i % 2].rearrange("p c k -> p (c k)"), bank((kind, i))[:, :]).then_inc(read[kind], 1)
                if kind == "tk":
                    act.wait_ge(made[kind], i + 1)
                    for h in range(CH):
                        rows = slice(FD * h, FD * h + FD)
                        ins = nc.scalar.copy(k_bd[rows, i % 2, :, h, :],
                                             bank((kind, i))[rows, :].rearrange("p (c k) -> p c k", c=DC))
                    ins.then_inc(read[kind], 1)
                if kind == "s":
                    act.wait_ge(fmax_ready, i + 1)
                    for h in range(CH):
                        ins = nc.scalar.activation(e[:, i % 2, h, :], e[:, i % 2, h, :], ACT.Exp,
                                                   bias=nmax[:, i % 2, h:h + 1])
                    ins.then_inc(exp_ready, 1)
                if kind == "ot":
                    act.wait_ge(made[kind], i + 1)
                    if i >= 2:
                        act.wait_ge(made["wo"], i - 1)
                    nc.scalar.copy(o_t[:, i % 2].rearrange("p c k -> p (c k)"), bank((kind, i))[:, :]).then_inc(read[kind], 1)
                if kind == "w1":
                    act.wait_ge(made[kind], i + 1)
                    if i == 0:
                        act.wait_ge(made["wo"], NT)
                    nc.scalar.activation(g_t[:, i // DC, i % DC, :], bank((kind, i))[:, :],
                                         ACT.Gelu_apprx_tanh).then_inc(read[kind], 1)

        @block.vector
        def _(dv):
            done = Tally(dve_step)

            def step(ins):
                done.mark(ins)
                done.wait(dv)

            dv.wait_ge(const_made, 1)
            for kind, i in plan:
                t, c = divmod(i, DC) if kind in ("s", "t", "pv") else (i, 0)
                if kind in ("info", "mask", "q", "k", "t", "pv", "wo", "th", "w2", "s"):
                    dv.wait_ge(made[kind], i + 1)
                if kind == "info":
                    nc.vector.tensor_copy(info[:, :, :], bank((kind, i))[:, 0:3 * NT].rearrange("p (t k) -> p t k", k=3)
                                          ).then_inc(read[kind], 1)
                    dv.wait_ge(read[kind], 1)
                    nc.vector.tensor_tensor(idx[:, :], info[:, :, 2], first_row[:, :], ALU.add).then_inc(idx_ready, 1)
                    nc.vector.tensor_scalar(w_sel[:, :], info[:, :, 0], live[:, 0:1], None, ALU.mult)
                    shape = (P, NT, FD // 2)
                    step(nc.vector.tensor_tensor(ang[:, :, :], info[:, :, 1].unsqueeze(2).broadcast_to(shape),
                                                 inv[:, :].unsqueeze(1).broadcast_to(shape), ALU.mult))
                    for n in range(2):
                        step(nc.vector.tensor_scalar(sc[:, n], ang[:, :, :], 1 / TURN, 0.25 * n, ALU.mult, ALU.add))
                        step(nc.vector.tensor_scalar(sc[:, n], sc[:, n], ROUNDING, None, ALU.add))
                        step(nc.vector.tensor_scalar(sc[:, n], sc[:, n], -ROUNDING, None, ALU.add))
                        src = ang[:, :, :]
                        for part in TURN_PARTS:
                            step(nc.vector.scalar_tensor_tensor(turns[:, n], sc[:, n], -part, src, ALU.mult, ALU.add))
                            src = turns[:, n]
                        if n:
                            step(nc.vector.tensor_scalar(turns[:, n], turns[:, n], TURN / 4, None, ALU.add))
                        ins = nc.vector.tensor_scalar(turns[:, n], turns[:, n], HALF_TURN, -HALF_TURN, ALU.min, ALU.max)
                    ins.then_inc(angles_ready, 1)
                if kind == "mask":
                    nc.vector.tensor_tensor(m_full[:, :, :], bank((kind, i))[:, :].rearrange("p (t k) -> p t k", t=NT),
                                            m_slot[:, :].unsqueeze(1).broadcast_to((P, NT, P)), ALU.add
                                            ).then_inc(read[kind], 1)
                if kind == "xs":
                    dv.wait_ge(read["xs"], i + 1)
                    nc.vector.tensor_tensor_reduce(junk[:, :], xs[:, i, :], xs[:, i, :], 1.0, 0.0, ALU.mult, ALU.add,
                                                   ss[:, i:i + 1]).then_inc(ss_ready, 1)
                    dv.wait_ge(ss_ready, i + 1)
                    if i == NT - 1:
                        dv.wait_ge(sincos_ready, 1)
                        step(nc.vector.tensor_scalar(minus_sin[:, :, :], sc[:, 0], -1.0, None, ALU.mult))
                        dv.wait_ge(r1_ready, 1)
                if kind in ("q", "k"):
                    n = 2 * t + (kind == "k")
                    scale = rq[:, t:t + 1] if kind == "q" else r1[:, 1, t:t + 1]
                    b4 = bank((kind, i))[:, :].rearrange("p (h m j) -> p h m j", h=FH, m=2)
                    r4 = rot_b[:, n % 2, :].rearrange("p (h m j) -> p h m j", h=FH, m=2)
                    if n >= 2:
                        dv.wait_ge(made["tq" if kind == "q" else "tk"], t)
                    done.mark(nc.vector.scalar_tensor_tensor(
                        rot[:, n % 2, :].rearrange("p (r j) -> p r j", j=16),
                        bank((kind, i))[:, :].rearrange("p (r j) -> p r j", j=16), scale,
                        sc[:, 1, t, :].unsqueeze(1).broadcast_to((P, 2 * FH, 16)), ALU.mult, ALU.mult))
                    done.mark(nc.vector.scalar_tensor_tensor(
                        r4[:, :, 0, :], b4[:, :, 1, :], scale, minus_sin[:, t, :].unsqueeze(1).broadcast_to((P, FH, 16)),
                        ALU.mult, ALU.mult))
                    nc.vector.scalar_tensor_tensor(
                        r4[:, :, 1, :], b4[:, :, 0, :], scale, sc[:, 0, t, :].unsqueeze(1).broadcast_to((P, FH, 16)),
                        ALU.mult, ALU.mult).then_inc(read[kind], 1)
                    dv.wait_ge(read[kind], i + 1)
                    nc.vector.tensor_tensor(rot[:, n % 2, :], rot[:, n % 2, :], rot_b[:, n % 2, :],
                                            ALU.add).then_inc(rot_ready, 1)
                if kind == "s":
                    if i >= 2:
                        dv.wait_ge(made["t"], i - 1)
                    nc.vector.tensor_tensor(e[:, i % 2], bank((kind, i))[:, :].rearrange("p (h k) -> p h k", h=CH),
                                            m_full[:, t, :].unsqueeze(1).broadcast_to((P, CH, P)),
                                            ALU.add).then_inc(read[kind], 1)
                    dv.wait_ge(read[kind], i + 1)
                    nc.vector.tensor_reduce(nmax[:, i % 2, :], e[:, i % 2], AX.X, ALU.max, negate=True
                                            ).then_inc(fmax_ready, 1)
                if kind == "t":
                    if i >= 2:
                        dv.wait_ge(made["pv"], i - 1)
                    nc.vector.tensor_copy(p_t[:, i % 2].rearrange("p h k -> p (h k)"), bank((kind, i))[:, :]
                                          ).then_inc(read[kind], 1)
                if kind == "pv":
                    o = bank((kind, i))[:, 0:CH * FV].rearrange("p (h v) -> p h v", v=FV)
                    step(nc.vector.reciprocal(den[:, i % 2, :], o[:, :, FD]))
                    if c == 0 and t >= 2:
                        dv.wait_ge(made["ot"], t - 1)
                    nc.vector.tensor_tensor(o_n[:, t % 2, P * c:P * c + P].rearrange("p (h d) -> p h d", h=CH), o[:, :, 0:FD],
                                            den[:, i % 2, :].unsqueeze(2).broadcast_to((P, CH, FD)),
                                            ALU.mult).then_inc(read[kind], 1)
                if kind == "wo":
                    nc.vector.tensor_tensor(x1f[:, i, :], bank((kind, i))[:, :], xs[:, i, :], ALU.add
                                            ).then_inc(read[kind], 1)
                    dv.wait_ge(read[kind], i + 1)
                    nc.vector.tensor_tensor_reduce(junk[:, :], x1f[:, i, :], x1f[:, i, :], 1.0, 0.0, ALU.mult, ALU.add,
                                                   ss2[:, i:i + 1]).then_inc(ss2_ready, 1)
                    dv.wait_ge(ss2_ready, i + 1)
                if kind == "th":
                    nc.vector.tensor_tensor(h2_t[:, :, P * i:P * i + P],
                                            bank((kind, i))[:, :].rearrange("p (c k) -> p c k", c=DC),
                                            l2[:, :].unsqueeze(2).broadcast_to((P, DC, P)), ALU.mult
                                            ).then_inc(read[kind], 1)
                if kind == "w2":
                    nc.vector.tensor_tensor(x1f[:, i, :], bank((kind, i))[:, :], x1f[:, i, :], ALU.add
                                            ).then_inc(read[kind], 1)
                    dv.wait_ge(read[kind], i + 1)
                    dv.wait_ge(rows_in, 16 * NT)
                    nc.vector.scalar_tensor_tensor(fin[:, i, :], x1f[:, i, :], w_sel[:, i:i + 1], fin[:, i, :], ALU.mult,
                                                   ALU.add).then_inc(fin_ready, 1)

        @block.tensor
        def _(pe):
            pe.wait_ge(ident_made, 1)
            for kind, i in plan:
                before = RINGS[kind, i][2]
                if before:
                    pe.wait_ge(read[before[0]], before[1] + 1)
                to = bank((kind, i))
                t, c = divmod(i, DC) if kind in ("s", "t", "pv") else (i, 0)
                tok = slice(P * i, P * i + P)
                if kind == "info":
                    for n in range(NT):
                        ins = nc.tensor.transpose(to[:, 3 * n:3 * n + 3], info_t[:, P * n:P * n + P], ident[0:3, 0:3])
                if kind == "mask":
                    for n in range(NT):
                        cols = slice(P * n, P * n + P)
                        for k in range(TT):
                            ins = nc.tensor.matmul(to[:, cols], mask_rows[:, k, cols], picked[:, k, cols],
                                                   start=(k == 0), stop=(k == TT - 1))
                if kind == "xs":
                    for n in range(DC):
                        ins = nc.tensor.transpose(to[:, P * n:P * n + P], xsel_t[:, n, tok], ident[:, :])
                if kind in ("q", "k", "v"):
                    pe.wait_ge(ht_ready, DC)
                    for n in range(DC):
                        ins = nc.tensor.matmul(to[:, :], h_t[:, n, tok], w4[:, "qkv".index(kind), n, :],
                                               start=(n == 0), stop=(n == DC - 1))
                if kind in ("tq", "tk"):
                    n = 2 * i + (kind == "tk")
                    pe.wait_ge(rot_ready, n + 1)
                    for k in range(DC):
                        ins = nc.tensor.transpose(to[:, P * k:P * k + P], rot[:, n % 2, P * k:P * k + P], ident[:, :])
                if kind == "s":
                    if i == 0:
                        pe.wait_ge(const_made, 1)
                    pe.wait_ge(read["tq"], t + 1)
                    pe.wait_ge(read["tk"], t + 1)
                    ins = nc.tensor.matmul(to[:, :], q_t[:, t % 2, c, :], k_bd[:, t % 2, c].rearrange("p h k -> p (h k)"),
                                           start=True, stop=True)
                if kind == "t":
                    pe.wait_ge(exp_ready, i + 1)
                    for h in range(CH):
                        ins = nc.tensor.transpose(to[:, P * h:P * h + P], e[:, i % 2, h, :], ident[:, :])
                if kind == "pv":
                    pe.wait_ge(read["t"], i + 1)
                    pe.wait_ge(read["v"], t + 1)
                    for h in range(CH):
                        ins = nc.tensor.matmul(to[:, FV * h:FV * h + FV], p_t[:, i % 2, h, :],
                                               v_sb[:, t % 2, CH * c + h, :], start=True, stop=True)
                if kind == "ot":
                    pe.wait_ge(read["pv"], DC * (i + 1))
                    for n in range(DC):
                        ins = nc.tensor.transpose(to[:, P * n:P * n + P], o_n[:, i % 2, P * n:P * n + P], ident[:, :])
                if kind == "wo":
                    pe.wait_ge(read["ot"], i + 1)
                    for n in range(DC):
                        ins = nc.tensor.matmul(to[:, :], o_t[:, i % 2, n, :], w4[:, 3, n, :], start=(n == 0),
                                               stop=(n == DC - 1))
                if kind == "th":
                    pe.wait_ge(hn_ready, i + 1)
                    for n in range(DC):
                        ins = nc.tensor.transpose(to[:, P * n:P * n + P], hn[:, i % 2, P * n:P * n + P], ident[:, :])
                if kind == "w1":
                    pe.wait_ge(w1_in, 16)
                    pe.wait_ge(read["th"], NT)
                    for n in range(DC):
                        ins = nc.tensor.matmul(to[:, :], w1_sb[:, n, P * i:P * i + P], h2_t[:, n, :], start=(n == 0),
                                               stop=(n == DC - 1))
                if kind == "w2":
                    pe.wait_ge(w2_in, 16)
                    pe.wait_ge(read["w1"], FC)
                    for f in range(FC):
                        ins = nc.tensor.matmul(to[:, :], g_t[:, f // DC, f % DC, tok], w2_sb[:, f, :], start=(f == 0),
                                               stop=(f == FC - 1))
                ins.then_inc(made[kind], 1)


def pre_ln_decoder_layer(nc, x, ctx_1024, mask_1x1xSxS2_fk0, L0_attn_norm_w, L0_attn_w_q, L0_attn_w_k, L0_attn_w_v,
                         L0_attn_w_out, L0_attn_scorer_w, L0_attn_scorer_b, L0_xattn_Wq, L0_xattn_Wk, L0_xattn_Wv,
                         L0_ffn_attention_mask, L0_ffn_position_ids, L0_ffn_router_w, L0_ffn_router_b, L0_ffn_wq,
                         L0_ffn_wk, L0_ffn_wv, L0_ffn_wo, L0_ffn_w1, L0_ffn_w2, L0_ffn_ln1, L0_ffn_ln2, out):
    x1 = nc.dram_tensor("x1", [B, S, D], F32, kind="Internal").ap()
    self_attention(nc, x, L0_attn_norm_w, L0_attn_w_q, L0_attn_w_k, L0_attn_w_v, L0_attn_w_out, L0_attn_scorer_w,
                   L0_attn_scorer_b, x1)
    with ExitStack() as ctx:
        def sb(name, shape):
            return ctx.enter_context(nc.sbuf_tensor(name, shape, F32))

        xsel_t, info_t = sb("xsel_t", [P, DC, NSEL]), sb("info_t", [3, NSEL])
        picked, mask_rows = sb("picked", [P, TT, NSEL]), sb("mask_rows", [P, TT, NSEL])
        w4 = sb("w4", [P, 4, DC, D])
        later = [(w4[:, k], w.rearrange("(c p) d -> p c d", p=P))
                 for k, w in enumerate((L0_ffn_wq, L0_ffn_wk, L0_ffn_wv, L0_ffn_wo))]
        cross_and_router(nc, x1, ctx_1024, mask_1x1xSxS2_fk0, L0_xattn_Wq, L0_xattn_Wk, L0_xattn_Wv,
                         L0_ffn_attention_mask, L0_ffn_position_ids, L0_ffn_router_w, L0_ffn_router_b, out,
                         xsel_t, info_t, picked, mask_rows, later)
        routed_block(nc, xsel_t, info_t, picked, mask_rows, w4, L0_ffn_ln1, L0_ffn_ln2, L0_ffn_w1, L0_ffn_w2, out)


_INS = ["x", "ctx_1024", "mask_1x1xSxS2_fk0", "L0_attn_norm_w", "L0_attn_w_q", "L0_attn_w_k", "L0_attn_w_v",
        "L0_attn_w_out", "L0_attn_scorer_w", "L0_attn_scorer_b", "L0_xattn_Wq", "L0_xattn_Wk", "L0_xattn_Wv",
        "L0_ffn_attention_mask", "L0_ffn_position_ids", "L0_ffn_router_w", "L0_ffn_router_b", "L0_ffn_wq",
        "L0_ffn_wk", "L0_ffn_wv", "L0_ffn_wo", "L0_ffn_w1", "L0_ffn_w2", "L0_ffn_ln1", "L0_ffn_ln2"]


def kernel(**inputs):
    import numpy as _np
    import concourse.bacc as _bacc
    from concourse import mybir as _mybir
    from concourse.bass_utils import run_bass_kernel_spmd as _run

    nc = _bacc.Bacc("TRN2", target_bir_lowering=False, num_devices=1)
    arrays, args = {}, []
    for name in _INS:
        a = _np.ascontiguousarray(inputs[name])
        arrays[f"in_{name}"] = a
        args.append(nc.dram_tensor(f"in_{name}", a.shape, _mybir.dt.from_np(a.dtype), kind="ExternalInput").ap())
    args.append(nc.dram_tensor("out_0", (B, S, D), F32, kind="ExternalOutput").ap())
    pre_ln_decoder_layer(nc, *args)
    r = _run(nc, [arrays], core_ids=[0])
    return r.results[0]["out_0"]
```
